# Optimizing a Trainium2 kernel written in Bass

```python
import numpy as np
import jax
import jax.numpy as jnp

def _softmax(x, axis=-1):
    return jax.nn.softmax(x, axis=axis)

def _gelu(x):
    return jax.nn.gelu(x, approximate=True)

def _silu(x):
    return jax.nn.silu(x)

def _sigmoid(x):
    return jax.nn.sigmoid(x)

def _layernorm(x, axis=-1, eps=1e-05):
    m = jnp.mean(x, axis=axis, keepdims=True)
    v = jnp.var(x, axis=axis, keepdims=True)
    return (x - m) / jnp.sqrt(v + eps)

def _scatter_add(tgt, idx, src, axis=0):
    return tgt.at[idx].add(src)

def _segment_sum(src, seg, n):
    return jax.ops.segment_sum(src, seg, n)
kernel_name = 'mk_decoder_postln_d1_seqx_r2_c735e5'

def setup_inputs(seed: int=0):
    np.random.seed(seed)
    _w = jnp.asarray

    def _rec_inputs():
        import jax
        import jax.numpy as jnp
        _rk = jax.random.key(seed)
        x = 7.22e-05 + 1 * jax.random.normal(jax.random.fold_in(_rk, 1), (16, 224, 512), jnp.float32)
        _lenS = 224 - jax.random.randint(jax.random.fold_in(_rk, 7), (16,), 0, max(1, 224 // 4) + 1, jnp.int32)
        _lenS2 = 750 - jax.random.randint(jax.random.fold_in(_rk, 8), (16,), 0, max(1, 750 // 4) + 1, jnp.int32)
        _ctx_1024P = jax.random.normal(jax.random.fold_in(_rk, 11), (16, 16, 512), jnp.float32)
        _ctx_1024c = jax.random.dirichlet(jax.random.fold_in(_rk, 511), 0.3 * jnp.ones((16,), jnp.float32), (16, 750))
        _ctx_1024t = jnp.einsum('bsk,bkd->bsd', _ctx_1024c, _ctx_1024P)
        _ctx_1024t = _ctx_1024t * jax.lax.rsqrt(jnp.mean(jnp.square(_ctx_1024t)) + 1e-12) * 0.953939
        ctx_1024 = 4.13588e-05 + 0.999923 * (_ctx_1024t + 0.3 * jax.random.normal(jax.random.fold_in(_rk, 611), (16, 750, 512), jnp.float32))
        return (x, ctx_1024)
    x, ctx_1024 = _rec_inputs()

    def _L0_attn_setup():
        import jax, jax.numpy as jnp
        import numpy as np
        B, T, EMB, HEADS = (4, 1024, 512, 16)
        CHUNK = EMB // HEADS
        key = jax.random.key(seed)
        kx, kq, kk, kv, ku = jax.random.split(key, 5)
        s = CHUNK ** (-0.5)
        return {'x': jax.random.normal(kx, (B, T, EMB), jnp.float32), 'Wq': jax.random.normal(kq, (CHUNK, CHUNK), jnp.float32) * s, 'Wk': jax.random.normal(kk, (CHUNK, CHUNK), jnp.float32) * s, 'Wv': jax.random.normal(kv, (CHUNK, CHUNK), jnp.float32) * s, 'Wu': jax.random.normal(ku, (EMB, EMB), jnp.float32) * EMB ** (-0.5), 'bu': jnp.zeros((EMB,), jnp.float32)}
    _L0_attn_all = _L0_attn_setup()
    _L0_attn_in = {k: v for k, v in _L0_attn_all.items() if k in ('Wq', 'Wk', 'Wv', 'Wu', 'bu')}
    del _L0_attn_all

    def _L0_xattn_setup():
        import jax, jax.numpy as jnp
        import numpy as np
        B, SQ, SK, D = (4, 1024, 1024, 512)
        key = jax.random.key(seed)
        ks = jax.random.split(key, 8)
        s = 1.0 / np.sqrt(D)
        return {'input_seq': jax.random.normal(ks[0], (B, SQ, D), jnp.float32), 'condition_seq': jax.random.normal(ks[1], (B, SK, D), jnp.float32), 'Wq': jax.random.normal(ks[2], (D, D), jnp.float32) * s, 'bq': jnp.zeros((D,), jnp.float32), 'Wk': jax.random.normal(ks[3], (D, D), jnp.float32) * s, 'bk': jnp.zeros((D,), jnp.float32), 'Wv': jax.random.normal(ks[4], (D, D), jnp.float32) * s, 'bv': jnp.zeros((D,), jnp.float32)}
    _L0_xattn_all = _L0_xattn_setup()
    _L0_xattn_in = {k: v for k, v in _L0_xattn_all.items() if k in ('Wq', 'bq', 'Wk', 'bk', 'Wv', 'bv')}
    del _L0_xattn_all

    def _L0_ffn_setup():
        import jax, jax.numpy as jnp
        import numpy as np
        from jax import lax
        T, B, I, M, O = (128, 64, 512, 512, 512)

        def _xavier(key, shape):
            fan_out, fan_in = shape
            limit = float(np.sqrt(6.0 / (fan_in + fan_out)))
            return jax.random.uniform(key, shape, jnp.float32, -limit, limit)
        key = jax.random.key(seed)
        ks = jax.random.split(key, 9)
        x = jax.random.normal(ks[0], (T, B, I), jnp.float32)
        return {'x': x, 'wf': _xavier(ks[1], (M, I)), 'uf': _xavier(ks[2], (M, M)), 'bf': jnp.zeros((M,), jnp.float32), 'wi': _xavier(ks[3], (M, I)), 'ui': _xavier(ks[4], (M, M)), 'bi': jnp.zeros((M,), jnp.float32), 'wc': _xavier(ks[5], (M, I)), 'uc': _xavier(ks[6], (M, M)), 'bc': jnp.zeros((M,), jnp.float32), 'wo': _xavier(ks[7], (O, I)), 'uo': _xavier(ks[8], (O, M)), 'bo': jnp.zeros((O,), jnp.float32), 'in_c': jnp.zeros((M,), jnp.float32)}
    _L0_ffn_all = _L0_ffn_setup()
    _L0_ffn_in = {k: v for k, v in _L0_ffn_all.items() if k in ('wf', 'uf', 'bf', 'wi', 'ui', 'bi', 'wc', 'uc', 'bc', 'wo', 'uo', 'bo', 'in_c')}
    del _L0_ffn_all
    return {'x': x, 'ctx_1024': ctx_1024, 'L0_attn_Wq': _L0_attn_in['Wq'], 'L0_attn_Wk': _L0_attn_in['Wk'], 'L0_attn_Wv': _L0_attn_in['Wv'], 'L0_attn_Wu': _L0_attn_in['Wu'], 'L0_attn_bu': _L0_attn_in['bu'], 'L0_xattn_Wq': _L0_xattn_in['Wq'], 'L0_xattn_bq': _L0_xattn_in['bq'], 'L0_xattn_Wk': _L0_xattn_in['Wk'], 'L0_xattn_bk': _L0_xattn_in['bk'], 'L0_xattn_Wv': _L0_xattn_in['Wv'], 'L0_xattn_bv': _L0_xattn_in['bv'], 'L0_ffn_wf': _L0_ffn_in['wf'], 'L0_ffn_uf': _L0_ffn_in['uf'], 'L0_ffn_bf': _L0_ffn_in['bf'], 'L0_ffn_wi': _L0_ffn_in['wi'], 'L0_ffn_ui': _L0_ffn_in['ui'], 'L0_ffn_bi': _L0_ffn_in['bi'], 'L0_ffn_wc': _L0_ffn_in['wc'], 'L0_ffn_uc': _L0_ffn_in['uc'], 'L0_ffn_bc': _L0_ffn_in['bc'], 'L0_ffn_wo': _L0_ffn_in['wo'], 'L0_ffn_uo': _L0_ffn_in['uo'], 'L0_ffn_bo': _L0_ffn_in['bo'], 'L0_ffn_in_c': _L0_ffn_in['in_c']}

def reference(x, ctx_1024, L0_attn_Wq, L0_attn_Wk, L0_attn_Wv, L0_attn_Wu, L0_attn_bu, L0_xattn_Wq, L0_xattn_bq, L0_xattn_Wk, L0_xattn_bk, L0_xattn_Wv, L0_xattn_bv, L0_ffn_wf, L0_ffn_uf, L0_ffn_bf, L0_ffn_wi, L0_ffn_ui, L0_ffn_bi, L0_ffn_wc, L0_ffn_uc, L0_ffn_bc, L0_ffn_wo, L0_ffn_uo, L0_ffn_bo, L0_ffn_in_c):
    import jax
    import jax.numpy as jnp

    def _L0_attn_ref(x, Wq, Wk, Wv, Wu, bu):
        import jax, jax.numpy as jnp
        import numpy as np
        B, T, EMB, HEADS = (4, 1024, 512, 16)
        CHUNK = EMB // HEADS
        b, t, d = x.shape
        h = HEADS
        c = d // h
        xh = x.reshape(b, t, h, c)
        scale = d ** (-0.25)
        q = jnp.einsum('bthc,oc->btho', xh, Wq) * scale
        k = jnp.einsum('bthc,oc->btho', xh, Wk) * scale
        v = jnp.einsum('bthc,oc->btho', xh, Wv)
        scores = jnp.einsum('bihc,bjhc->bhij', q, k)
        i = jnp.arange(t)[:, None]
        j = jnp.arange(t)[None, :]
        scores = jnp.where(j > i, -jnp.inf, scores)
        attn = jax.nn.softmax(scores, axis=-1)
        y = jnp.einsum('bhij,bjhc->bihc', attn, v).reshape(b, t, d)
        return y @ Wu.T + bu

    def _L0_xattn_ref(input_seq, condition_seq, Wq, bq, Wk, bk, Wv, bv):
        import jax, jax.numpy as jnp
        import numpy as np
        B, SQ, SK, D = (4, 1024, 1024, 512)
        q = jnp.einsum('bsd,ed->bse', input_seq, Wq) + bq
        k = jnp.einsum('btd,ed->bte', condition_seq, Wk) + bk
        v = jnp.einsum('btd,ed->bte', condition_seq, Wv) + bv
        scores = jnp.einsum('bse,bte->bst', q, k)
        attn = jax.nn.softmax(scores, axis=-1)
        attended = jnp.einsum('bst,bte->bse', attn, v)
        return attended

    def _L0_ffn_ref(x, wf, uf, bf, wi, ui, bi, wc, uc, bc, wo, uo, bo, in_c):
        import jax, jax.numpy as jnp
        import numpy as np
        from jax import lax
        T, B, I, M, O = (128, 64, 512, 512, 512)

        def _xavier(key, shape):
            fan_out, fan_in = shape
            limit = float(np.sqrt(6.0 / (fan_in + fan_out)))
            return jax.random.uniform(key, shape, jnp.float32, -limit, limit)
        batch = x.shape[1]
        c0 = jnp.broadcast_to(in_c, (batch, in_c.shape[0]))

        def step(c, xt):
            ft = jax.nn.sigmoid(xt @ wf.T + c @ uf.T + bf)
            it = jax.nn.sigmoid(xt @ wi.T + c @ ui.T + bi)
            gt = jnp.tanh(xt @ wc.T + c @ uc.T + bc)
            c = ft * c + it * gt
            return (c, None)
        c_final, _ = lax.scan(step, c0, x)
        h = jnp.tanh(jnp.einsum('tbi,oi->tbo', x, wo) + c_final @ uo.T + bo)
        return h
    x = _layernorm(x + _L0_attn_ref(x, L0_attn_Wq, L0_attn_Wk, L0_attn_Wv, L0_attn_Wu, L0_attn_bu), axis=-1)
    x = _layernorm(x + _L0_xattn_ref(x, ctx_1024, L0_xattn_Wq, L0_xattn_bq, L0_xattn_Wk, L0_xattn_bk, L0_xattn_Wv, L0_xattn_bv), axis=-1)
    x = _layernorm(x + _L0_ffn_ref(x, L0_ffn_wf, L0_ffn_uf, L0_ffn_bf, L0_ffn_wi, L0_ffn_ui, L0_ffn_bi, L0_ffn_wc, L0_ffn_uc, L0_ffn_bc, L0_ffn_wo, L0_ffn_uo, L0_ffn_bo, L0_ffn_in_c), axis=-1)
    return x

_drawn_inputs = setup_inputs


def setup_inputs(seed=0):
    import zlib

    import numpy as np

    out = dict(_drawn_inputs(seed))
    spreads = {'L0_attn_bu': (0.0, 0.1),
     'L0_xattn_bq': (0.0, 0.1),
     'L0_xattn_bk': (0.0, 0.8),
     'L0_xattn_bv': (0.0, 0.1),
     'L0_ffn_bf': (0.0, 0.707),
     'L0_ffn_bi': (0.0, 0.691),
     'L0_ffn_bc': (0.0, 0.1),
     'L0_ffn_bo': (0.0, 0.1),
     'L0_ffn_in_c': (0.0, 0.8)}
    factors = {}
    for name, (base, spread) in spreads.items():
        noise = np.random.default_rng([zlib.crc32(name.encode()), seed]).standard_normal(out[name].shape)
        drawn = base * np.exp(spread * noise) if base else spread * noise
        out[name] = jnp.asarray(drawn.astype(out[name].dtype))
    for name, factor in factors.items():
        out[name] = (out[name] * factor).astype(out[name].dtype)
    return out
```

```python
from contextlib import ExitStack

import numpy as np
import concourse.bass as bass
from concourse import mybir

F32 = mybir.dt.float32
F32R = mybir.dt.float32r
BF16 = mybir.dt.bfloat16
ALU = mybir.AluOpType
ACT = mybir.ActivationFunctionType
AX = mybir.AxisListType

B, T, D = 16, 224, 512
H, C = 16, 32
TC = 2
R = T // TC
KC = D // 128
TX = 750
XC, XR = 6, 125
XH = TX // 2
G = 4
NG = H // G
NEG = -1.0e30
EPS = 1e-5


def wait(eng, sem, value):
    if not (isinstance(value, int) and value <= 0):
        eng.wait_ge(sem, value)


def within(n, end):
    return not isinstance(n, int) or 0 <= n < end


def self_attention(nc, io, x1):
    with ExitStack() as ctx:
        def sb(name, shape, dt=F32):
            return ctx.enter_context(nc.sbuf_tensor("a_" + name, shape, dt))

        def sem(name):
            return ctx.enter_context(nc.semaphore("a_" + name))

        identity = sb("identity", [128, 128])
        identity_b = sb("identity_b", [R, R], BF16)
        mask = sb("mask", [R, G, R], BF16)
        wq3 = sb("wq3", [C, 3, C])
        wk3 = sb("wk3", [C, 3, C])
        a_f = sb("a_f", [3 * C, 3 * C])
        a_stack = sb("a_stack", [3 * C, 3 * C], F32R)
        wv_diag = sb("wv_diag", [128, 128])
        wu_raw = sb("wu_raw", [128, KC, D])
        w_hi = sb("w_hi", [128, KC, D], F32R)
        w_lo = sb("w_lo", [128, KC, D], F32R)
        bu_all = sb("bu_all", [R, D])
        xs_raw = sb("xs_raw", [3 * C, 2, G, T])
        xs = sb("xs", [3 * C, 2, G, T], F32R)
        v_raw = sb("v_raw", [R, 2, TC, 128])
        v_hi = sb("v_hi", [R, 2, TC, 128], F32R)
        v_lo = sb("v_lo", [R, 2, TC, 128], F32R)
        zs = sb("zs", [3 * C, 2, G, T], F32R)
        nmax = sb("nmax", [R, 2, TC, G])
        rsum = sb("rsum", [R, 2, TC, G])
        rinv = sb("rinv", [R, 2, TC, G])
        p0 = sb("p0", [R, 2, G, R])
        p1 = sb("p1", [R, 2, G, T])
        pt0_hi = sb("pt0_hi", [R, 2, G, T], F32R)
        pt0_lo = sb("pt0_lo", [R, 2, G, T], F32R)
        pt1_hi = sb("pt1_hi", [R, 2, G, R], F32R)
        pt1_lo = sb("pt1_lo", [R, 2, G, R], F32R)
        yt_hi = sb("yt_hi", [128, NG, T], F32R)
        yt_lo = sb("yt_lo", [128, NG, T], F32R)
        xres = sb("xres", [R, TC, D])
        xb = sb("xb", [R, TC, D])
        r = sb("r", [R, TC, D])
        stats = sb("stats", [R, TC, 6])
        mv = sb("mv", [R, TC, 2])
        veps = sb("veps", [R, TC, 1])
        mhalf = sb("mhalf", [R, TC, 1])
        rstd = sb("rstd", [R, TC, 1])
        xn = sb("xn", [R, TC, D])

        ps_s = ctx.enter_context(nc.psum_tensor("a_ps_s", [128, 3, 512], F32))
        ps_t = ctx.enter_context(nc.psum_tensor("a_ps_t", [128, 3, 512], F32))
        ps_y = ctx.enter_context(nc.psum_tensor("a_ps_y", [128, 2, 512], F32))

        const_ready = sem("const_ready")
        w_in = sem("w_in")
        diag_in = sem("diag_in")
        bu_in = sem("bu_in")
        prep_id = sem("prep_id")
        prep_mm = sem("prep_mm")
        prep_act = sem("prep_act")
        prep_dve = sem("prep_dve")
        xs_in = [sem(f"xs_in{i}") for i in range(2)]
        v_in = [sem(f"v_in{i}") for i in range(2)]
        res_in = sem("res_in")
        xh_done = sem("xh_done")
        xl_done = sem("xl_done")
        vh_done = sem("vh_done")
        vl_done = sem("vl_done")
        z_done = sem("z_done")
        zh_done = sem("zh_done")
        zl_done = sem("zl_done")
        s_done = sem("s_done")
        max_done = sem("max_done")
        exp_done = sem("exp_done")
        rinv_done = sem("rinv_done")
        norm_done = sem("norm_done")
        t_done = sem("t_done")
        pth_done = sem("pth_done")
        ptl_done = sem("ptl_done")
        pv_done = sem("pv_done")
        yh_done = sem("yh_done")
        yl_done = sem("yl_done")
        wu_done = sem("wu_done")
        xb_done = sem("xb_done")
        r_done = sem("r_done")
        stats_done = sem("stats_done")
        mv_done = sem("mv_done")
        veps_done = sem("veps_done")
        rstd_done = sem("rstd_done")
        xn_done = sem("xn_done")
        stored = sem("stored")

        STEPS = B * NG
        block = ctx.enter_context(nc.Block())

        @block.sync
        def _(sp):
            for j in range(3):
                sp.dma_start(wq3[:, j, :], io["wq"]).then_inc(w_in, 16)
                sp.dma_start(wk3[:, j, :], io["wk"]).then_inc(w_in, 16)
            sp.dma_start(wu_raw[:], io["wu_t"].rearrange("(k p) e -> p k e", p=128)).then_inc(w_in, 16)
            sp.wait_ge(const_ready, 1)
            for g in range(G):
                sp.dma_start(wv_diag[C * g:C * g + C, C * g:C * g + C], io["wv"]).then_inc(diag_in, 16)
            sp.dma_start(bu_all[:], io["bu"].rearrange("(a d) -> a d", a=1).to_broadcast((R, D))).then_inc(bu_in, 16)

            def loads(b, g):
                n = NG * b + g
                wait(sp, xl_done, n - 1)
                for j in range(3):
                    sp.dma_start(xs_raw[C * j:C * j + C, g % 2, :, :],
                                 io["xt"][b, :, G * g:G * g + G, :]).then_inc(xs_in[g % 2], 16)
                if g >= 2:
                    values(b, g - 2)
                elif within(b - 1, B):
                    values(b - 1, g + 2)
                if g == 1:
                    wait(sp, xb_done, b)
                    sp.dma_start(xres[:], io["x"][b].rearrange("(c p) d -> p c d", p=R)).then_inc(res_in, 16)

                    if within(b - 2, B):
                        store(b - 2)

            def values(b, g):
                wait(sp, vl_done, NG * b + g - 1)
                sp.dma_start(v_raw[:, g % 2, :, :], io["x"][b, :, 128 * g:128 * g + 128]
                             .rearrange("(c p) d -> p c d", p=R)).then_inc(v_in[g % 2], 16)

            def store(b):
                sp.wait_ge(xn_done, TC * (b + 1))
                sp.dma_start(x1[b].rearrange("(c p) d -> p c d", p=R), xn[:]).then_inc(stored, 16)

            for b in range(2):
                for g in range(NG):
                    loads(b, g)
            with sp.Fori(2, B) as b:
                for g in range(NG):
                    loads(b, g)
            values(B - 1, 2)
            values(B - 1, 3)
            store(B - 2)
            store(B - 1)
            sp.wait_ge(stored, 16 * B)

        @block.tensor
        def _(pe):
            pe.wait_ge(const_ready, 5)
            pe.wait_ge(w_in, 7 * 16)
            pe.wait_ge(diag_in, 4 * 16)
            pe.matmul(ps_y[0:3 * C, 0, 0:3 * C], wq3[:, :, :], wk3[:, :, :], start=True, stop=True).then_inc(prep_mm, 1)
            for k in range(KC):
                if k >= 2:
                    pe.wait_ge(prep_dve, k)
                pe.matmul(ps_s[:, k % 2, :], wv_diag[:], wu_raw[:, k, :], start=True, stop=True).then_inc(prep_mm, 1)

            def z(n, g):
                if not within(n, STEPS):
                    return
                wait(pe, xl_done, n + 1)
                wait(pe, zl_done, n)
                wait(pe, yl_done, n - 3)
                for half in range(2):
                    mm = pe.matmul(ps_y[0:3 * C, half, 0:2 * T], a_stack[:], xs[:, g % 2, 2 * half:2 * half + 2, :],
                                   start=True, stop=True)
                mm.then_inc(z_done, 1)

            def s(n, g):
                if not within(n, STEPS):
                    return
                wait(pe, zl_done, n + 1)
                wait(pe, exp_done, n)
                for h in range(G):
                    pe.matmul(ps_s[0:R, 0, h * R:h * R + R], zs[:, g % 2, h, 0:R], xs[:, g % 2, h, 0:R],
                              start=(h == 0), stop=False, skip_group_check=True)
                pe.matmul(ps_s[0:R, 0, 0:G * R], identity_b[:], mask[:, :, :], start=False, stop=True,
                          skip_group_check=True)
                for half in range(2):
                    for h in range(2):
                        pe.matmul(ps_s[0:R, 1 + half, h * T:h * T + T], zs[:, g % 2, 2 * half + h, R:T],
                                  xs[:, g % 2, 2 * half + h, :], start=(h == 0), stop=False, skip_group_check=True)
                    diagonal = ps_s[0:R, 1 + half, 0:2 * T].rearrange("p (h t) -> p h t", h=2)[:, :, R:T]
                    mm = pe.matmul(diagonal, identity_b[:], mask[:, 0:2, :], start=False, stop=True,
                                   skip_group_check=True)
                mm.then_inc(s_done, 1)

            def t(n, g):
                if not within(n, STEPS):
                    return
                wait(pe, norm_done, 2 * (n + 1))
                wait(pe, ptl_done, n)
                for h in range(G):
                    pe.transpose(ps_t[0:R, h // 2, (h % 2) * T:(h % 2) * T + R], p0[:, g % 2, h, :], identity[0:R, 0:R])
                    pe.transpose(ps_t[0:R, h // 2, (h % 2) * T + R:(h % 2) * T + T], p1[:, g % 2, h, 0:R], identity[0:R, 0:R])
                    mm = pe.transpose(ps_t[0:R, 2, h * R:h * R + R], p1[:, g % 2, h, R:T], identity[0:R, 0:R])
                mm.then_inc(t_done, 1)

            def pv(n, g, b):
                if not within(n, STEPS):
                    return
                wait(pe, ptl_done, n + 1)
                wait(pe, vl_done, n + 1)
                wait(pe, zl_done, min(n + 4, STEPS) if isinstance(n, int) else n + 4)
                wait(pe, yl_done, n)
                if g == 0:
                    wait(pe, r_done, TC * b)
                for half in range(2):
                    terms = ((v_hi, pt0_hi, pt1_hi), (v_hi, pt0_lo, pt1_lo), (v_lo, pt0_hi, pt1_hi))
                    for i, (v, pt0, pt1) in enumerate(terms):
                        pe.matmul(ps_y[:, half, 0:2 * T], v[:, g % 2, 0, :], pt0[:, g % 2, 2 * half:2 * half + 2, :],
                                  start=(i == 0), stop=False, skip_group_check=True)
                        later = ps_y[:, half, 0:2 * T].rearrange("p (h t) -> p h t", h=2)[:, :, R:T]
                        mm = pe.matmul(later, v[:, g % 2, 1, :], pt1[:, g % 2, 2 * half:2 * half + 2, :],
                                       start=False, stop=(i == 2), skip_group_check=True)
                mm.then_inc(pv_done, 1)

            def wu(b):
                if not within(b, B):
                    return
                wait(pe, yl_done, NG * (b + 1))
                wait(pe, zl_done, min(NG * b + 8, STEPS) if isinstance(b, int) else NG * b + 8)
                for c in range(TC):
                    i = 0
                    for y, w in ((yt_hi, w_hi), (yt_hi, w_lo), (yt_lo, w_hi)):
                        for k in range(KC):
                            mm = pe.matmul(ps_y[0:R, c, :], y[:, k, c * R:c * R + R], w[:, k, :],
                                           start=(i == 0), stop=(i == 3 * KC - 1))
                            i += 1
                mm.then_inc(wu_done, 1)

            pe.wait_ge(prep_dve, 1 + KC)
            z(0, 0)
            z(1, 1)

            def steps(b):
                for g in range(NG):
                    n = NG * b + g
                    s(n, g)
                    t(n - 1, (g - 1) % NG)
                    if g == 2:
                        wu(b - 1)
                    pv(n - 2, (g - 2) % NG, b if g >= 2 else b - 1)
                    z(n + 2, (g + 2) % NG)

            steps(0)
            with pe.Fori(1, B - 1) as b:
                steps(b)
            steps(B - 1)
            steps(B)

        @block.scalar
        def _(act):
            act.wait_ge(prep_mm, 1)
            act.activation(a_f[:], ps_y[0:3 * C, 0, 0:3 * C], ACT.Copy, scale=float(D) ** -0.5).then_inc(prep_act, 1)
            act.wait_ge(prep_act, 1)
            act.activation(a_stack[:], a_f[:], ACT.Copy).then_inc(prep_act, 1)
            for k in range(KC):
                act.wait_ge(prep_mm, 2 + k)
                act.activation(w_hi[:, k, :], ps_s[:, k % 2, :], ACT.Copy).then_inc(prep_act, 1)

            def exp(n, g):
                if not within(n, STEPS):
                    return
                wait(act, max_done, n + 1)
                wait(act, t_done, n - 1)
                for c, p in ((0, p0), (1, p1)):
                    for h in range(G):
                        src = ps_s[0:R, 0, h * R:h * R + R] if c == 0 else ps_s[0:R, 1 + h // 2, (h % 2) * T:(h % 2) * T + T]
                        e = act.activation(p[:, g % 2, h, :], src, ACT.Exp, bias=nmax[:, g % 2, c, h:h + 1],
                                           accum_out=rsum[:, g % 2, c, h:h + 1])
                e.then_inc(exp_done, 1)

            def pth(n, g):
                if not within(n, STEPS):
                    return
                wait(act, t_done, n + 1)
                wait(act, pv_done, n - 1)
                act.activation(pt0_hi[:, g % 2, 0:2, :], ps_t[0:R, 0, 0:2 * T], ACT.Copy)
                act.activation(pt0_hi[:, g % 2, 2:4, :], ps_t[0:R, 1, 0:2 * T], ACT.Copy)
                act.activation(pt1_hi[:, g % 2, :, :], ps_t[0:R, 2, 0:G * R], ACT.Copy).then_inc(pth_done, 1)

            def yh(n, g, b):
                if not within(n, STEPS):
                    return
                wait(act, pv_done, n + 1)
                if g == 0:
                    wait(act, wu_done, b)
                for h in range(G):
                    y = act.activation(yt_hi[C * h:C * h + C, g, :], ps_y[C * h:C * h + C, h // 2, (h % 2) * T:(h % 2) * T + T], ACT.Copy)
                y.then_inc(yh_done, 1)

            def zh(n, g):
                if not within(n, STEPS):
                    return
                wait(act, z_done, n + 1)
                wait(act, s_done, n - 1)
                act.activation(zs[:, g % 2, 0:2, :], ps_y[0:3 * C, 0, 0:2 * T], ACT.Copy)
                act.activation(zs[:, g % 2, 2:4, :], ps_y[0:3 * C, 1, 0:2 * T], ACT.Copy).then_inc(zh_done, 1)

            zh(0, 0)
            zh(1, 1)

            def steps(b):
                for g in range(NG):
                    n = NG * b + g
                    exp(n, g)
                    pth(n - 1, (g - 1) % NG)
                    yh(n - 2, (g - 2) % NG, b)
                    zh(n + 2, (g + 2) % NG)

            steps(0)
            with act.Fori(1, B - 1) as b:
                steps(b)
            steps(B - 1)
            steps(B)

        @block.vector
        def _(dve):
            dve.wait_ge(prep_act, 2)
            dve.tensor_tensor(a_stack[2 * C:3 * C, :], a_f[2 * C:3 * C, :], a_stack[2 * C:3 * C, :], ALU.subtract).then_inc(prep_dve, 1)
            for k in range(KC):
                dve.wait_ge(prep_act, 3 + k)
                dve.tensor_tensor(w_lo[:, k, :], ps_s[:, k % 2, :], w_hi[:, k, :], ALU.subtract).then_inc(prep_dve, 1)

            def xh(n, g, b):
                if not within(n, STEPS):
                    return
                wait(dve, xs_in[g % 2], 48 * (2 * b + g // 2 + 1))
                wait(dve, s_done, n - 1)
                dve.tensor_copy(xs[:, g % 2, :, :], xs_raw[:, g % 2, :, :]).then_inc(xh_done, 1)

            def vh(n, g, b):
                if not within(n, STEPS):
                    return
                wait(dve, v_in[g % 2], 16 * (2 * b + g // 2 + 1))
                wait(dve, pv_done, n - 1)
                dve.tensor_copy(v_hi[:, g % 2, :, :], v_raw[:, g % 2, :, :]).then_inc(vh_done, 1)

            def smax(n, g):
                if not within(n, STEPS):
                    return
                wait(dve, s_done, n + 1)
                dve.tensor_reduce(nmax[:, g % 2, 0, :], ps_s[0:R, 0, 0:G * R].rearrange("p (h t) -> p h t", h=G),
                                  AX.X, ALU.max, negate=True)
                dve.tensor_reduce(nmax[:, g % 2, 1, :], ps_s[0:R, 1:3, 0:2 * T].rearrange("p a (h t) -> p a h t", h=2),
                                  AX.X, ALU.max, negate=True).then_inc(max_done, 1)

            def inverse(n, g):
                if not within(n, STEPS):
                    return
                wait(dve, exp_done, n + 1)
                wait(dve, norm_done, 2 * (n - 1))
                dve.reciprocal(rinv[:, g % 2, :, :], rsum[:, g % 2, :, :]).then_inc(rinv_done, 1)

            def ptl(n, g):
                if not within(n, STEPS):
                    return
                wait(dve, pth_done, n + 1)
                dve.tensor_tensor(pt0_lo[:, g % 2, 0:2, :], ps_t[0:R, 0, 0:2 * T], pt0_hi[:, g % 2, 0:2, :], ALU.subtract)
                dve.tensor_tensor(pt0_lo[:, g % 2, 2:4, :], ps_t[0:R, 1, 0:2 * T], pt0_hi[:, g % 2, 2:4, :], ALU.subtract)
                dve.tensor_tensor(pt1_lo[:, g % 2, :, :], ps_t[0:R, 2, 0:G * R], pt1_hi[:, g % 2, :, :], ALU.subtract)\
                   .then_inc(ptl_done, 1)

            def yl(n, g):
                if not within(n, STEPS):
                    return
                wait(dve, yh_done, n + 1)
                for h in range(G):
                    y = dve.tensor_tensor(yt_lo[C * h:C * h + C, g, :], ps_y[C * h:C * h + C, h // 2, (h % 2) * T:(h % 2) * T + T],
                                          yt_hi[C * h:C * h + C, g, :], ALU.subtract)
                y.then_inc(yl_done, 1)

            def zl(n, g):
                if not within(n, STEPS):
                    return
                wait(dve, zh_done, n + 1)
                for half in range(2):
                    low = zs[2 * C:3 * C, g % 2, 2 * half:2 * half + 2, :]
                    q = dve.tensor_tensor(low, ps_y[2 * C:3 * C, half, 0:2 * T], low, ALU.subtract)
                q.then_inc(zl_done, 1)

            def residual(b):
                if not within(b, B):
                    return
                wait(dve, wu_done, b + 1)
                wait(dve, xb_done, b + 1)
                for c in range(TC):
                    dve.tensor_tensor(r[:, c, :], ps_y[0:R, c, :], xb[:, c, :], ALU.add).then_inc(r_done, 1)

            def statistics(b):
                if not within(b, B):
                    return
                for c in range(TC):
                    wait(dve, r_done, TC * b + c + 1)
                    dve.bn_stats(stats[:, c, :], r[:, c, :]).then_inc(stats_done, 1)
                for c in range(TC):
                    dve.wait_ge(prep_act, 1)
                    wait(dve, stats_done, TC * b + c + 1)
                    dve.bn_aggr(mv[:, c, :], stats[:, c, :]).then_inc(mv_done, 1)
                wait(dve, mv_done, TC * (b + 1))
                dve.tensor_scalar(veps[:, :, 0], mv[:, :, 1], EPS, None, ALU.add).then_inc(veps_done, 1)

            def norm(b):
                if not within(b, B):
                    return
                wait(dve, rstd_done, b + 1)
                wait(dve, stored, 16 * b)
                for c in range(TC):
                    dve.tensor_scalar(xn[:, c, :], r[:, c, :], mv[:, c, 0:1], rstd[:, c, :], ALU.subtract, ALU.mult)\
                       .then_inc(xn_done, 1)

            xh(0, 0, 0)
            xh(1, 1, 0)
            zl(0, 0)
            zl(1, 1)

            def steps(b):
                for g in range(NG):
                    n = NG * b + g
                    smax(n, g)
                    xh(n + 2, (g + 2) % NG, b + (g + 2) // NG)
                    if g == 3:
                        norm(b - 1)
                    inverse(n, g)
                    ptl(n - 1, (g - 1) % NG)
                    if g == 2:
                        residual(b - 1)
                    yl(n - 2, (g - 2) % NG)
                    zl(n + 2, (g + 2) % NG)
                    vh(n, g, b)
                    if g == 2:
                        statistics(b - 1)

            steps(0)
            with dve.Fori(1, B - 1) as b:
                steps(b)
            steps(B - 1)
            steps(B)

        @block.gpsimd
        def _(pool):
            pool.memset(wv_diag[:], 0.0).then_inc(const_ready, 1)
            pool.memset(identity[:], 1.0).then_inc(const_ready, 1)
            pool.memset(mask[:], 0.0).then_inc(const_ready, 1)
            pool.memset(mhalf[:], -0.5).then_inc(const_ready, 1)
            pool.wait_ge(const_ready, 4)
            pool.affine_select(out=identity[:], in_=identity[:], compare_op=ALU.is_equal, fill=0.0, base=0,
                               pattern=[[-1, 128]], channel_multiplier=1).then_inc(prep_id, 1)
            pool.affine_select(out=mask[:], in_=mask[:], compare_op=ALU.is_ge, fill=NEG, base=0,
                               pattern=[[0, G], [-1, R]], channel_multiplier=1).then_inc(prep_id, 1)
            pool.wait_ge(prep_id, 2)
            pool.tensor_copy(identity_b[:], identity[0:R, 0:R]).then_inc(const_ready, 1)
            pool.wait_ge(bu_in, 16)

            def xl(n, g):
                if not within(n, STEPS):
                    return
                wait(pool, xh_done, n + 1)
                wait(pool, norm_done, 2 * (n - 2))
                wait(pool, vl_done, n - 2)
                low = xs[C:2 * C, g % 2, :, :]
                pool.tensor_tensor(low, xs_raw[C:2 * C, g % 2, :, :], low, ALU.subtract).then_inc(xl_done, 1)

            def vl(n, g):
                if not within(n, STEPS):
                    return
                wait(pool, vh_done, n + 1)
                wait(pool, pv_done, n - 1)
                pool.tensor_tensor(v_lo[:, g % 2, :, :], v_raw[:, g % 2, :, :], v_hi[:, g % 2, :, :], ALU.subtract)\
                    .then_inc(vl_done, 1)

            def normalise(n, g):
                if not within(n, STEPS):
                    return
                wait(pool, rinv_done, n + 1)
                wait(pool, xl_done, min(n + 3, STEPS) if isinstance(n, int) else n + 3)
                for c, p, w in ((0, p0, R), (1, p1, T)):
                    inv = rinv[:, g % 2, c, :].rearrange("p (h a) -> p h a", a=1).to_broadcast((R, G, w))
                    pool.tensor_tensor(p[:, g % 2, :, :], p[:, g % 2, :, :], inv, ALU.mult).then_inc(norm_done, 1)

            def residual_bias(b):
                if not within(b, B):
                    return
                wait(pool, res_in, 16 * (b + 1))
                wait(pool, r_done, TC * b)
                pool.tensor_tensor(xb[:], xres[:], bu_all[:, :].rearrange("p (a d) -> p a d", a=1).to_broadcast((R, TC, D)), ALU.add)\
                    .then_inc(xb_done, 1)
                wait(pool, xb_done, b + 1)

            def power(b):
                if not within(b, B):
                    return
                wait(pool, veps_done, b + 1)
                wait(pool, xn_done, TC * b)
                pool.tensor_tensor(rstd[:], veps[:], mhalf[:], ALU.pow).then_inc(rstd_done, 1)
                wait(pool, rstd_done, b + 1)

            xl(0, 0)
            xl(1, 1)

            def steps(b):
                for g in range(NG):
                    n = NG * b + g
                    xl(n + 2, (g + 2) % NG)
                    normalise(n, g)
                    vl(n, g)
                    if g == 2:
                        power(b - 1)
                    if g == 3:
                        residual_bias(b)

            steps(0)
            with pool.Fori(1, B - 1) as b:
                steps(b)
            steps(B - 1)
            steps(B)


def split_weights(nc, name, plan, extra=None):
    with ExitStack() as ctx:
        raw = [ctx.enter_context(nc.sbuf_tensor(f"{name}_raw{i}", [128, KC, D], F32)) for i in range(2)]
        landed = [ctx.enter_context(nc.semaphore(f"{name}_landed{i}")) for i in range(2)]
        rounded = ctx.enter_context(nc.semaphore(f"{name}_rounded"))
        split = ctx.enter_context(nc.semaphore(f"{name}_split"))
        block = ctx.enter_context(nc.Block())

        @block.sync
        def _(sp):
            for i, (dram, _, _) in enumerate(plan):
                wait(sp, split, i - 1)
                sp.dma_start(raw[i % 2][:], dram.rearrange("(k p) e -> p k e", p=128)).then_inc(landed[i % 2], 16)

        @block.scalar
        def _(act):
            for i, (_, hi, _) in enumerate(plan):
                act.wait_ge(landed[i % 2], 16 * (i // 2 + 1))
                act.activation(hi[:], raw[i % 2][:], ACT.Copy).then_inc(rounded, 1)

        @block.vector
        def _(dve):
            for i, (_, hi, lo) in enumerate(plan):
                dve.wait_ge(rounded, i + 1)
                dve.tensor_tensor(lo[:], raw[i % 2][:], hi[:], ALU.subtract).then_inc(split, 1)


def cross_attention(nc, io, x1, x2):
    with ExitStack() as ctx:
        def sb(name, shape, dt=F32):
            return ctx.enter_context(nc.sbuf_tensor("x_" + name, shape, dt))

        def sem(name):
            return ctx.enter_context(nc.semaphore("x_" + name))

        identity = sb("identity", [128, 128])
        m_hi = sb("m_hi", [128, KC, D], F32R)
        m_lo = sb("m_lo", [128, KC, D], F32R)
        wv_hi = sb("wv_hi", [128, KC, D], F32R)
        wv_lo = sb("wv_lo", [128, KC, D], F32R)
        zbias = sb("zbias", [128, KC])
        kbias = sb("kbias", [R, D])
        qk_bias = sb("qk_bias", [R, 1])
        bv_all = sb("bv_all", [R, D])
        mhalf = sb("mhalf", [R, TC, 1])

        split_weights(nc, "x_wv", [(io["xwv_t"], wv_hi, wv_lo)])
        weight_products(nc, io, identity, m_hi, m_lo, zbias, kbias, qk_bias, bv_all, mhalf)

        x1_raw = sb("x1_raw", [R, TC, D])
        x1b = sb("x1b", [R, TC, D])
        x1t_hi = sb("x1t_hi", [128, KC, T], F32R)
        x1t_lo = sb("x1t_lo", [128, KC, T], F32R)
        zt_hi = sb("zt_hi", [128, KC, T], F32R)
        zt_lo = sb("zt_lo", [128, KC, T], F32R)
        ct_raw = sb("ct_raw", [128, KC, TX])
        ct_hi = sb("ct_hi", [128, KC, TX + 2], F32R)
        ct_lo = sb("ct_lo", [128, KC, TX + 2], F32R)
        cx_raw = sb("cx_raw", [XR, XC, D])
        cx_hi = sb("cx_hi", [XR, XC, D], F32R)
        cx_lo = sb("cx_lo", [XR, XC, D], F32R)
        dot = sb("dot", [R, D])
        rowdot = sb("rowdot", [R, TC])
        rowbias = sb("rowbias", [R, TC])
        smax = sb("smax", [R, TC])
        biased_max = sb("biased_max", [R, TC])
        shift = sb("shift", [R, TC])
        rsum = sb("rsum", [R, TC])
        rinv = sb("rinv", [R, TC])
        p = sb("p", [R, TC, TX])
        pt_hi = sb("pt_hi", [XR, XC, T], F32R)
        pt_lo = sb("pt_lo", [XR, XC, T], F32R)
        ot_hi = sb("ot_hi", [128, KC, T], F32R)
        ot_lo = sb("ot_lo", [128, KC, T], F32R)
        r = sb("r", [R, TC, D])
        stats = sb("stats", [R, TC, 6])
        mv = sb("mv", [R, TC, 2])
        veps = sb("veps", [R, TC, 1])
        rstd = sb("rstd", [R, TC, 1])
        xn = sb("xn", [R, TC, D])

        ps_s = ctx.enter_context(nc.psum_tensor("x_ps_s", [128, 4, 512], F32))
        ps_g = ctx.enter_context(nc.psum_tensor("x_ps_g", [128, 2, 512], F32))
        ps_h = ctx.enter_context(nc.psum_tensor("x_ps_h", [128, 2, 512], F32))

        pad_done = sem("pad_done")
        x1_in = sem("x1_in")
        ct_in = sem("ct_in")
        cx_in = sem("cx_in")
        x1b_done = sem("x1b_done")
        x1t_done = sem("x1t_done")
        x1th_done = sem("x1th_done")
        x1tl_done = sem("x1tl_done")
        cth_done = sem("cth_done")
        ctl_done = sem("ctl_done")
        cxh_done = sem("cxh_done")
        cxl_done = sem("cxl_done")
        zt_done = sem("zt_done")
        zth_done = sem("zth_done")
        ztl_done = sem("ztl_done")
        s_done = sem("s_done")
        dot_done = sem("dot_done")
        rowbias_done = sem("rowbias_done")
        max_done = sem("max_done")
        biased_done = sem("biased_done")
        shift_done = sem("shift_done")
        exp_done = sem("exp_done")
        rinv_done = sem("rinv_done")
        pt_done = sem("pt_done")
        pth_done = sem("pth_done")
        ptl_done = sem("ptl_done")
        ot_done = sem("ot_done")
        oth_done = sem("oth_done")
        otl_done = sem("otl_done")
        out_done = sem("out_done")
        r_done = sem("r_done")
        stats_done = sem("stats_done")
        mv_done = sem("mv_done")
        veps_done = sem("veps_done")
        rstd_done = sem("rstd_done")
        xn_done = sem("xn_done")
        stored = sem("stored")

        block = ctx.enter_context(nc.Block())

        def pair(bank, k):
            return bank[:, k // 2, (k % 2) * T:(k % 2) * T + T]

        @block.sync
        def _(sp):
            def loads(b):
                wait(sp, x1b_done, b)
                wait(sp, x1t_done, b)
                wait(sp, rowbias_done, b)
                sp.dma_start(x1_raw[:], x1[b].rearrange("(c p) d -> p c d", p=R)).then_inc(x1_in, 16)
                wait(sp, ctl_done, KC * b)
                sp.dma_start(ct_raw[:], io["ct"][b].rearrange("(k p) t -> p k t", p=128)).then_inc(ct_in, 16)
                wait(sp, cxl_done, XC * b)
                sp.dma_start(cx_raw[:], io["cx"][b].rearrange("(c p) d -> p c d", p=XR)).then_inc(cx_in, 16)

            def store(b):
                sp.wait_ge(xn_done, TC * (b + 1))
                sp.dma_start(x2[b].rearrange("(c p) d -> p c d", p=R), xn[:]).then_inc(stored, 16)

            loads(0)
            loads(1)
            with sp.Fori(2, B) as b:
                loads(b)
                store(b - 2)
            store(B - 2)
            store(B - 1)
            sp.wait_ge(stored, 16 * B)

        @block.tensor
        def _(pe):
            pe.wait_ge(pad_done, 2)

            def x1_turn(b):
                wait(pe, x1_in, 16 * (b + 1))
                wait(pe, otl_done, b - 1)
                for k in range(KC):
                    for c in range(TC):
                        mm = pe.transpose(ps_g[:, k // 2, (k % 2) * T + c * R:(k % 2) * T + c * R + R],
                                          x1_raw[:, c, 128 * k:128 * k + 128], identity[0:R, 0:R])
                mm.then_inc(x1t_done, 1)

            def p_turn(b):
                wait(pe, exp_done, TC * (b + 1))
                for j in range(XC):
                    for c in range(TC):
                        mm = pe.transpose(ps_s[0:XR, j // 2, (j % 2) * T + c * R:(j % 2) * T + c * R + R],
                                          p[:, c, XR * j:XR * j + XR], identity[0:R, 0:R])
                mm.then_inc(pt_done, 1)

            def zt(b):
                wait(pe, x1tl_done, b + 1)
                wait(pe, r_done, TC * (b - 1))
                for ck in range(KC):
                    i = 0
                    for m, x in ((m_hi, x1t_hi), (m_lo, x1t_hi), (m_hi, x1t_lo)):
                        for k in range(KC):
                            mm = pe.matmul(pair(ps_h, ck), m[:, k, 128 * ck:128 * ck + 128], x[:, k, :],
                                           start=(i == 0), stop=(i == 3 * KC - 1))
                            i += 1
                mm.then_inc(zt_done, 1)

            def ot(b):
                wait(pe, ptl_done, b + 1)
                wait(pe, cxl_done, XC * (b + 1))
                wait(pe, x1tl_done, min(b + 2, B) if isinstance(b, int) else b + 2)
                for dk in range(KC):
                    i = 0
                    for v, q in ((cx_hi, pt_hi), (cx_lo, pt_hi), (cx_hi, pt_lo)):
                        for j in range(XC):
                            mm = pe.matmul(pair(ps_g, dk), v[:, j, 128 * dk:128 * dk + 128], q[:, j, :],
                                           start=(i == 0), stop=(i == 3 * XC - 1))
                            i += 1
                mm.then_inc(ot_done, 1)

            def s(b):
                wait(pe, ztl_done, b + 1)
                wait(pe, ctl_done, KC * (b + 1))
                wait(pe, ptl_done, b)
                for c in range(TC):
                    i = 0
                    for z, x in ((zt_hi, ct_hi), (zt_hi, ct_lo), (zt_lo, ct_hi)):
                        for k in range(KC):
                            for half in range(2):
                                mm = pe.matmul(ps_s[0:R, 2 * c + half, 0:XH + 1], z[:, k, c * R:c * R + R],
                                               x[:, k, half * XH:half * XH + XH + 1], start=(i == 0), stop=(i == 3 * KC - 1))
                            i += 1
                    mm.then_inc(s_done, 1)

            def out(b):
                wait(pe, otl_done, b + 1)
                wait(pe, ztl_done, min(b + 2, B) if isinstance(b, int) else b + 2)
                for c in range(TC):
                    i = 0
                    for y, w in ((ot_hi, wv_hi), (ot_hi, wv_lo), (ot_lo, wv_hi)):
                        for k in range(KC):
                            mm = pe.matmul(ps_h[0:R, c, :], y[:, k, c * R:c * R + R], w[:, k, :],
                                           start=(i == 0), stop=(i == 3 * KC - 1))
                            i += 1
                mm.then_inc(out_done, 1)

            def step(b):
                if within(b, B):
                    x1_turn(b)
                if within(b - 1, B):
                    p_turn(b - 1)
                if within(b, B):
                    zt(b)
                if within(b - 1, B):
                    ot(b - 1)
                if within(b, B):
                    s(b)
                if within(b - 1, B):
                    out(b - 1)

            step(0)
            with pe.Fori(1, B) as b:
                step(b)
            step(B)

        @block.scalar
        def _(act):
            def x1th(b):
                wait(act, x1t_done, b + 1)
                wait(act, zt_done, b)
                act.activation(x1t_hi[:, 0:2, :], ps_g[:, 0, 0:2 * T], ACT.Copy)
                act.activation(x1t_hi[:, 2:4, :], ps_g[:, 1, 0:2 * T], ACT.Copy).then_inc(x1th_done, 1)

            def cth(b):
                wait(act, ct_in, 16 * (b + 1))
                wait(act, s_done, TC * b)
                for k in range(KC):
                    act.activation(ct_hi[:, k, 0:TX], ct_raw[:, k, :], ACT.Copy).then_inc(cth_done, 1)

            def pth(b):
                wait(act, pt_done, b + 1)
                wait(act, ot_done, b)
                for j in range(XC // 2):
                    a = act.activation(pt_hi[:, 2 * j:2 * j + 2, :], ps_s[0:XR, j, 0:2 * T], ACT.Copy)
                a.then_inc(pth_done, 1)

            def zth(b):
                wait(act, zt_done, b + 1)
                wait(act, s_done, TC * b)
                for k in range(KC):
                    a = act.activation(zt_hi[:, k, :], pair(ps_h, k), ACT.Identity, bias=zbias[:, k:k + 1])
                a.then_inc(zth_done, 1)

            def oth(b):
                wait(act, ot_done, b + 1)
                wait(act, out_done, b)
                act.activation(ot_hi[:, 0:2, :], ps_g[:, 0, 0:2 * T], ACT.Copy)
                act.activation(ot_hi[:, 2:4, :], ps_g[:, 1, 0:2 * T], ACT.Copy).then_inc(oth_done, 1)

            def cxh(b):
                wait(act, cx_in, 16 * (b + 1))
                wait(act, ot_done, b)
                for j in range(XC):
                    act.activation(cx_hi[:, j, :], cx_raw[:, j, :], ACT.Copy).then_inc(cxh_done, 1)

            def exp(b):
                wait(act, pt_done, b)
                wait(act, rinv_done, b)
                for c in range(TC):
                    wait(act, shift_done, TC * b + c + 1)
                    act.activation(p[:, c, :].rearrange("p (a t) -> p a t", a=2), ps_s[0:R, 2 * c:2 * c + 2, 0:XH],
                                   ACT.Exp, bias=shift[:, c:c + 1], accum_out=rsum[:, c:c + 1]).then_inc(exp_done, 1)

            def step(b):
                if within(b, B):
                    x1th(b)
                    cth(b)
                if within(b - 1, B):
                    pth(b - 1)
                if within(b, B):
                    zth(b)
                if within(b - 1, B):
                    oth(b - 1)
                if within(b, B):
                    cxh(b)
                    exp(b)

            step(0)
            with act.Fori(1, B) as b:
                step(b)
            step(B)

        @block.vector
        def _(dve):
            def x1tl(b):
                wait(dve, x1th_done, b + 1)
                dve.tensor_tensor(x1t_lo[:, 0:2, :], ps_g[:, 0, 0:2 * T], x1t_hi[:, 0:2, :], ALU.subtract)
                dve.tensor_tensor(x1t_lo[:, 2:4, :], ps_g[:, 1, 0:2 * T], x1t_hi[:, 2:4, :], ALU.subtract).then_inc(x1tl_done, 1)

            def row_bias(b):
                for c in range(TC):
                    wait(dve, dot_done, TC * b + c)
                    dve.tensor_tensor_reduce(out=dot[:], in0=x1_raw[:, c, :], in1=kbias[:], scale=1.0, scalar=0.0,
                                             op0=ALU.mult, op1=ALU.add, accum_out=rowdot[:, c:c + 1]).then_inc(dot_done, 1)
                wait(dve, dot_done, TC * (b + 1))
                wait(dve, shift_done, TC * b)
                dve.tensor_scalar(rowbias[:], rowdot[:], qk_bias[:, 0:1], None, ALU.add).then_inc(rowbias_done, 1)

            def ptl(b):
                wait(dve, pth_done, b + 1)
                for j in range(XC // 2):
                    q = dve.tensor_tensor(pt_lo[:, 2 * j:2 * j + 2, :], ps_s[0:XR, j, 0:2 * T], pt_hi[:, 2 * j:2 * j + 2, :],
                                          ALU.subtract)
                q.then_inc(ptl_done, 1)

            def ztl(b):
                wait(dve, zth_done, b + 1)
                for k in range(KC):
                    q = dve.scalar_tensor_tensor(out=zt_lo[:, k, :], in0=pair(ps_h, k), scalar=zbias[:, k:k + 1],
                                                 in1=zt_hi[:, k, :], op0=ALU.add, op1=ALU.subtract)
                q.then_inc(ztl_done, 1)

            def otl(b):
                wait(dve, oth_done, b + 1)
                dve.tensor_tensor(ot_lo[:, 0:2, :], ps_g[:, 0, 0:2 * T], ot_hi[:, 0:2, :], ALU.subtract)
                dve.tensor_tensor(ot_lo[:, 2:4, :], ps_g[:, 1, 0:2 * T], ot_hi[:, 2:4, :], ALU.subtract).then_inc(otl_done, 1)

            def row_max(b):
                wait(dve, rowbias_done, b + 1)
                for c in range(TC):
                    wait(dve, s_done, TC * b + c + 1)
                    dve.tensor_reduce(smax[:, c:c + 1], ps_s[0:R, 2 * c:2 * c + 2, 0:XH], AX.XY, ALU.max).then_inc(max_done, 1)
                    wait(dve, max_done, TC * b + c + 1)
                    dve.tensor_tensor(biased_max[:, c:c + 1], smax[:, c:c + 1], rowbias[:, c:c + 1], ALU.add).then_inc(biased_done, 1)
                    wait(dve, biased_done, TC * b + c + 1)
                    wait(dve, exp_done, TC * (b - 1) + c + 1)
                    dve.tensor_tensor(shift[:, c:c + 1], rowbias[:, c:c + 1], biased_max[:, c:c + 1], ALU.subtract)\
                       .then_inc(shift_done, 1)

            def residual(b):
                wait(dve, out_done, b + 1)
                wait(dve, x1b_done, b + 1)
                for c in range(TC):
                    dve.scalar_tensor_tensor(out=r[:, c, :], in0=ps_h[0:R, c, :], scalar=rinv[:, c:c + 1], in1=x1b[:, c, :],
                                             op0=ALU.mult, op1=ALU.add).then_inc(r_done, 1)
                for c in range(TC):
                    wait(dve, r_done, TC * b + c + 1)
                    dve.bn_stats(stats[:, c, :], r[:, c, :]).then_inc(stats_done, 1)
                for c in range(TC):
                    dve.wait_ge(pad_done, 1)
                    wait(dve, stats_done, TC * b + c + 1)
                    dve.bn_aggr(mv[:, c, :], stats[:, c, :]).then_inc(mv_done, 1)
                wait(dve, mv_done, TC * (b + 1))
                dve.tensor_scalar(veps[:, :, 0], mv[:, :, 1], EPS, None, ALU.add).then_inc(veps_done, 1)

            def inverse(b):
                wait(dve, exp_done, TC * (b + 1))
                wait(dve, r_done, TC * b)
                dve.reciprocal(rinv[:], rsum[:]).then_inc(rinv_done, 1)

            def norm(b):
                wait(dve, rstd_done, b + 1)
                wait(dve, stored, 16 * b)
                for c in range(TC):
                    dve.tensor_scalar(xn[:, c, :], r[:, c, :], mv[:, c, 0:1], rstd[:, c, :], ALU.subtract, ALU.mult)\
                       .then_inc(xn_done, 1)

            def step(b):
                if within(b, B):
                    x1tl(b)
                    row_bias(b)
                if within(b - 1, B):
                    ptl(b - 1)
                if within(b, B):
                    ztl(b)
                if within(b - 1, B):
                    otl(b - 1)
                if within(b, B):
                    row_max(b)
                if within(b - 1, B):
                    residual(b - 1)
                    norm(b - 1)
                if within(b, B):
                    inverse(b)

            step(0)
            with dve.Fori(1, B) as b:
                step(b)
            step(B)

        @block.gpsimd
        def _(pool):
            pool.memset(ct_hi[:, :, TX:TX + 2].bitcast(F32), 0.0).then_inc(pad_done, 1)
            pool.memset(ct_lo[:, :, TX:TX + 2].bitcast(F32), 0.0).then_inc(pad_done, 1)

            def step(b):
                if within(b, B):
                    for k in range(KC):
                        wait(pool, cth_done, KC * b + k + 1)
                        pool.tensor_tensor(ct_lo[:, k, 0:TX], ct_raw[:, k, :], ct_hi[:, k, 0:TX], ALU.subtract).then_inc(ctl_done, 1)
                    for j in range(XC):
                        wait(pool, cxh_done, XC * b + j + 1)
                        pool.tensor_tensor(cx_lo[:, j, :], cx_raw[:, j, :], cx_hi[:, j, :], ALU.subtract).then_inc(cxl_done, 1)
                if within(b - 1, B):
                    wait(pool, veps_done, b)
                    wait(pool, xn_done, TC * (b - 1))
                    pool.tensor_tensor(rstd[:], veps[:], mhalf[:], ALU.pow).then_inc(rstd_done, 1)
                if within(b, B):
                    wait(pool, x1_in, 16 * (b + 1))
                    wait(pool, r_done, TC * b)
                    pool.tensor_tensor(x1b[:], x1_raw[:], bv_all[:, :].rearrange("p (a d) -> p a d", a=1).to_broadcast((R, TC, D)),
                                       ALU.add).then_inc(x1b_done, 1)

            step(0)
            with pool.Fori(1, B) as b:
                step(b)
            step(B)


def weight_products(nc, io, identity, m_hi, m_lo, zbias, kbias, qk_bias, bv_all, mhalf):
    with ExitStack() as ctx:
        wq = ctx.enter_context(nc.sbuf_tensor("xp_wq", [128, KC, D], F32))
        wk = ctx.enter_context(nc.sbuf_tensor("xp_wk", [128, KC, D], F32))
        bq = ctx.enter_context(nc.sbuf_tensor("xp_bq", [128, KC, 1], F32))
        bk = ctx.enter_context(nc.sbuf_tensor("xp_bk", [128, KC, 1], F32))
        bk_all = ctx.enter_context(nc.sbuf_tensor("xp_bk_all", [128, KC, R], F32))
        ones = ctx.enter_context(nc.sbuf_tensor("xp_ones", [128, R], F32))
        ps = ctx.enter_context(nc.psum_tensor("xp_ps", [128, 8, 512], F32))
        w_in = ctx.enter_context(nc.semaphore("xp_w_in"))
        made = ctx.enter_context(nc.semaphore("xp_made"))
        spread = ctx.enter_context(nc.semaphore("xp_spread"))
        mm_done = ctx.enter_context(nc.semaphore("xp_mm_done"))
        hi_done = ctx.enter_context(nc.semaphore("xp_hi_done"))
        lo_done = ctx.enter_context(nc.semaphore("xp_lo_done"))
        block = ctx.enter_context(nc.Block())

        @block.sync
        def _(sp):
            sp.dma_start(wq[:], io["xwq"].rearrange("(k p) e -> p k e", p=128)).then_inc(w_in, 16)
            sp.dma_start(wk[:], io["xwk"].rearrange("(k p) e -> p k e", p=128)).then_inc(w_in, 16)
            sp.dma_start(bv_all[:], io["xbv"].rearrange("(a d) -> a d", a=1).to_broadcast((R, D))).then_inc(w_in, 16)
            with nc.allow_non_contiguous_dma(reason="biases by partition"):
                sp.dma_start(bq[:], io["xbq"].rearrange("(k p a) -> p k a", p=128, a=1)).then_inc(w_in, 16)
                sp.dma_start(bk[:], io["xbk"].rearrange("(k p a) -> p k a", p=128, a=1)).then_inc(w_in, 16)
            sp.wait_ge(w_in, 80)

        @block.gpsimd
        def _(pool):
            pool.memset(identity[:], 1.0).then_inc(made, 1)
            pool.memset(mhalf[:], -0.5).then_inc(made, 1)
            pool.memset(ones[:], 1.0).then_inc(made, 1)
            pool.wait_ge(made, 3)
            pool.affine_select(out=identity[:], in_=identity[:], compare_op=ALU.is_equal, fill=0.0, base=0,
                               pattern=[[-1, 128]], channel_multiplier=1).then_inc(made, 1)

        @block.vector
        def _(dve):
            dve.wait_ge(made, 3)
            dve.wait_ge(w_in, 80)
            for k in range(KC):
                dve.tensor_scalar(bk_all[:, k, :], ones[:], bk[:, k, :], None, ALU.mult).then_inc(spread, 1)
            for dk in range(KC):
                dve.wait_ge(hi_done, dk + 1)
                dve.tensor_tensor(m_lo[:, dk, :], ps[:, dk, :], m_hi[:, dk, :], ALU.subtract).then_inc(lo_done, 1)
            dve.wait_ge(mm_done, KC + 1)
            dve.tensor_copy(zbias[:], ps[:, 4, 0:KC])
            dve.tensor_copy(kbias[:], ps[0:R, 5, :])
            dve.tensor_copy(qk_bias[:], ps[0:R, 6, 0:1]).then_inc(lo_done, 1)

        @block.scalar
        def _(act):
            for dk in range(KC):
                act.wait_ge(mm_done, dk + 1)
                act.activation(m_hi[:, dk, :], ps[:, dk, :], ACT.Copy).then_inc(hi_done, 1)

        @block.tensor
        def _(pe):
            pe.wait_ge(w_in, 80)
            for dk in range(KC):
                for k in range(KC):
                    mm = pe.matmul(ps[:, dk, :], wq[:, k, 128 * dk:128 * dk + 128], wk[:, k, :], start=(k == 0), stop=(k == KC - 1))
                mm.then_inc(mm_done, 1)
            pe.wait_ge(spread, KC)
            for ck in range(KC):
                for k in range(KC):
                    pe.matmul(ps[:, 4, ck:ck + 1], wk[:, k, 128 * ck:128 * ck + 128], bq[:, k, :], start=(k == 0), stop=(k == KC - 1))
            for k in range(KC):
                pe.matmul(ps[0:R, 5, :], bk_all[:, k, :], wq[:, k, :], start=(k == 0), stop=(k == KC - 1))
            for k in range(KC):
                mm = pe.matmul(ps[0:R, 6, 0:1], bk_all[:, k, :], bq[:, k, :], start=(k == 0), stop=(k == KC - 1))
            mm.then_inc(mm_done, 1)


def feed_forward(nc, io, x2, out):
    with ExitStack() as ctx:
        c_hi = ctx.enter_context(nc.sbuf_tensor("f_c_hi", [128, KC, T], F32R))
        c_lo = ctx.enter_context(nc.sbuf_tensor("f_c_lo", [128, KC, T], F32R))
        identity = ctx.enter_context(nc.sbuf_tensor("f_identity", [128, 128], F32))
        recurrence(nc, io, x2, identity, c_hi, c_lo)
        output_gate(nc, io, x2, out, identity, c_hi, c_lo)


def recurrence(nc, io, x2, identity, c_hi, c_lo):
    GATES = ("f", "i", "c")
    HC = KC // 2
    with ExitStack() as ctx:
        def sb(name, shape, dt=F32):
            return ctx.enter_context(nc.sbuf_tensor("f_" + name, shape, dt))

        def sem(name):
            return ctx.enter_context(nc.semaphore("f_" + name))

        w = {n: (sb(n + "_hi", [128, KC, D], F32R), sb(n + "_lo", [128, KC, D], F32R))
             for n in ("wf", "uf", "wi", "ui", "wc", "uc")}
        split_weights(nc, "f_w", [(io[n + "_t"], *w[n]) for n in w])

        bias = sb("bias", [128, 3, KC])
        bias_raw = sb("bias_raw", [128, 3, KC])
        c0 = sb("c0", [128, KC])
        x2_raw = sb("x2_raw", [R, TC, D])
        xt_hi = sb("xt_hi", [128, KC, T], F32R)
        xt_lo = sb("xt_lo", [128, KC, T], F32R)
        gate = sb("gate", [128, 3, KC, T])
        keep = sb("keep", [128, KC, T])
        fresh = sb("fresh", [128, KC, T])
        c = sb("c", [128, KC, T])

        ps_gate = ctx.enter_context(nc.psum_tensor("f_ps_gate", [128, 6, 512], F32))
        ps_x = ctx.enter_context(nc.psum_tensor("f_ps_x", [128, 2, 512], F32))

        made = sem("made")
        b_in = sem("b_in")
        bias_done = sem("bias_done")
        x2_in = sem("x2_in")
        xt_done = sem("xt_done")
        xth_done = sem("xth_done")
        xtl_done = sem("xtl_done")
        xpart_done = sem("xpart_done")
        gate_done = sem("gate_done")
        act_done = sem("act_done")
        c_start = sem("c_start")
        keep_done = sem("keep_done")
        fresh_done = sem("fresh_done")
        sum_done = sem("sum_done")
        c_done = sem("c_done")
        ch_done = sem("ch_done")
        cl_done = sem("cl_done")

        block = ctx.enter_context(nc.Block())

        def region(bank, k):
            return ps_gate[:, bank, k * T:k * T + T]

        @block.sync
        def _(sp):
            with nc.allow_non_contiguous_dma(reason="biases by partition"):
                for j, n in enumerate(GATES):
                    sp.dma_start(bias_raw[:, j, :], io["b" + n].rearrange("(k p) -> p k", p=128)).then_inc(b_in, 16)
                sp.dma_start(c0[:], io["in_c"].rearrange("(k p) -> p k", p=128)).then_inc(b_in, 16)

            def load(b):
                wait(sp, xt_done, b)
                sp.dma_start(x2_raw[:], x2[b].rearrange("(c p) d -> p c d", p=R)).then_inc(x2_in, 16)

            load(0)
            with sp.Fori(1, B) as b:
                load(b)

        @block.gpsimd
        def _(pool):
            pool.memset(identity[:], 1.0).then_inc(made, 1)
            pool.memset(keep[:], 0.0).then_inc(made, 1)
            pool.wait_ge(made, 2)
            pool.affine_select(out=identity[:], in_=identity[:], compare_op=ALU.is_equal, fill=0.0, base=0,
                               pattern=[[-1, 128]], channel_multiplier=1).then_inc(made, 1)

        @block.tensor
        def _(pe):
            pe.wait_ge(made, 3)

            def x_turn(b):
                wait(pe, x2_in, 16 * (b + 1))
                wait(pe, xtl_done, b)
                for k in range(KC):
                    for q in range(TC):
                        mm = pe.transpose(ps_x[:, k // 2, (k % 2) * T + q * R:(k % 2) * T + q * R + R],
                                          x2_raw[:, q, 128 * k:128 * k + 128], identity[0:R, 0:R])
                mm.then_inc(xt_done, 1)

            def x_part(b):
                wait(pe, xtl_done, b + 1)
                for half in range(2):
                    for j, n in enumerate(GATES):
                        bank = 3 * half + j
                        wait(pe, act_done, 6 * (b - 1) + bank + 1)
                        for k2 in range(HC):
                            i = 0
                            for wp, xp in ((0, xt_hi), (1, xt_hi), (0, xt_lo)):
                                for k in range(KC):
                                    m = HC * half + k2
                                    mm = pe.matmul(region(bank, k2), w["w" + n][wp][:, k, 128 * m:128 * m + 128], xp[:, k, :],
                                                   start=(k2 == 0 and i == 0), stop=False, skip_group_check=True)
                                    i += 1
                mm.then_inc(xpart_done, 1)

            def c_part(b):
                wait(pe, cl_done, 2 * (b + 1))
                for half in range(2):
                    for j, n in enumerate(GATES):
                        bank = 3 * half + j
                        for k2 in range(HC):
                            i = 0
                            for up, cp in ((0, c_hi), (1, c_hi), (0, c_lo)):
                                for k in range(KC):
                                    m = HC * half + k2
                                    mm = pe.matmul(region(bank, k2), w["u" + n][up][:, k, 128 * m:128 * m + 128], cp[:, k, :],
                                                   start=False, stop=(i == 3 * KC - 1), skip_group_check=True)
                                    i += 1
                        mm.then_inc(gate_done, 1)

            def step(b, more=True):
                x_part(b)
                if more:
                    x_turn(b + 1)
                c_part(b)

            x_turn(0)
            step(0)
            with pe.Fori(1, B - 1) as b:
                step(b)
            step(B - 1, more=False)

        @block.scalar
        def _(act):
            act.wait_ge(b_in, 64)
            act.activation(bias[:, 0:2, :], bias_raw[:, 0:2, :], ACT.Copy, scale=0.5).then_inc(bias_done, 1)
            act.activation(bias[:, 2, :], bias_raw[:, 2, :], ACT.Copy).then_inc(bias_done, 1)
            act.wait_ge(bias_done, 2)

            def xth(b):
                wait(act, xt_done, b + 1)
                wait(act, xpart_done, b)
                act.activation(xt_hi[:, 0:2, :], ps_x[:, 0, 0:2 * T], ACT.Copy)
                act.activation(xt_hi[:, 2:4, :], ps_x[:, 1, 0:2 * T], ACT.Copy).then_inc(xth_done, 1)

            def gates(b):
                for half in range(2):
                    for j in range(3):
                        wait(act, gate_done, 6 * b + 3 * half + j + 1)
                        wait(act, sum_done, 2 * (b - 1) + half + 1)
                        for k2 in range(HC):
                            m = HC * half + k2
                            a = act.activation(gate[:, j, m, :], region(3 * half + j, k2), ACT.Tanh, bias=bias[:, j, m:m + 1],
                                               scale=0.5 if j < 2 else 1.0)
                        a.then_inc(act_done, 1)

            def step(b, more=True):
                if more:
                    xth(b + 1)
                gates(b)

            xth(0)
            step(0)
            with act.Fori(1, B - 1) as b:
                step(b)
            step(B - 1, more=False)

        @block.vector
        def _(dve):
            dve.wait_ge(b_in, 64)
            dve.wait_ge(made, 2)
            for k in range(KC):
                dve.tensor_scalar(c[:, k, :], keep[:, k, :], c0[:, k:k + 1], None, ALU.add).then_inc(c_start, 1)
            dve.wait_ge(c_start, KC)
            dve.tensor_copy(c_hi[:], c[:]).then_inc(c_start, 1)
            dve.wait_ge(c_start, KC + 1)
            dve.tensor_tensor(c_lo[:], c[:], c_hi[:], ALU.subtract).then_inc(cl_done, 2)

            def xtl(b):
                wait(dve, xth_done, b + 1)
                dve.tensor_tensor(xt_lo[:, 0:2, :], ps_x[:, 0, 0:2 * T], xt_hi[:, 0:2, :], ALU.subtract)
                dve.tensor_tensor(xt_lo[:, 2:4, :], ps_x[:, 1, 0:2 * T], xt_hi[:, 2:4, :], ALU.subtract).then_inc(xtl_done, 1)

            def state(b):
                for half in range(2):
                    n = 2 * b + half
                    cols = slice(HC * half, HC * half + HC)
                    wait(dve, act_done, 6 * b + 3 * half + 1)
                    dve.scalar_tensor_tensor(out=keep[:, cols, :], in0=gate[:, 0, cols, :], scalar=1.0, in1=c[:, cols, :],
                                             op0=ALU.add, op1=ALU.mult).then_inc(keep_done, 1)
                    wait(dve, act_done, 6 * b + 3 * half + 3)
                    dve.scalar_tensor_tensor(out=fresh[:, cols, :], in0=gate[:, 1, cols, :], scalar=1.0, in1=gate[:, 2, cols, :],
                                             op0=ALU.add, op1=ALU.mult).then_inc(fresh_done, 1)
                    wait(dve, keep_done, n + 1)
                    wait(dve, fresh_done, n + 1)
                    dve.tensor_tensor(keep[:, cols, :], keep[:, cols, :], fresh[:, cols, :], ALU.add).then_inc(sum_done, 1)
                    wait(dve, sum_done, n + 1)
                    dve.tensor_scalar(c[:, cols, :], keep[:, cols, :], 0.5, None, ALU.mult).then_inc(c_done, 1)
                for half in range(2):
                    n = 2 * b + half
                    cols = slice(HC * half, HC * half + HC)
                    wait(dve, c_done, n + 1)
                    wait(dve, gate_done, 6 * (b + 1))
                    dve.tensor_copy(c_hi[:, cols, :], c[:, cols, :]).then_inc(ch_done, 1)
                    wait(dve, ch_done, n + 1)
                    dve.tensor_tensor(c_lo[:, cols, :], c[:, cols, :], c_hi[:, cols, :], ALU.subtract).then_inc(cl_done, 1)

            def step(b, more=True):
                if more:
                    xtl(b + 1)
                state(b)

            xtl(0)
            step(0)
            with dve.Fori(1, B - 1) as b:
                step(b)
            step(B - 1, more=False)


def output_gate(nc, io, x2, out, identity, c_hi, c_lo):
    with ExitStack() as ctx:
        def sb(name, shape, dt=F32):
            return ctx.enter_context(nc.sbuf_tensor("o_" + name, shape, dt))

        def sem(name):
            return ctx.enter_context(nc.semaphore("o_" + name))

        wo = (sb("wo_hi", [128, KC, D], F32R), sb("wo_lo", [128, KC, D], F32R))
        uo = (sb("uo_hi", [128, KC, D], F32R), sb("uo_lo", [128, KC, D], F32R))
        split_weights(nc, "o_w", [(io["uo_t"], *uo), (io["wo_t"], *wo)])

        bo_all = sb("bo_all", [R, D])
        mhalf = sb("mhalf", [R, TC, 1])
        base = sb("base", [R, TC, D])
        x2_raw = sb("x2_raw", [R, 2, TC, D])
        xt_hi = sb("xt_hi", [128, 2, KC, T], F32R)
        xt_lo = sb("xt_lo", [128, 2, KC, T], F32R)
        pre = sb("pre", [R, 2, TC, D])
        h = sb("h", [R, 2, TC, D])
        r = sb("r", [R, 2, TC, D])
        stats = sb("stats", [R, 2, TC, 6])
        mv = sb("mv", [R, 2, TC, 2])
        veps = sb("veps", [R, 2, TC, 1])
        rstd = sb("rstd", [R, 2, TC, 1])
        y = sb("y", [R, 2, TC, D])

        ps_x = ctx.enter_context(nc.psum_tensor("o_ps_x", [128, 2, 2, 512], F32))
        ps_o = ctx.enter_context(nc.psum_tensor("o_ps_o", [128, 2, 2, 512], F32))

        made = sem("made")
        bo_in = sem("bo_in")
        x2_in = [sem(f"x2_in{i}") for i in range(2)]
        base_mm = sem("base_mm")
        base_done = sem("base_done")
        xt_done = sem("xt_done")
        xth_done = sem("xth_done")
        xtl_done = sem("xtl_done")
        o_done = sem("o_done")
        pre_done = sem("pre_done")
        h_done = sem("h_done")
        r_done = sem("r_done")
        stats_done = sem("stats_done")
        mv_done = sem("mv_done")
        veps_done = sem("veps_done")
        rstd_done = sem("rstd_done")
        y_done = sem("y_done")
        stored = [sem(f"stored{i}") for i in range(2)]

        block = ctx.enter_context(nc.Block())


        @block.sync
        def _(sp):
            sp.dma_start(bo_all[:], io["bo"].rearrange("(a d) -> a d", a=1).to_broadcast((R, D))).then_inc(bo_in, 16)

            def load(i, s):
                wait(sp, r_done, 2 * i + s - 1)
                sp.dma_start(x2_raw[:, s, :, :], x2[2 * i + s].rearrange("(c p) d -> p c d", p=R)).then_inc(x2_in[s], 16)

            def store(i, s):
                sp.wait_ge(y_done, 2 * i + s + 1)
                sp.dma_start(out[2 * i + s].rearrange("(c p) d -> p c d", p=R), y[:, s, :, :]).then_inc(stored[s], 16)

            for s in range(2):
                load(0, s)
            with sp.Fori(1, B // 2) as i:
                for s in range(2):
                    load(i, s)
                    store(i - 1, s)
            for s in range(2):
                store(B // 2 - 1, s)
            for s in range(2):
                sp.wait_ge(stored[s], 16 * (B // 2))

        @block.tensor
        def _(pe):
            for q in range(TC):
                i = 0
                for cp, up in ((c_hi, 0), (c_hi, 1), (c_lo, 0)):
                    for k in range(KC):
                        mm = pe.matmul(ps_o[0:R, 0, q, :], cp[:, k, q * R:q * R + R], uo[up][:, k, :],
                                       start=(i == 0), stop=(i == 3 * KC - 1))
                        i += 1
            mm.then_inc(base_mm, 1)

            def turn(i, s):
                n = 2 * i + s
                wait(pe, x2_in[s], 16 * (i + 1))
                wait(pe, xtl_done, n - 1)
                for k in range(KC):
                    for q in range(TC):
                        mm = pe.transpose(ps_x[:, s, k // 2, (k % 2) * T + q * R:(k % 2) * T + q * R + R],
                                          x2_raw[:, s, q, 128 * k:128 * k + 128], identity[0:R, 0:R])
                mm.then_inc(xt_done, 1)

            def product(i, s):
                n = 2 * i + s
                wait(pe, xtl_done, n + 1)
                wait(pe, pre_done, n - 1)
                if s == 0:
                    pe.wait_ge(base_done, 1)
                for q in range(TC):
                    j = 0
                    for xp, wp in ((xt_hi, 0), (xt_hi, 1), (xt_lo, 0)):
                        for k in range(KC):
                            mm = pe.matmul(ps_o[0:R, s, q, :], xp[:, s, k, q * R:q * R + R], wo[wp][:, k, :],
                                           start=(j == 0), stop=(j == 3 * KC - 1))
                            j += 1
                mm.then_inc(o_done, 1)

            turn(0, 0)

            def step(i, more=True):
                turn(i, 1)
                product(i, 0)
                if more:
                    turn(i + 1, 0)
                product(i, 1)

            step(0)
            with pe.Fori(1, B // 2 - 1) as i:
                step(i)
            step(B // 2 - 1, more=False)

        @block.scalar
        def _(act):
            def xth(i, s):
                n = 2 * i + s
                wait(act, xt_done, n + 1)
                wait(act, o_done, n - 1)
                for k in range(2):
                    a = act.activation(xt_hi[:, s, 2 * k:2 * k + 2, :], ps_x[:, s, k, 0:2 * T], ACT.Copy)
                a.then_inc(xth_done, 1)

            def tanh(i, s):
                n = 2 * i + s
                wait(act, pre_done, n + 1)
                wait(act, r_done, n - 1)
                act.activation(h[:, s, :, :], pre[:, s, :, :], ACT.Tanh).then_inc(h_done, 1)

            xth(0, 0)

            def step(i, more=True):
                xth(i, 1)
                tanh(i, 0)
                if more:
                    xth(i + 1, 0)
                tanh(i, 1)

            step(0)
            with act.Fori(1, B // 2 - 1) as i:
                step(i)
            step(B // 2 - 1, more=False)

        @block.vector
        def _(dve):
            dve.wait_ge(base_mm, 1)
            dve.wait_ge(bo_in, 16)
            dve.tensor_tensor(base[:], ps_o[0:R, 0, :, :], bo_all[:, :].rearrange("p (a d) -> p a d", a=1).to_broadcast((R, TC, D)),
                              ALU.add).then_inc(base_done, 1)
            dve.wait_ge(base_done, 1)

            def xtl(i, s):
                n = 2 * i + s
                wait(dve, xth_done, n + 1)
                for k in range(2):
                    v = dve.tensor_tensor(xt_lo[:, s, 2 * k:2 * k + 2, :], ps_x[:, s, k, 0:2 * T], xt_hi[:, s, 2 * k:2 * k + 2, :],
                                          ALU.subtract)
                v.then_inc(xtl_done, 1)

            def with_base(i, s):
                n = 2 * i + s
                wait(dve, o_done, n + 1)
                wait(dve, h_done, n - 1)
                dve.tensor_tensor(pre[:, s, :, :], ps_o[0:R, s, :, :], base[:], ALU.add).then_inc(pre_done, 1)

            def statistics(i, s):
                n = 2 * i + s
                wait(dve, r_done, n + 1)
                for q in range(TC):
                    v = dve.bn_stats(stats[:, s, q, :], r[:, s, q, :])
                v.then_inc(stats_done, 1)
                dve.wait_ge(base_done, 1)
                wait(dve, stats_done, n + 1)
                for q in range(TC):
                    v = dve.bn_aggr(mv[:, s, q, :], stats[:, s, q, :])
                v.then_inc(mv_done, 1)
                wait(dve, mv_done, n + 1)
                dve.tensor_scalar(veps[:, s, :, 0], mv[:, s, :, 1], EPS, None, ALU.add).then_inc(veps_done, 1)

            def norm(i, s):
                n = 2 * i + s
                wait(dve, rstd_done, n + 1)
                wait(dve, stored[s], 16 * i)
                for q in range(TC):
                    v = dve.tensor_scalar(y[:, s, q, :], r[:, s, q, :], mv[:, s, q, 0:1], rstd[:, s, q, :], ALU.subtract, ALU.mult)
                v.then_inc(y_done, 1)

            xtl(0, 0)

            def step(i, more=True, first=False):
                xtl(i, 1)
                with_base(i, 0)
                if not first:
                    statistics(i - 1, 1)
                    norm(i - 1, 1)
                if more:
                    xtl(i + 1, 0)
                with_base(i, 1)
                statistics(i, 0)
                norm(i, 0)

            step(0, first=True)
            with dve.Fori(1, B // 2 - 1) as i:
                step(i)
            step(B // 2 - 1, more=False)
            statistics(B // 2 - 1, 1)
            norm(B // 2 - 1, 1)

        @block.gpsimd
        def _(pool):
            pool.memset(mhalf[:], -0.5).then_inc(made, 1)
            pool.wait_ge(made, 1)

            def residual(i, s):
                n = 2 * i + s
                wait(pool, h_done, n + 1)
                wait(pool, y_done, n - 1)
                pool.tensor_tensor(r[:, s, :, :], h[:, s, :, :], x2_raw[:, s, :, :], ALU.add).then_inc(r_done, 1)

            def power(i, s):
                n = 2 * i + s
                wait(pool, veps_done, n + 1)
                wait(pool, y_done, n - 1)
                pool.tensor_tensor(rstd[:, s, :, :], veps[:, s, :, :], mhalf[:], ALU.pow).then_inc(rstd_done, 1)

            def step(i, first=False):
                residual(i, 0)
                if not first:
                    power(i - 1, 1)
                residual(i, 1)
                power(i, 0)

            step(0, first=True)
            with pool.Fori(1, B // 2) as i:
                step(i)
            power(B // 2 - 1, 1)


def decoder(nc, io, out):
    x1 = nc.dram_tensor("x1_scratch", (B, T, D), F32, kind="Internal").ap()
    x2 = nc.dram_tensor("x2_scratch", (B, T, D), F32, kind="Internal").ap()
    self_attention(nc, io, x1)
    cross_attention(nc, io, x1, x2)
    feed_forward(nc, io, x2, out)


def kernel(**inputs):
    from concourse import bacc
    from concourse.bass_utils import run_bass_kernel_spmd

    a = {k: np.asarray(v) for k, v in inputs.items()}
    laid_out = {
        "x": a["x"],
        "xt": a["x"].reshape(B, T, H, C).transpose(0, 3, 2, 1),
        "cx": a["ctx_1024"],
        "ct": a["ctx_1024"].transpose(0, 2, 1),
        "wq": a["L0_attn_Wq"],
        "wk": a["L0_attn_Wk"],
        "wv": a["L0_attn_Wv"],
        "wu_t": a["L0_attn_Wu"].T,
        "bu": a["L0_attn_bu"],
        "xwq": a["L0_xattn_Wq"],
        "xwk": a["L0_xattn_Wk"],
        "xwv_t": a["L0_xattn_Wv"].T,
        "xbq": a["L0_xattn_bq"],
        "xbk": a["L0_xattn_bk"],
        "xbv": a["L0_xattn_bv"],
        "in_c": a["L0_ffn_in_c"],
    }
    for n in "fico":
        laid_out["w" + n + "_t"] = a["L0_ffn_w" + n].T
        laid_out["u" + n + "_t"] = a["L0_ffn_u" + n].T
        laid_out["b" + n] = a["L0_ffn_b" + n]

    nc = bacc.Bacc("TRN2", target_bir_lowering=False, num_devices=1)
    arrays, io = {}, {}
    for name, array in laid_out.items():
        arrays["in_" + name] = np.ascontiguousarray(array)
        io[name] = nc.dram_tensor("in_" + name, array.shape, F32, kind="ExternalInput").ap()
    out = nc.dram_tensor("out", (B, T, D), F32, kind="ExternalOutput").ap()
    decoder(nc, io, out)
    result = run_bass_kernel_spmd(nc, [arrays], core_ids=[0])
    return result.results[0]["out"]
```

```python
from contextlib import ExitStack

import numpy as np
import concourse.bass as bass
from concourse import mybir

F32 = mybir.dt.float32
F32R = mybir.dt.float32r
BF16 = mybir.dt.bfloat16
ALU = mybir.AluOpType
ACT = mybir.ActivationFunctionType
AX = mybir.AxisListType

B, T, D = 16, 224, 512
H, C = 16, 32
TC = 2
R = T // TC
KC = D // 128
TX = 750
XC, XR = 6, 125
XH = TX // 2
G = 4
NG = H // G
NEG = -1.0e30
EPS = 1e-5


def wait(eng, sem, value):
    if not (isinstance(value, int) and value <= 0):
        eng.wait_ge(sem, value)


def within(n, end):
    return not isinstance(n, int) or 0 <= n < end


def load_weight(sp, buffer, landed, dram):
    sp.dma_start(buffer[:], dram.rearrange("(k p) e -> p k e", p=128)).then_inc(landed, 16)


def self_attention(nc, io, x1, raw, raw_in):
    with ExitStack() as ctx:
        def sb(name, shape, dt=F32):
            return ctx.enter_context(nc.sbuf_tensor("a_" + name, shape, dt))

        def sem(name):
            return ctx.enter_context(nc.semaphore("a_" + name))

        identity = sb("identity", [128, 128])
        identity_b = sb("identity_b", [R, R], BF16)
        mask = sb("mask", [R, G, R], BF16)
        wq3 = sb("wq3", [C, 3, C])
        wk3 = sb("wk3", [C, 3, C])
        a_f = sb("a_f", [3 * C, 3 * C])
        a_stack = sb("a_stack", [3 * C, 3 * C], F32R)
        wv_diag = sb("wv_diag", [128, 128])
        wu_raw = sb("wu_raw", [128, KC, D])
        w_hi = sb("w_hi", [128, KC, D], F32R)
        w_lo = sb("w_lo", [128, KC, D], F32R)
        identity_r = sb("identity_r", [R, R], F32R)
        bu_all = sb("bu_all", [R, D])
        bu_hi = sb("bu_hi", [R, D], F32R)
        bu_lo = sb("bu_lo", [R, D], F32R)
        xs_raw = sb("xs_raw", [3 * C, NG, G, T])
        xs = sb("xs", [3 * C, NG, G, T], F32R)
        v_raw = sb("v_raw", [R, NG, TC, 128])
        v_hi = sb("v_hi", [R, 2, TC, 128], F32R)
        v_lo = sb("v_lo", [R, 2, TC, 128], F32R)
        zs = sb("zs", [3 * C, 2, G, T], F32R)
        nmax = sb("nmax", [R, 2, TC, G])
        rsum = sb("rsum", [R, 2, TC, G])
        rinv = sb("rinv", [R, 2, TC, G])
        p0 = sb("p0", [R, 2, G, R])
        p1 = sb("p1", [R, 2, G, T])
        pt0_hi = sb("pt0_hi", [R, 2, G, T], F32R)
        pt0_lo = sb("pt0_lo", [R, 2, G, T], F32R)
        pt1_hi = sb("pt1_hi", [R, 2, G, R], F32R)
        pt1_lo = sb("pt1_lo", [R, 2, G, R], F32R)
        yt_hi = sb("yt_hi", [128, NG, T], F32R)
        yt_lo = sb("yt_lo", [128, NG, T], F32R)
        xres = sb("xres", [R, TC, D])
        r = sb("r", [R, TC, D])
        stats = sb("stats", [R, TC, 6])
        mv = sb("mv", [R, TC, 2])
        veps = sb("veps", [R, TC, 1])
        mhalf = sb("mhalf", [R, TC, 1])
        rstd = sb("rstd", [R, TC, 1])
        xn = sb("xn", [R, TC, D])

        ps_s = ctx.enter_context(nc.psum_tensor("a_ps_s", [128, 3, 512], F32))
        ps_t = ctx.enter_context(nc.psum_tensor("a_ps_t", [128, 3, 512], F32))
        ps_y = ctx.enter_context(nc.psum_tensor("a_ps_y", [128, 2, 512], F32))

        const_ready = sem("const_ready")
        w_in = sem("w_in")
        diag_in = sem("diag_in")
        bu_in = sem("bu_in")
        prep_id = sem("prep_id")
        prep_mm = sem("prep_mm")
        prep_act = sem("prep_act")
        prep_dve = sem("prep_dve")
        xs_in = [sem(f"xs_in{i}") for i in range(NG)]
        v_in = [sem(f"v_in{i}") for i in range(NG)]
        res_in = sem("res_in")
        xh_done = sem("xh_done")
        xl_done = sem("xl_done")
        vh_done = sem("vh_done")
        vl_done = sem("vl_done")
        z_done = sem("z_done")
        zh_done = sem("zh_done")
        zl_done = sem("zl_done")
        s_done = sem("s_done")
        max_done = sem("max_done")
        exp_done = sem("exp_done")
        rinv_done = sem("rinv_done")
        norm_done = sem("norm_done")
        t_done = sem("t_done")
        pth_done = sem("pth_done")
        ptl_done = sem("ptl_done")
        pv_done = sem("pv_done")
        yh_done = sem("yh_done")
        yl_done = sem("yl_done")
        wu_done = sem("wu_done")
        r_done = sem("r_done")
        stats_done = sem("stats_done")
        mv_done = sem("mv_done")
        veps_done = sem("veps_done")
        rstd_done = sem("rstd_done")
        xn_done = sem("xn_done")
        stored = sem("stored")

        STEPS = B * NG
        block = ctx.enter_context(nc.Block())

        @block.sync
        def _(sp):
            for j in range(3):
                sp.dma_start(wq3[:, j, :], io["wq"]).then_inc(w_in, 16)
                sp.dma_start(wk3[:, j, :], io["wk"]).then_inc(w_in, 16)
            sp.dma_start(wu_raw[:], io["wu_t"].rearrange("(k p) e -> p k e", p=128)).then_inc(w_in, 16)
            sp.wait_ge(const_ready, 1)
            for g in range(G):
                sp.dma_start(wv_diag[C * g:C * g + C, C * g:C * g + C], io["wv"]).then_inc(diag_in, 16)
            sp.dma_start(bu_all[:], io["bu"].rearrange("(a d) -> a d", a=1).to_broadcast((R, D))).then_inc(bu_in, 16)

            def loads(b, g):
                n = NG * b + g
                wait(sp, xl_done, n - 3)
                for j in range(3):
                    sp.dma_start(xs_raw[C * j:C * j + C, g, :, :],
                                 io["xt"][b, :, G * g:G * g + G, :]).then_inc(xs_in[g], 16)
                if g == 3 and within(b - 1, B):
                    wait(sp, r_done, TC * (b - 1))
                if g >= 2:
                    values(b, g - 2)
                elif within(b - 1, B):
                    values(b - 1, g + 2)
                if g == 2 and within(b - 3, B):
                    store(b - 3)
                if g == 3 and within(b - 1, B):
                    residual_input(b - 1)

            def values(b, g):
                wait(sp, vl_done, NG * b + g - 3)
                sp.dma_start(v_raw[:, g, :, :], io["x"][b, :, 128 * g:128 * g + 128]
                             .rearrange("(c p) d -> p c d", p=R)).then_inc(v_in[g], 16)

            def residual_input(b):
                sp.dma_start(xres[:], io["x"][b].rearrange("(c p) d -> p c d", p=R)).then_inc(res_in, 16)

            def store(b):
                sp.wait_ge(xn_done, TC * (b + 1))
                sp.dma_start(x1[b].rearrange("(c p) d -> p c d", p=R), xn[:]).then_inc(stored, 16)

            for b in range(3):
                for g in range(NG):
                    loads(b, g)
            for i, name in enumerate(("xwq", "xwk", "xwv_t")):
                load_weight(sp, raw[i], raw_in[i], io[name])
            with sp.Fori(3, B) as b:
                for g in range(NG):
                    loads(b, g)
            values(B - 1, 2)
            values(B - 1, 3)
            sp.wait_ge(r_done, TC * (B - 1))
            residual_input(B - 1)
            for b in range(B - 3, B):
                store(b)
            sp.wait_ge(stored, 16 * B)

        @block.tensor
        def _(pe):
            pe.wait_ge(const_ready, 5)
            pe.wait_ge(w_in, 7 * 16)
            pe.wait_ge(diag_in, 4 * 16)
            pe.matmul(ps_y[0:3 * C, 0, 0:3 * C], wq3[:, :, :], wk3[:, :, :], start=True, stop=True).then_inc(prep_mm, 1)
            for k in range(KC):
                if k >= 2:
                    pe.wait_ge(prep_dve, k)
                pe.matmul(ps_s[:, k % 2, :], wv_diag[:], wu_raw[:, k, :], start=True, stop=True).then_inc(prep_mm, 1)


            def z(n, g):
                if not within(n, STEPS):
                    return
                wait(pe, xl_done, n + 1)
                for half in range(2):
                    wait(pe, zl_done, 2 * (n - 1) + half + 1)
                    wait(pe, yl_done, 2 * (n - 5) + half + 1)
                    pe.matmul(ps_y[0:3 * C, half, 0:2 * T], a_stack[:], xs[:, g, 2 * half:2 * half + 2, :],
                              start=True, stop=True).then_inc(z_done, 1)

            def s(n, g):
                if not within(n, STEPS):
                    return
                wait(pe, zl_done, 2 * (n + 1))
                wait(pe, exp_done, 3 * (n - 1) + 1)
                for h in range(G):
                    pe.matmul(ps_s[0:R, 0, h * R:h * R + R], zs[:, g % 2, h, 0:R], xs[:, g, h, 0:R],
                              start=(h == 0), stop=False, skip_group_check=True)
                pe.matmul(ps_s[0:R, 0, 0:G * R], identity_b[:], mask[:, :, :], start=False, stop=True,
                          skip_group_check=True).then_inc(s_done, 1)
                for half in range(2):
                    wait(pe, exp_done, 3 * (n - 1) + half + 2)
                    for h in range(2):
                        pe.matmul(ps_s[0:R, 1 + half, h * T:h * T + T], zs[:, g % 2, 2 * half + h, R:T],
                                  xs[:, g, 2 * half + h, :], start=(h == 0), stop=False, skip_group_check=True)
                    diagonal = ps_s[0:R, 1 + half, 0:2 * T].rearrange("p (h t) -> p h t", h=2)[:, :, R:T]
                    pe.matmul(diagonal, identity_b[:], mask[:, 0:2, :], start=False, stop=True,
                              skip_group_check=True).then_inc(s_done, 1)

            def t(n, g):
                if not within(n, STEPS):
                    return
                wait(pe, norm_done, 2 * (n + 1))
                for half in range(2):
                    wait(pe, ptl_done, 3 * (n - 1) + half + 1)
                    for h in (2 * half, 2 * half + 1):
                        at = (h % 2) * T
                        pe.transpose(ps_t[0:R, half, at:at + R], p0[:, g % 2, h, :], identity[0:R, 0:R])
                        mm = pe.transpose(ps_t[0:R, half, at + R:at + T], p1[:, g % 2, h, 0:R], identity[0:R, 0:R])
                    mm.then_inc(t_done, 1)
                wait(pe, ptl_done, 3 * n)
                for h in range(G):
                    mm = pe.transpose(ps_t[0:R, 2, h * R:h * R + R], p1[:, g % 2, h, R:T], identity[0:R, 0:R])
                mm.then_inc(t_done, 1)

            def pv(n, g, b):
                if not within(n, STEPS):
                    return
                wait(pe, ptl_done, 3 * (n + 1))
                wait(pe, vl_done, n + 1)
                last_z = min(n + 4, STEPS - 1) if isinstance(n, int) else n + 4
                for half in range(2):
                    wait(pe, zl_done, 2 * last_z + half + 1)
                    wait(pe, yl_done, 2 * (n - 1) + half + 1)
                    if g == 0:
                        wait(pe, r_done, TC * (b - 1) + half + 1)
                    terms = ((v_hi, pt0_hi, pt1_hi), (v_hi, pt0_lo, pt1_lo), (v_lo, pt0_hi, pt1_hi))
                    for i, (v, pt0, pt1) in enumerate(terms):
                        pe.matmul(ps_y[:, half, 0:2 * T], v[:, g % 2, 0, :], pt0[:, g % 2, 2 * half:2 * half + 2, :],
                                  start=(i == 0), stop=False, skip_group_check=True)
                        later = ps_y[:, half, 0:2 * T].rearrange("p (h t) -> p h t", h=2)[:, :, R:T]
                        mm = pe.matmul(later, v[:, g % 2, 1, :], pt1[:, g % 2, 2 * half:2 * half + 2, :],
                                       start=False, stop=(i == 2), skip_group_check=True)
                    mm.then_inc(pv_done, 1)

            def wu(b):
                if not within(b, B):
                    return
                wait(pe, yl_done, 2 * NG * (b + 1))
                last_z = min(NG * b + 8, STEPS - 1) if isinstance(b, int) else NG * b + 8
                for c in range(TC):
                    wait(pe, zl_done, 2 * last_z + c + 1)
                    for bu in (bu_hi, bu_lo):
                        pe.matmul(ps_y[0:R, c, :], identity_r[:], bu[:], start=(bu is bu_hi), stop=False)
                    i = 0
                    for y, w in ((yt_hi, w_hi), (yt_hi, w_lo), (yt_lo, w_hi)):
                        for k in range(KC):
                            mm = pe.matmul(ps_y[0:R, c, :], y[:, k, c * R:c * R + R], w[:, k, :],
                                           start=False, stop=(i == 3 * KC - 1))
                            i += 1
                    mm.then_inc(wu_done, 1)

            pe.wait_ge(prep_dve, 2 + KC)
            z(0, 0)
            z(1, 1)

            def steps(b):
                for g in range(NG):
                    n = NG * b + g
                    s(n, g)
                    if g == 3:
                        wu(b - 1)
                    pv(n - 3, (g - 3) % NG, b if g == 3 else b - 1)
                    t(n - 1, (g - 1) % NG)
                    z(n + 2, (g + 2) % NG)

            steps(0)
            steps(1)
            with pe.Fori(2, B - 1) as b:
                steps(b)
            steps(B - 1)
            steps(B)

        @block.scalar
        def _(act):
            act.wait_ge(prep_mm, 1)
            act.activation(a_f[:], ps_y[0:3 * C, 0, 0:3 * C], ACT.Copy, scale=float(D) ** -0.5).then_inc(prep_act, 1)
            act.wait_ge(prep_act, 1)
            act.activation(a_stack[:], a_f[:], ACT.Copy).then_inc(prep_act, 1)
            for k in range(KC):
                act.wait_ge(prep_mm, 2 + k)
                act.activation(w_hi[:, k, :], ps_s[:, k % 2, :], ACT.Copy).then_inc(prep_act, 1)
            act.wait_ge(const_ready, 5)
            act.activation(identity_r[:], identity[0:R, 0:R], ACT.Copy).then_inc(prep_act, 1)
            act.wait_ge(bu_in, 16)
            act.activation(bu_hi[:], bu_all[:], ACT.Copy).then_inc(prep_act, 1)

            def exp(n, g, banks):
                if not within(n, STEPS):
                    return
                wait(act, t_done, 3 * (n - 1))
                for bank in banks:
                    wait(act, max_done, 3 * n + bank + 1)
                    c = 0 if bank == 0 else 1
                    for h in range(G) if bank == 0 else (2 * bank - 2, 2 * bank - 1):
                        src = ps_s[0:R, 0, h * R:h * R + R] if c == 0 else ps_s[0:R, bank, (h % 2) * T:(h % 2) * T + T]
                        e = act.activation((p1 if c else p0)[:, g % 2, h, :], src, ACT.Exp, bias=nmax[:, g % 2, c, h:h + 1],
                                           accum_out=rsum[:, g % 2, c, h:h + 1])
                    e.then_inc(exp_done, 1)

            def pth(n, g):
                if not within(n, STEPS):
                    return
                wait(act, pv_done, 2 * (n - 1))
                for half in range(2):
                    wait(act, t_done, 3 * n + half + 1)
                    act.activation(pt0_hi[:, g % 2, 2 * half:2 * half + 2, :], ps_t[0:R, half, 0:2 * T], ACT.Copy).then_inc(pth_done, 1)
                wait(act, t_done, 3 * (n + 1))
                act.activation(pt1_hi[:, g % 2, :, :], ps_t[0:R, 2, 0:G * R], ACT.Copy).then_inc(pth_done, 1)

            def yh(n, g, b):
                if not within(n, STEPS):
                    return
                if g == 0:
                    wait(act, wu_done, TC * b)
                for half in range(2):
                    wait(act, pv_done, 2 * n + half + 1)
                    for h in (2 * half, 2 * half + 1):
                        y = act.activation(yt_hi[C * h:C * h + C, g, :], ps_y[C * h:C * h + C, half, (h % 2) * T:(h % 2) * T + T], ACT.Copy)
                    y.then_inc(yh_done, 1)

            def zh(n, g):
                if not within(n, STEPS):
                    return
                wait(act, s_done, 3 * (n - 1))
                for half in range(2):
                    wait(act, z_done, 2 * n + half + 1)
                    act.activation(zs[:, g % 2, 2 * half:2 * half + 2, :], ps_y[0:3 * C, half, 0:2 * T], ACT.Copy).then_inc(zh_done, 1)

            zh(0, 0)
            zh(1, 1)

            def steps(b):
                for g in range(NG):
                    n = NG * b + g
                    pth(n - 2, (g - 2) % NG)
                    exp(n, g, (0, 1))
                    if g == 3:
                        exp(n, g, (2,))
                    yh(n - 3, (g - 3) % NG, b)
                    if g != 3:
                        exp(n, g, (2,))
                    zh(n + 2, (g + 2) % NG)

            steps(0)
            steps(1)
            with act.Fori(2, B - 1) as b:
                steps(b)
            steps(B - 1)
            steps(B)

        @block.vector
        def _(dve):
            dve.wait_ge(prep_act, 2)
            dve.tensor_tensor(a_stack[2 * C:3 * C, :], a_f[2 * C:3 * C, :], a_stack[2 * C:3 * C, :], ALU.subtract).then_inc(prep_dve, 1)
            for k in range(KC):
                dve.wait_ge(prep_act, 3 + k)
                dve.tensor_tensor(w_lo[:, k, :], ps_s[:, k % 2, :], w_hi[:, k, :], ALU.subtract).then_inc(prep_dve, 1)
            dve.wait_ge(prep_act, 4 + KC)
            dve.tensor_tensor(bu_lo[:], bu_all[:], bu_hi[:], ALU.subtract).then_inc(prep_dve, 1)

            def xh(n, g, b):
                if not within(n, STEPS):
                    return
                wait(dve, xs_in[g], 48 * (b + 1))
                wait(dve, s_done, 3 * (n - 3))
                dve.tensor_copy(xs[:, g, :, :], xs_raw[:, g, :, :]).then_inc(xh_done, 1)

            def vh(n, g, b):
                if not within(n, STEPS):
                    return
                wait(dve, v_in[g], 16 * (b + 1))
                wait(dve, pv_done, 2 * (n - 1))
                dve.tensor_copy(v_hi[:, g % 2, :, :], v_raw[:, g, :, :]).then_inc(vh_done, 1)

            def smax(n, g, banks):
                if not within(n, STEPS):
                    return
                for bank in banks:
                    wait(dve, s_done, 3 * n + bank + 1)
                    if bank == 0:
                        dve.tensor_reduce(nmax[:, g % 2, 0, :], ps_s[0:R, 0, 0:G * R].rearrange("p (h t) -> p h t", h=G),
                                          AX.X, ALU.max, negate=True).then_inc(max_done, 1)
                        continue
                    dve.tensor_reduce(nmax[:, g % 2, 1, 2 * bank - 2:2 * bank], ps_s[0:R, bank, 0:2 * T].rearrange("p (h t) -> p h t", h=2),
                                      AX.X, ALU.max, negate=True).then_inc(max_done, 1)

            def inverse(n, g):
                if not within(n, STEPS):
                    return
                wait(dve, exp_done, 3 * (n + 1))
                wait(dve, norm_done, 2 * (n - 1))
                dve.reciprocal(rinv[:, g % 2, :, :], rsum[:, g % 2, :, :]).then_inc(rinv_done, 1)

            def ptl(n, g, banks):
                if not within(n, STEPS):
                    return
                for bank in banks:
                    wait(dve, pth_done, 3 * n + bank + 1)
                    if bank < 2:
                        hi, lo = (pt[:, g % 2, 2 * bank:2 * bank + 2, :] for pt in (pt0_hi, pt0_lo))
                        src = ps_t[0:R, bank, 0:2 * T]
                    else:
                        hi, lo = (pt[:, g % 2, :, :] for pt in (pt1_hi, pt1_lo))
                        src = ps_t[0:R, 2, 0:G * R]
                    dve.tensor_tensor(lo, src, hi, ALU.subtract).then_inc(ptl_done, 1)

            def yl(n, g, half):
                if not within(n, STEPS):
                    return
                wait(dve, yh_done, 2 * n + half + 1)
                for h in (2 * half, 2 * half + 1):
                    y = dve.tensor_tensor(yt_lo[C * h:C * h + C, g, :], ps_y[C * h:C * h + C, half, (h % 2) * T:(h % 2) * T + T],
                                          yt_hi[C * h:C * h + C, g, :], ALU.subtract)
                y.then_inc(yl_done, 1)

            def zl(n, g):
                if not within(n, STEPS):
                    return
                for half in range(2):
                    wait(dve, zh_done, 2 * n + half + 1)
                    low = zs[2 * C:3 * C, g % 2, 2 * half:2 * half + 2, :]
                    dve.tensor_tensor(low, ps_y[2 * C:3 * C, half, 0:2 * T], low, ALU.subtract).then_inc(zl_done, 1)

            def residual(b):
                if not within(b, B):
                    return
                wait(dve, res_in, 16 * (b + 1))
                for c in range(TC):
                    wait(dve, wu_done, TC * b + c + 1)
                    dve.tensor_tensor(r[:, c, :], ps_y[0:R, c, :], xres[:, c, :], ALU.add).then_inc(r_done, 1)

            def statistics(b):
                if not within(b, B):
                    return
                for c in range(TC):
                    wait(dve, r_done, TC * b + c + 1)
                    dve.bn_stats(stats[:, c, :], r[:, c, :]).then_inc(stats_done, 1)
                for c in range(TC):
                    dve.wait_ge(prep_act, 1)
                    wait(dve, stats_done, TC * b + c + 1)
                    dve.bn_aggr(mv[:, c, :], stats[:, c, :]).then_inc(mv_done, 1)
                wait(dve, mv_done, TC * (b + 1))
                dve.tensor_scalar(veps[:, :, 0], mv[:, :, 1], EPS, None, ALU.add).then_inc(veps_done, 1)

            def norm(b):
                if not within(b, B):
                    return
                wait(dve, rstd_done, b + 1)
                wait(dve, stored, 16 * b)
                for c in range(TC):
                    dve.tensor_scalar(xn[:, c, :], r[:, c, :], mv[:, c, 0:1], rstd[:, c, :], ALU.subtract, ALU.mult)\
                       .then_inc(xn_done, 1)

            xh(0, 0, 0)
            xh(1, 1, 0)
            xh(2, 2, 0)
            zl(0, 0)
            zl(1, 1)

            def steps(b):
                for g in range(NG):
                    n = NG * b + g
                    inverse(n - 1, (g - 1) % NG)
                    smax(n, g, (0,))
                    ptl(n - 2, (g - 2) % NG, (0,))
                    smax(n, g, (1, 2))
                    ptl(n - 2, (g - 2) % NG, (1, 2))
                    xh(n + 3, (g + 3) % NG, b + (g + 3) // NG)
                    if g == 3:
                        residual(b - 1)
                    yl(n - 3, (g - 3) % NG, 0)
                    yl(n - 3, (g - 3) % NG, 1)
                    vh(n - 1, (g - 1) % NG, b if g else b - 1)
                    zl(n + 2, (g + 2) % NG)
                    if g == 3:
                        statistics(b - 1)
                    if g == 0:
                        norm(b - 2)

            for b in range(3):
                steps(b)
            with dve.Fori(3, B - 1) as b:
                steps(b)
            steps(B - 1)
            steps(B)
            norm(B - 1)

        @block.gpsimd
        def _(pool):
            pool.memset(wv_diag[:], 0.0).then_inc(const_ready, 1)
            pool.memset(identity[:], 1.0).then_inc(const_ready, 1)
            pool.memset(mask[:], 0.0).then_inc(const_ready, 1)
            pool.memset(mhalf[:], -0.5).then_inc(const_ready, 1)
            pool.wait_ge(const_ready, 4)
            pool.affine_select(out=identity[:], in_=identity[:], compare_op=ALU.is_equal, fill=0.0, base=0,
                               pattern=[[-1, 128]], channel_multiplier=1).then_inc(prep_id, 1)
            pool.affine_select(out=mask[:], in_=mask[:], compare_op=ALU.is_ge, fill=NEG, base=0,
                               pattern=[[0, G], [-1, R]], channel_multiplier=1).then_inc(prep_id, 1)
            pool.wait_ge(prep_id, 2)
            pool.tensor_copy(identity_b[:], identity[0:R, 0:R]).then_inc(const_ready, 1)

            def xl(n, g):
                if not within(n, STEPS):
                    return
                wait(pool, xh_done, n + 1)
                wait(pool, norm_done, 2 * (n - 3))
                wait(pool, vl_done, n - 5)
                low = xs[C:2 * C, g, :, :]
                pool.tensor_tensor(low, xs_raw[C:2 * C, g, :, :], low, ALU.subtract).then_inc(xl_done, 1)

            def vl(n, g):
                if not within(n, STEPS):
                    return
                wait(pool, vh_done, n + 1)
                wait(pool, xl_done, min(n + 6, STEPS) if isinstance(n, int) else n + 6)
                wait(pool, pv_done, 2 * (n - 1))
                pool.tensor_tensor(v_lo[:, g % 2, :, :], v_raw[:, g, :, :], v_hi[:, g % 2, :, :], ALU.subtract)\
                    .then_inc(vl_done, 1)

            def normalise(n, g):
                if not within(n, STEPS):
                    return
                wait(pool, rinv_done, n + 1)
                wait(pool, xl_done, min(n + 4, STEPS) if isinstance(n, int) else n + 4)
                for c, p, w in ((0, p0, R), (1, p1, T)):
                    inv = rinv[:, g % 2, c, :].rearrange("p (h a) -> p h a", a=1).to_broadcast((R, G, w))
                    pool.tensor_tensor(p[:, g % 2, :, :], p[:, g % 2, :, :], inv, ALU.mult).then_inc(norm_done, 1)

            def power(b):
                if not within(b, B):
                    return
                wait(pool, veps_done, b + 1)
                wait(pool, xn_done, TC * b)
                pool.tensor_tensor(rstd[:], veps[:], mhalf[:], ALU.pow).then_inc(rstd_done, 1)
                wait(pool, rstd_done, b + 1)

            xl(0, 0)
            xl(1, 1)
            xl(2, 2)

            def steps(b):
                for g in range(NG):
                    n = NG * b + g
                    normalise(n - 1, (g - 1) % NG)
                    if g == 0:
                        power(b - 2)
                    xl(n + 3, (g + 3) % NG)
                    vl(n - 2, (g - 2) % NG)

            for b in range(3):
                steps(b)
            with pool.Fori(3, B - 1) as b:
                steps(b)
            steps(B - 1)
            steps(B)
            power(B - 1)


def cross_attention(nc, io, x1, x2, raw, raw_in):
    with ExitStack() as ctx:
        def sb(name, shape, dt=F32):
            return ctx.enter_context(nc.sbuf_tensor("x_" + name, shape, dt))

        def sem(name):
            return ctx.enter_context(nc.semaphore("x_" + name))

        identity = sb("identity", [128, 128])
        m_hi = sb("m_hi", [128, KC, D], F32R)
        m_lo = sb("m_lo", [128, KC, D], F32R)
        wv_hi = sb("wv_hi", [128, KC, D], F32R)
        wv_lo = sb("wv_lo", [128, KC, D], F32R)
        zbias = sb("zbias", [128, KC])
        kbias = sb("kbias", [R, D])
        qk_bias = sb("qk_bias", [R, 1])
        bv_all = sb("bv_all", [R, D])
        mhalf = sb("mhalf", [R, TC, 1])

        wq, wk, wv = raw
        bq = sb("bq", [128, KC, 1])
        bk = sb("bk", [128, KC, 1])
        bk_all = sb("bk_all", [128, KC, R])
        ones = sb("ones", [128, R])

        x1_raw = sb("x1_raw", [R, TC, D])
        x1b = sb("x1b", [R, 2, TC, D])
        x1t_hi = sb("x1t_hi", [128, KC, T], F32R)
        x1t_lo = sb("x1t_lo", [128, KC, T], F32R)
        zt_hi = sb("zt_hi", [128, KC, T], F32R)
        zt_lo = sb("zt_lo", [128, KC, T], F32R)
        ct_raw = sb("ct_raw", [128, KC, TX])
        ct_hi = sb("ct_hi", [128, KC, TX + 2], F32R)
        ct_lo = sb("ct_lo", [128, KC, TX + 2], F32R)
        cx_raw = sb("cx_raw", [XR, XC, D])
        cx_hi = sb("cx_hi", [XR, XC, D], F32R)
        cx_lo = sb("cx_lo", [XR, XC, D], F32R)
        dot = sb("dot", [R, D])
        rowdot = sb("rowdot", [R, TC])
        rowbias = sb("rowbias", [R, TC])
        smax = sb("smax", [R, TC])
        biased_max = sb("biased_max", [R, TC])
        shift = sb("shift", [R, TC])
        rsum = sb("rsum", [R, TC])
        rinv = sb("rinv", [R, TC])
        p = sb("p", [R, TC, TX])
        pt_hi = sb("pt_hi", [XR, XC, T], F32R)
        pt_lo = sb("pt_lo", [XR, XC, T], F32R)
        ot_hi = sb("ot_hi", [128, KC, T], F32R)
        ot_lo = sb("ot_lo", [128, KC, T], F32R)
        r = sb("r", [R, TC, D])
        stats = sb("stats", [R, TC, 6])
        mv = sb("mv", [R, TC, 2])
        veps = sb("veps", [R, TC, 1])
        rstd = sb("rstd", [R, TC, 1])
        xn = sb("xn", [R, TC, D])

        ps_s = ctx.enter_context(nc.psum_tensor("x_ps_s", [128, 4, 512], F32))
        ps_g = ctx.enter_context(nc.psum_tensor("x_ps_g", [128, 2, 512], F32))
        ps_h = ctx.enter_context(nc.psum_tensor("x_ps_h", [128, 2, 512], F32))

        bias_in = sem("bias_in")
        made = sem("made")
        spread = sem("spread")
        prep_mm = sem("prep_mm")
        prep_hi = sem("prep_hi")
        prep_lo = sem("prep_lo")
        PREPARED = 2 * KC + 1
        pad_done = sem("pad_done")
        x1_in = sem("x1_in")
        ct_in = sem("ct_in")
        cx_in = sem("cx_in")
        x1b_done = sem("x1b_done")
        x1t_done = sem("x1t_done")
        x1th_done = sem("x1th_done")
        x1tl_done = sem("x1tl_done")
        cth_done = sem("cth_done")
        ctl_done = sem("ctl_done")
        cxh_done = sem("cxh_done")
        cxl_done = sem("cxl_done")
        zt_done = sem("zt_done")
        zth_done = sem("zth_done")
        ztl_done = sem("ztl_done")
        s_done = sem("s_done")
        dot_done = sem("dot_done")
        rowbias_done = sem("rowbias_done")
        max_done = sem("max_done")
        biased_done = sem("biased_done")
        shift_done = sem("shift_done")
        exp_done = sem("exp_done")
        rinv_done = sem("rinv_done")
        pt_done = sem("pt_done")
        pth_done = sem("pth_done")
        ptl_done = sem("ptl_done")
        ot_done = sem("ot_done")
        oth_done = sem("oth_done")
        otl_done = sem("otl_done")
        out_done = sem("out_done")
        r_done = sem("r_done")
        stats_done = sem("stats_done")
        mv_done = sem("mv_done")
        veps_done = sem("veps_done")
        rstd_done = sem("rstd_done")
        xn_done = sem("xn_done")
        stored = sem("stored")

        block = ctx.enter_context(nc.Block())

        def pair(bank, k):
            return bank[:, k // 2, (k % 2) * T:(k % 2) * T + T]

        @block.sync
        def _(sp):
            def loads(b):
                wait(sp, x1b_done, b)
                wait(sp, x1t_done, b)
                wait(sp, rowbias_done, b)
                sp.dma_start(x1_raw[:], x1[b].rearrange("(c p) d -> p c d", p=R)).then_inc(x1_in, 16)
                wait(sp, ctl_done, KC * b)
                sp.dma_start(ct_raw[:], io["ct"][b].rearrange("(k p) t -> p k t", p=128)).then_inc(ct_in, 16)
                if within(b - 3, B):
                    store(b - 3)
                wait(sp, cxl_done, XC * b)
                sp.dma_start(cx_raw[:], io["cx"][b].rearrange("(c p) d -> p c d", p=XR)).then_inc(cx_in, 16)

            def store(b):
                sp.wait_ge(xn_done, TC * (b + 1))
                sp.dma_start(x2[b].rearrange("(c p) d -> p c d", p=R), xn[:]).then_inc(stored, 16)

            sp.dma_start(bv_all[:], io["xbv"].rearrange("(a d) -> a d", a=1).to_broadcast((R, D))).then_inc(bias_in, 16)
            with nc.allow_non_contiguous_dma(reason="biases by partition"):
                sp.dma_start(bq[:], io["xbq"].rearrange("(k p a) -> p k a", p=128, a=1)).then_inc(bias_in, 16)
                sp.dma_start(bk[:], io["xbk"].rearrange("(k p a) -> p k a", p=128, a=1)).then_inc(bias_in, 16)
            for b in range(3):
                loads(b)
            sp.wait_ge(prep_lo, PREPARED)
            for i, name in enumerate(("wf_t", "wi_t", "wc_t")):
                load_weight(sp, raw[i], raw_in[i], io[name])
            with sp.Fori(3, B) as b:
                loads(b)
            for b in range(B - 3, B):
                store(b)
            sp.wait_ge(stored, 16 * B)

        @block.tensor
        def _(pe):
            pe.wait_ge(raw_in[0], 16)
            pe.wait_ge(raw_in[1], 16)
            for dk in range(KC):
                for k in range(KC):
                    mm = pe.matmul(ps_s[:, dk, :], wq[:, k, 128 * dk:128 * dk + 128], wk[:, k, :], start=(k == 0), stop=(k == KC - 1))
                mm.then_inc(prep_mm, 1)
            pe.wait_ge(bias_in, 48)
            pe.wait_ge(spread, KC)
            for k in range(KC):
                pe.matmul(ps_g[0:R, 1, :], bk_all[:, k, :], wq[:, k, :], start=(k == 0), stop=(k == KC - 1))
            for ck in range(KC):
                for k in range(KC):
                    pe.matmul(ps_g[:, 0, ck:ck + 1], wk[:, k, 128 * ck:128 * ck + 128], bq[:, k, :], start=(k == 0), stop=(k == KC - 1))
            for k in range(KC):
                mm = pe.matmul(ps_h[0:R, 0, 0:1], bk_all[:, k, :], bq[:, k, :], start=(k == 0), stop=(k == KC - 1))
            mm.then_inc(prep_mm, 1)
            pe.wait_ge(made, 4)
            pe.wait_ge(pad_done, 2)
            pe.wait_ge(prep_lo, PREPARED)

            def x1_turn(b):
                wait(pe, x1_in, 16 * (b + 1))
                wait(pe, otl_done, b - 1)
                for k in range(KC):
                    for c in range(TC):
                        mm = pe.transpose(ps_g[:, k // 2, (k % 2) * T + c * R:(k % 2) * T + c * R + R],
                                          x1_raw[:, c, 128 * k:128 * k + 128], identity[0:R, 0:R])
                mm.then_inc(x1t_done, 1)

            def p_turn(b):
                wait(pe, exp_done, TC * (b + 1))
                for j in range(XC):
                    for c in range(TC):
                        mm = pe.transpose(ps_s[0:XR, j // 2, (j % 2) * T + c * R:(j % 2) * T + c * R + R],
                                          p[:, c, XR * j:XR * j + XR], identity[0:R, 0:R])
                mm.then_inc(pt_done, 1)

            def zt(b):
                wait(pe, x1tl_done, b + 1)
                wait(pe, r_done, TC * (b - 1))
                for ck in range(KC):
                    i = 0
                    for m, x in ((m_hi, x1t_hi), (m_lo, x1t_hi), (m_hi, x1t_lo)):
                        for k in range(KC):
                            mm = pe.matmul(pair(ps_h, ck), m[:, k, 128 * ck:128 * ck + 128], x[:, k, :],
                                           start=(i == 0), stop=(i == 3 * KC - 1))
                            i += 1
                mm.then_inc(zt_done, 1)

            def ot(b):
                wait(pe, ptl_done, b + 1)
                wait(pe, cxl_done, XC * (b + 1))
                wait(pe, x1tl_done, min(b + 2, B) if isinstance(b, int) else b + 2)
                for dk in range(KC):
                    i = 0
                    for v, q in ((cx_hi, pt_hi), (cx_lo, pt_hi), (cx_hi, pt_lo)):
                        for j in range(XC):
                            mm = pe.matmul(pair(ps_g, dk), v[:, j, 128 * dk:128 * dk + 128], q[:, j, :],
                                           start=(i == 0), stop=(i == 3 * XC - 1))
                            i += 1
                mm.then_inc(ot_done, 1)

            def s(b):
                wait(pe, ztl_done, b + 1)
                wait(pe, ctl_done, KC * (b + 1))
                wait(pe, ptl_done, b)
                for c in range(TC):
                    i = 0
                    for z, x in ((zt_hi, ct_hi), (zt_hi, ct_lo), (zt_lo, ct_hi)):
                        for k in range(KC):
                            for half in range(2):
                                mm = pe.matmul(ps_s[0:R, 2 * c + half, 0:XH + 1], z[:, k, c * R:c * R + R],
                                               x[:, k, half * XH:half * XH + XH + 1], start=(i == 0), stop=(i == 3 * KC - 1))
                            i += 1
                    mm.then_inc(s_done, 1)

            def out(b):
                wait(pe, otl_done, b + 1)
                wait(pe, ztl_done, min(b + 2, B) if isinstance(b, int) else b + 2)
                for c in range(TC):
                    i = 0
                    for y, w in ((ot_hi, wv_hi), (ot_hi, wv_lo), (ot_lo, wv_hi)):
                        for k in range(KC):
                            mm = pe.matmul(ps_h[0:R, c, :], y[:, k, c * R:c * R + R], w[:, k, :],
                                           start=(i == 0), stop=(i == 3 * KC - 1))
                            i += 1
                    mm.then_inc(out_done, 1)

            def step(b):
                if within(b - 1, B):
                    p_turn(b - 1)
                if within(b, B):
                    zt(b)
                if within(b - 1, B):
                    ot(b - 1)
                if within(b, B):
                    s(b)
                if within(b + 1, B):
                    x1_turn(b + 1)
                if within(b - 1, B):
                    out(b - 1)

            x1_turn(0)
            for b in range(2):
                step(b)
            with pe.Fori(2, B - 1) as b:
                step(b)
            step(B - 1)
            step(B)

        @block.scalar
        def _(act):
            act.wait_ge(raw_in[2], 16)
            for dk in range(KC):
                act.activation(wv_hi[:, dk, :], wv[:, dk, :], ACT.Copy).then_inc(prep_hi, 1)
                act.wait_ge(prep_mm, dk + 1)
                act.activation(m_hi[:, dk, :], ps_s[:, dk, :], ACT.Copy).then_inc(prep_hi, 1)

            def x1th(b):
                wait(act, x1t_done, b + 1)
                wait(act, zt_done, b)
                act.activation(x1t_hi[:, 0:2, :], ps_g[:, 0, 0:2 * T], ACT.Copy)
                act.activation(x1t_hi[:, 2:4, :], ps_g[:, 1, 0:2 * T], ACT.Copy).then_inc(x1th_done, 1)

            def cth(b):
                wait(act, ct_in, 16 * (b + 1))
                wait(act, s_done, TC * b)
                for k in range(KC):
                    act.activation(ct_hi[:, k, 0:TX], ct_raw[:, k, :], ACT.Copy).then_inc(cth_done, 1)

            def pth(b):
                wait(act, pt_done, b + 1)
                wait(act, ot_done, b)
                for j in range(XC // 2):
                    a = act.activation(pt_hi[:, 2 * j:2 * j + 2, :], ps_s[0:XR, j, 0:2 * T], ACT.Copy)
                a.then_inc(pth_done, 1)

            def zth(b):
                wait(act, zt_done, b + 1)
                wait(act, s_done, TC * b)
                for k in range(KC):
                    a = act.activation(zt_hi[:, k, :], pair(ps_h, k), ACT.Identity, bias=zbias[:, k:k + 1])
                a.then_inc(zth_done, 1)

            def oth(b):
                wait(act, ot_done, b + 1)
                wait(act, out_done, TC * b)
                act.activation(ot_hi[:, 0:2, :], ps_g[:, 0, 0:2 * T], ACT.Copy)
                act.activation(ot_hi[:, 2:4, :], ps_g[:, 1, 0:2 * T], ACT.Copy).then_inc(oth_done, 1)

            def cxh(b):
                wait(act, cx_in, 16 * (b + 1))
                wait(act, ot_done, b)
                for j in range(XC):
                    act.activation(cx_hi[:, j, :], cx_raw[:, j, :], ACT.Copy).then_inc(cxh_done, 1)

            def exp(b):
                wait(act, pt_done, b)
                wait(act, rinv_done, b)
                for c in range(TC):
                    wait(act, shift_done, TC * b + c + 1)
                    act.activation(p[:, c, :].rearrange("p (a t) -> p a t", a=2), ps_s[0:R, 2 * c:2 * c + 2, 0:XH],
                                   ACT.Exp, bias=shift[:, c:c + 1], accum_out=rsum[:, c:c + 1]).then_inc(exp_done, 1)

            def step(b):
                if within(b - 1, B):
                    pth(b - 1)
                if within(b, B):
                    if not (isinstance(b, int) and b == 0):
                        cth(b)
                    zth(b)
                if within(b - 1, B):
                    oth(b - 1)
                if within(b, B):
                    cxh(b)
                    exp(b)
                if within(b + 1, B):
                    x1th(b + 1)

            cth(0)
            x1th(0)
            for b in range(2):
                step(b)
            with act.Fori(2, B - 1) as b:
                step(b)
            step(B - 1)
            step(B)

        @block.vector
        def _(dve):
            dve.wait_ge(made, 3)
            dve.wait_ge(bias_in, 48)
            for k in range(KC):
                dve.tensor_scalar(bk_all[:, k, :], ones[:], bk[:, k, :], None, ALU.mult).then_inc(spread, 1)
            for dk in range(KC):
                dve.wait_ge(prep_hi, 2 * dk + 1)
                dve.tensor_tensor(wv_lo[:, dk, :], wv[:, dk, :], wv_hi[:, dk, :], ALU.subtract).then_inc(prep_lo, 1)
                dve.wait_ge(prep_hi, 2 * dk + 2)
                dve.tensor_tensor(m_lo[:, dk, :], ps_s[:, dk, :], m_hi[:, dk, :], ALU.subtract).then_inc(prep_lo, 1)
            dve.wait_ge(prep_mm, KC + 1)
            dve.tensor_copy(zbias[:], ps_g[:, 0, 0:KC])
            dve.tensor_copy(kbias[:], ps_g[0:R, 1, :])
            dve.tensor_copy(qk_bias[:], ps_h[0:R, 0, 0:1]).then_inc(prep_lo, 1)
            dve.wait_ge(prep_lo, PREPARED)

            def x1tl(b):
                wait(dve, x1th_done, b + 1)
                dve.tensor_tensor(x1t_lo[:, 0:2, :], ps_g[:, 0, 0:2 * T], x1t_hi[:, 0:2, :], ALU.subtract)
                dve.tensor_tensor(x1t_lo[:, 2:4, :], ps_g[:, 1, 0:2 * T], x1t_hi[:, 2:4, :], ALU.subtract).then_inc(x1tl_done, 1)

            def row_bias(b):
                for c in range(TC):
                    wait(dve, dot_done, TC * b + c)
                    dve.tensor_tensor_reduce(out=dot[:], in0=x1_raw[:, c, :], in1=kbias[:], scale=1.0, scalar=0.0,
                                             op0=ALU.mult, op1=ALU.add, accum_out=rowdot[:, c:c + 1]).then_inc(dot_done, 1)
                wait(dve, dot_done, TC * (b + 1))
                wait(dve, shift_done, TC * b)
                dve.tensor_scalar(rowbias[:], rowdot[:], qk_bias[:, 0:1], None, ALU.add).then_inc(rowbias_done, 1)

            def ptl(b):
                wait(dve, pth_done, b + 1)
                for j in range(XC // 2):
                    q = dve.tensor_tensor(pt_lo[:, 2 * j:2 * j + 2, :], ps_s[0:XR, j, 0:2 * T], pt_hi[:, 2 * j:2 * j + 2, :],
                                          ALU.subtract)
                q.then_inc(ptl_done, 1)

            def ztl(b):
                wait(dve, zth_done, b + 1)
                for k in range(KC):
                    q = dve.scalar_tensor_tensor(out=zt_lo[:, k, :], in0=pair(ps_h, k), scalar=zbias[:, k:k + 1],
                                                 in1=zt_hi[:, k, :], op0=ALU.add, op1=ALU.subtract)
                q.then_inc(ztl_done, 1)

            def otl(b):
                wait(dve, oth_done, b + 1)
                dve.tensor_tensor(ot_lo[:, 0:2, :], ps_g[:, 0, 0:2 * T], ot_hi[:, 0:2, :], ALU.subtract)
                dve.tensor_tensor(ot_lo[:, 2:4, :], ps_g[:, 1, 0:2 * T], ot_hi[:, 2:4, :], ALU.subtract).then_inc(otl_done, 1)

            def row_max(b):
                wait(dve, rowbias_done, b + 1)
                for c in range(TC):
                    wait(dve, s_done, TC * b + c + 1)
                    dve.tensor_reduce(smax[:, c:c + 1], ps_s[0:R, 2 * c:2 * c + 2, 0:XH], AX.XY, ALU.max).then_inc(max_done, 1)
                    wait(dve, max_done, TC * b + c + 1)
                    dve.tensor_tensor(biased_max[:, c:c + 1], smax[:, c:c + 1], rowbias[:, c:c + 1], ALU.add).then_inc(biased_done, 1)
                    wait(dve, biased_done, TC * b + c + 1)
                    wait(dve, exp_done, TC * (b - 1) + c + 1)
                    dve.tensor_tensor(shift[:, c:c + 1], rowbias[:, c:c + 1], biased_max[:, c:c + 1], ALU.subtract)\
                       .then_inc(shift_done, 1)

            def residual(b, odd):
                wait(dve, x1b_done, b + 1)
                for c in range(TC):
                    wait(dve, out_done, TC * b + c + 1)
                    dve.scalar_tensor_tensor(out=r[:, c, :], in0=ps_h[0:R, c, :], scalar=rinv[:, c:c + 1], in1=x1b[:, odd, c, :],
                                             op0=ALU.mult, op1=ALU.add).then_inc(r_done, 1)

            def statistics(b):
                for c in range(TC):
                    wait(dve, r_done, TC * b + c + 1)
                    dve.bn_stats(stats[:, c, :], r[:, c, :]).then_inc(stats_done, 1)
                for c in range(TC):
                    dve.wait_ge(pad_done, 1)
                    wait(dve, stats_done, TC * b + c + 1)
                    dve.bn_aggr(mv[:, c, :], stats[:, c, :]).then_inc(mv_done, 1)
                wait(dve, mv_done, TC * (b + 1))
                dve.tensor_scalar(veps[:, :, 0], mv[:, :, 1], EPS, None, ALU.add).then_inc(veps_done, 1)

            def inverse(b):
                wait(dve, exp_done, TC * (b + 1))
                wait(dve, r_done, TC * b)
                dve.reciprocal(rinv[:], rsum[:]).then_inc(rinv_done, 1)

            def norm(b):
                wait(dve, rstd_done, b + 1)
                wait(dve, stored, 16 * b)
                for c in range(TC):
                    dve.tensor_scalar(xn[:, c, :], r[:, c, :], mv[:, c, 0:1], rstd[:, c, :], ALU.subtract, ALU.mult)\
                       .then_inc(xn_done, 1)

            def step(b, odd):
                if within(b - 1, B):
                    ptl(b - 1)
                if within(b, B):
                    row_bias(b)
                if within(b - 2, B):
                    statistics(b - 2)
                if within(b, B):
                    ztl(b)
                if within(b - 2, B):
                    norm(b - 2)
                if within(b - 1, B):
                    otl(b - 1)
                if within(b, B):
                    row_max(b)
                if within(b + 1, B):
                    x1tl(b + 1)
                if within(b - 1, B):
                    residual(b - 1, 1 - odd)
                if within(b, B):
                    inverse(b)

            x1tl(0)
            for b in range(4):
                step(b, b % 2)
            with dve.Fori(2, B // 2 - 1) as i:
                for odd in range(2):
                    step(2 * i + odd, odd)
            for b in range(B - 2, B + 2):
                step(b, b % 2)

        @block.gpsimd
        def _(pool):
            pool.memset(identity[:], 1.0).then_inc(made, 1)
            pool.memset(mhalf[:], -0.5).then_inc(made, 1)
            pool.memset(ones[:], 1.0).then_inc(made, 1)
            pool.wait_ge(made, 3)
            pool.affine_select(out=identity[:], in_=identity[:], compare_op=ALU.is_equal, fill=0.0, base=0,
                               pattern=[[-1, 128]], channel_multiplier=1).then_inc(made, 1)
            pool.wait_ge(bias_in, 48)
            pool.memset(ct_hi[:, :, TX:TX + 2].bitcast(F32), 0.0).then_inc(pad_done, 1)
            pool.memset(ct_lo[:, :, TX:TX + 2].bitcast(F32), 0.0).then_inc(pad_done, 1)

            def residual_bias(b, odd):
                wait(pool, x1_in, 16 * (b + 1))
                wait(pool, r_done, TC * (b - 1))
                pool.tensor_tensor(x1b[:, odd, :, :], x1_raw[:], bv_all[:, :].rearrange("p (a d) -> p a d", a=1).to_broadcast((R, TC, D)),
                                   ALU.add).then_inc(x1b_done, 1)

            def ctl(b):
                for k in range(KC):
                    wait(pool, cth_done, KC * b + k + 1)
                    pool.tensor_tensor(ct_lo[:, k, 0:TX], ct_raw[:, k, :], ct_hi[:, k, 0:TX], ALU.subtract).then_inc(ctl_done, 1)

            def cxl(b):
                for j in range(XC):
                    wait(pool, cxh_done, XC * b + j + 1)
                    pool.tensor_tensor(cx_lo[:, j, :], cx_raw[:, j, :], cx_hi[:, j, :], ALU.subtract).then_inc(cxl_done, 1)

            def power(b):
                wait(pool, veps_done, b + 1)
                wait(pool, xn_done, TC * b)
                pool.tensor_tensor(rstd[:], veps[:], mhalf[:], ALU.pow).then_inc(rstd_done, 1)

            def step(b, odd):
                if within(b, B):
                    residual_bias(b, odd)
                    ctl(b)
                if within(b - 2, B):
                    power(b - 2)
                if within(b, B):
                    cxl(b)

            for b in range(4):
                step(b, b % 2)
            with pool.Fori(2, B // 2) as i:
                for odd in range(2):
                    step(2 * i + odd, odd)
            for b in range(B, B + 2):
                step(b, b % 2)


def feed_forward(nc, io, x2, out, raw, raw_in):
    with ExitStack() as ctx:
        c_hi = ctx.enter_context(nc.sbuf_tensor("f_c_hi", [128, KC, T], F32R))
        c_lo = ctx.enter_context(nc.sbuf_tensor("f_c_lo", [128, KC, T], F32R))
        identity = ctx.enter_context(nc.sbuf_tensor("f_identity", [128, 128], F32))
        wo, uo = (tuple(ctx.enter_context(nc.sbuf_tensor(f"f_{n}_{part}", [128, KC, D], F32R)) for part in ("hi", "lo"))
                  for n in ("wo", "uo"))
        recurrence(nc, io, x2, identity, c_hi, c_lo, wo, uo, raw, raw_in)
        output_gate(nc, io, x2, out, identity, c_hi, c_lo, wo, uo)


def recurrence(nc, io, x2, identity, c_hi, c_lo, wo, uo, raw, raw_in):
    GATES = ("f", "i", "c")
    HC = KC // 2
    with ExitStack() as ctx:
        def sb(name, shape, dt=F32):
            return ctx.enter_context(nc.sbuf_tensor("f_" + name, shape, dt))

        def sem(name):
            return ctx.enter_context(nc.semaphore("f_" + name))

        w = {n: (sb(n + "_hi", [128, KC, D], F32R), sb(n + "_lo", [128, KC, D], F32R))
             for n in ("wf", "wi", "wc", "uf", "ui", "uc")}
        plan = [(io[n + "_t"], *w[n]) for n in w] + [(io["uo_t"], *uo), (io["wo_t"], *wo)]

        bias = sb("bias", [128, 3, KC])
        bias_raw = sb("bias_raw", [128, 3, KC])
        c0 = sb("c0", [128, KC])
        x2_raw = sb("x2_raw", [R, TC, D])
        xt_hi = sb("xt_hi", [128, KC, T], F32R)
        xt_lo = sb("xt_lo", [128, KC, T], F32R)
        gate = sb("gate", [128, 3, KC, T])
        keep = sb("keep", [128, KC, T])
        fresh = sb("fresh", [128, KC, T])
        c = sb("c", [128, KC, T])

        ps_gate = ctx.enter_context(nc.psum_tensor("f_ps_gate", [128, 6, 512], F32))
        ps_x = ctx.enter_context(nc.psum_tensor("f_ps_x", [128, 2, 512], F32))

        made = sem("made")
        w_rounded = sem("w_rounded")
        w_split = sem("w_split")
        b_in = sem("b_in")
        bias_done = sem("bias_done")
        x2_in = sem("x2_in")
        xt_done = sem("xt_done")
        xth_done = sem("xth_done")
        xtl_done = sem("xtl_done")
        xpart_done = sem("xpart_done")
        gate_done = sem("gate_done")
        act_done = sem("act_done")
        c_start = sem("c_start")
        keep_done = sem("keep_done")
        fresh_done = sem("fresh_done")
        sum_done = sem("sum_done")
        c_done = sem("c_done")
        ch_done = sem("ch_done")
        cl_done = sem("cl_done")

        block = ctx.enter_context(nc.Block())

        def region(bank, k):
            return ps_gate[:, bank, k * T:k * T + T]

        @block.sync
        def _(sp):
            def load(b):
                wait(sp, xt_done, b)
                sp.dma_start(x2_raw[:], x2[b].rearrange("(c p) d -> p c d", p=R)).then_inc(x2_in, 16)

            load(0)
            with nc.allow_non_contiguous_dma(reason="biases by partition"):
                for j, n in enumerate(GATES):
                    sp.dma_start(bias_raw[:, j, :], io["b" + n].rearrange("(k p) -> p k", p=128)).then_inc(b_in, 16)
                sp.dma_start(c0[:], io["in_c"].rearrange("(k p) -> p k", p=128)).then_inc(b_in, 16)

            for i in range(3, len(plan)):
                sp.wait_ge(w_split, i - 2)
                load_weight(sp, raw[i % 3], raw_in[i % 3], plan[i][0])
            with sp.Fori(1, B) as b:
                load(b)

        @block.gpsimd
        def _(pool):
            pool.memset(identity[:], 1.0).then_inc(made, 1)
            pool.memset(keep[:], 0.0).then_inc(made, 1)
            pool.wait_ge(made, 2)
            pool.affine_select(out=identity[:], in_=identity[:], compare_op=ALU.is_equal, fill=0.0, base=0,
                               pattern=[[-1, 128]], channel_multiplier=1).then_inc(made, 1)
            for i in range(6, 8):
                _, hi, lo = plan[i]
                pool.wait_ge(raw_in[i % 3], 16 * (i // 3 + 2))
                pool.wait_ge(w_split, i)
                pool.tensor_copy(hi[:], raw[i % 3][:]).then_inc(w_rounded, 1)
                pool.wait_ge(w_rounded, i + 1)
                pool.tensor_tensor(lo[:], raw[i % 3][:], hi[:], ALU.subtract).then_inc(w_split, 1)

        @block.tensor
        def _(pe):
            pe.wait_ge(made, 3)

            def x_turn(b):
                wait(pe, x2_in, 16 * (b + 1))
                wait(pe, xtl_done, b)
                for k in range(KC):
                    for q in range(TC):
                        mm = pe.transpose(ps_x[:, k // 2, (k % 2) * T + q * R:(k % 2) * T + q * R + R],
                                          x2_raw[:, q, 128 * k:128 * k + 128], identity[0:R, 0:R])
                mm.then_inc(xt_done, 1)

            def x_part(b):
                wait(pe, xtl_done, b + 1)
                for half in range(2):
                    for j, n in enumerate(GATES):
                        bank = 3 * half + j
                        if isinstance(b, int) and b == 0 and half == 0:
                            pe.wait_ge(w_split, j + 1)
                        wait(pe, act_done, 6 * (b - 1) + bank + 1)
                        for k2 in range(HC):
                            i = 0
                            for wp, xp in ((0, xt_hi), (1, xt_hi), (0, xt_lo)):
                                for k in range(KC):
                                    m = HC * half + k2
                                    mm = pe.matmul(region(bank, k2), w["w" + n][wp][:, k, 128 * m:128 * m + 128], xp[:, k, :],
                                                   start=(k2 == 0 and i == 0), stop=False, skip_group_check=True)
                                    i += 1
                mm.then_inc(xpart_done, 1)

            def c_part(b):
                wait(pe, cl_done, 2 * (b + 1))
                for half in range(2):
                    for j, n in enumerate(GATES):
                        bank = 3 * half + j
                        if isinstance(b, int) and b == 0 and half == 0:
                            pe.wait_ge(w_split, 3 + j + 1)
                        for k2 in range(HC):
                            i = 0
                            for up, cp in ((0, c_hi), (1, c_hi), (0, c_lo)):
                                for k in range(KC):
                                    m = HC * half + k2
                                    mm = pe.matmul(region(bank, k2), w["u" + n][up][:, k, 128 * m:128 * m + 128], cp[:, k, :],
                                                   start=False, stop=(i == 3 * KC - 1), skip_group_check=True)
                                    i += 1
                        mm.then_inc(gate_done, 1)

            def step(b, more=True):
                x_part(b)
                if more:
                    x_turn(b + 1)
                c_part(b)

            x_turn(0)
            step(0)
            with pe.Fori(1, B - 1) as b:
                step(b)
            step(B - 1, more=False)

        @block.scalar
        def _(act):
            act.wait_ge(b_in, 64)
            act.activation(bias[:, 0:2, :], bias_raw[:, 0:2, :], ACT.Copy, scale=0.5).then_inc(bias_done, 1)
            act.activation(bias[:, 2, :], bias_raw[:, 2, :], ACT.Copy).then_inc(bias_done, 1)
            act.wait_ge(bias_done, 2)

            def xth(b):
                wait(act, xt_done, b + 1)
                wait(act, xpart_done, b)
                act.activation(xt_hi[:, 0:2, :], ps_x[:, 0, 0:2 * T], ACT.Copy)
                act.activation(xt_hi[:, 2:4, :], ps_x[:, 1, 0:2 * T], ACT.Copy).then_inc(xth_done, 1)

            def gates(b):
                for half in range(2):
                    for j in range(3):
                        wait(act, gate_done, 6 * b + 3 * half + j + 1)
                        wait(act, sum_done, 2 * (b - 1) + half + 1)
                        for k2 in range(HC):
                            m = HC * half + k2
                            a = act.activation(gate[:, j, m, :], region(3 * half + j, k2), ACT.Tanh, bias=bias[:, j, m:m + 1],
                                               scale=0.5 if j < 2 else 1.0)
                        a.then_inc(act_done, 1)

            def step(b, more=True):
                if more:
                    xth(b + 1)
                gates(b)

            xth(0)
            for i in range(6):
                act.wait_ge(raw_in[i % 3], 16 * (i // 3 + 2))
                act.activation(plan[i][1][:], raw[i % 3][:], ACT.Copy).then_inc(w_rounded, 1)
            step(0)
            with act.Fori(1, B - 1) as b:
                step(b)
            step(B - 1, more=False)

        @block.vector
        def _(dve):
            def start():
                dve.wait_ge(b_in, 64)
                dve.wait_ge(made, 2)
                for k in range(KC):
                    dve.tensor_scalar(c[:, k, :], keep[:, k, :], c0[:, k:k + 1], None, ALU.add).then_inc(c_start, 1)
                dve.wait_ge(c_start, KC)
                dve.tensor_copy(c_hi[:], c[:]).then_inc(c_start, 1)
                dve.wait_ge(c_start, KC + 1)
                dve.tensor_tensor(c_lo[:], c[:], c_hi[:], ALU.subtract).then_inc(cl_done, 2)

            def xtl(b):
                wait(dve, xth_done, b + 1)
                dve.tensor_tensor(xt_lo[:, 0:2, :], ps_x[:, 0, 0:2 * T], xt_hi[:, 0:2, :], ALU.subtract)
                dve.tensor_tensor(xt_lo[:, 2:4, :], ps_x[:, 1, 0:2 * T], xt_hi[:, 2:4, :], ALU.subtract).then_inc(xtl_done, 1)

            def state(b):
                for half in range(2):
                    n = 2 * b + half
                    cols = slice(HC * half, HC * half + HC)
                    wait(dve, act_done, 6 * b + 3 * half + 1)
                    dve.scalar_tensor_tensor(out=keep[:, cols, :], in0=gate[:, 0, cols, :], scalar=1.0, in1=c[:, cols, :],
                                             op0=ALU.add, op1=ALU.mult).then_inc(keep_done, 1)
                    wait(dve, act_done, 6 * b + 3 * half + 3)
                    dve.scalar_tensor_tensor(out=fresh[:, cols, :], in0=gate[:, 1, cols, :], scalar=1.0, in1=gate[:, 2, cols, :],
                                             op0=ALU.add, op1=ALU.mult).then_inc(fresh_done, 1)
                    wait(dve, keep_done, n + 1)
                    wait(dve, fresh_done, n + 1)
                    dve.tensor_tensor(keep[:, cols, :], keep[:, cols, :], fresh[:, cols, :], ALU.add).then_inc(sum_done, 1)
                    wait(dve, sum_done, n + 1)
                    dve.tensor_scalar(c[:, cols, :], keep[:, cols, :], 0.5, None, ALU.mult).then_inc(c_done, 1)
                for half in range(2):
                    n = 2 * b + half
                    cols = slice(HC * half, HC * half + HC)
                    wait(dve, c_done, n + 1)
                    wait(dve, gate_done, 6 * (b + 1))
                    dve.tensor_copy(c_hi[:, cols, :], c[:, cols, :]).then_inc(ch_done, 1)
                    wait(dve, ch_done, n + 1)
                    dve.tensor_tensor(c_lo[:, cols, :], c[:, cols, :], c_hi[:, cols, :], ALU.subtract).then_inc(cl_done, 1)

            def step(b, more=True):
                if more:
                    xtl(b + 1)
                state(b)

            xtl(0)
            for i in range(6):
                dve.wait_ge(w_rounded, i + 1)
                dve.tensor_tensor(plan[i][2][:], raw[i % 3][:], plan[i][1][:], ALU.subtract).then_inc(w_split, 1)
                if i == 1:
                    start()
            step(0)
            with dve.Fori(1, B - 1) as b:
                step(b)
            step(B - 1, more=False)


def output_gate(nc, io, x2, out, identity, c_hi, c_lo, wo, uo):
    SLOTS = 4
    with ExitStack() as ctx:
        def sb(name, shape, dt=F32):
            return ctx.enter_context(nc.sbuf_tensor("o_" + name, shape, dt))

        def sem(name):
            return ctx.enter_context(nc.semaphore("o_" + name))

        bo_all = sb("bo_all", [R, D])
        mhalf = sb("mhalf", [R, TC, 1])
        base = sb("base", [R, TC, D])
        x2_raw = sb("x2_raw", [R, SLOTS, TC, D])
        xt_hi = sb("xt_hi", [128, 2, KC, T], F32R)
        xt_lo = sb("xt_lo", [128, 2, KC, T], F32R)
        pre = sb("pre", [R, 2, TC, D])
        h = sb("h", [R, 2, TC, D])
        r = sb("r", [R, 2, TC, D])
        stats = sb("stats", [R, 2, TC, 6])
        mv = sb("mv", [R, 2, TC, 2])
        veps = sb("veps", [R, 2, TC, 1])
        rstd = sb("rstd", [R, 2, TC, 1])
        y = sb("y", [R, 2, TC, D])

        ps_x = ctx.enter_context(nc.psum_tensor("o_ps_x", [128, 2, 2, 512], F32))
        ps_o = ctx.enter_context(nc.psum_tensor("o_ps_o", [128, 2, 2, 512], F32))

        made = sem("made")
        bo_in = sem("bo_in")
        x2_in = [sem(f"x2_in{i}") for i in range(SLOTS)]
        base_mm = sem("base_mm")
        base_done = sem("base_done")
        xt_done = sem("xt_done")
        xth_done = sem("xth_done")
        xtl_done = sem("xtl_done")
        o_done = sem("o_done")
        pre_done = sem("pre_done")
        h_done = sem("h_done")
        r_done = sem("r_done")
        stats_done = sem("stats_done")
        mv_done = sem("mv_done")
        veps_done = sem("veps_done")
        rstd_done = sem("rstd_done")
        y_done = sem("y_done")
        stored = [sem(f"stored{i}") for i in range(2)]

        block = ctx.enter_context(nc.Block())


        @block.sync
        def _(sp):
            sp.dma_start(bo_all[:], io["bo"].rearrange("(a d) -> a d", a=1).to_broadcast((R, D))).then_inc(bo_in, 16)

            def load(n, u):
                wait(sp, r_done, n - SLOTS + 1)
                sp.dma_start(x2_raw[:, u, :, :], x2[n].rearrange("(c p) d -> p c d", p=R)).then_inc(x2_in[u], 16)

            def store(n, s):
                sp.wait_ge(y_done, n + 1)
                sp.dma_start(out[n].rearrange("(c p) d -> p c d", p=R), y[:, s, :, :]).then_inc(stored[s], 16)

            for u in range(SLOTS):
                load(u, u)
            with sp.Fori(1, B // SLOTS) as i:
                for u in range(SLOTS):
                    load(SLOTS * i + u, u)
                    store(SLOTS * (i - 1) + u, u % 2)
            for u in range(SLOTS):
                store(B - SLOTS + u, u % 2)
            for s in range(2):
                sp.wait_ge(stored[s], 16 * (B // 2))

        @block.tensor
        def _(pe):
            for q in range(TC):
                i = 0
                for cp, up in ((c_hi, 0), (c_hi, 1), (c_lo, 0)):
                    for k in range(KC):
                        mm = pe.matmul(ps_o[0:R, 0, q, :], cp[:, k, q * R:q * R + R], uo[up][:, k, :],
                                       start=(i == 0), stop=(i == 3 * KC - 1))
                        i += 1
            mm.then_inc(base_mm, 1)

            def turn(i, u):
                n, s = SLOTS * i + u, u % 2
                if not within(n, B):
                    return
                wait(pe, x2_in[u % SLOTS], 16 * (i + u // SLOTS + 1))
                wait(pe, xtl_done, n - 1)
                for k in range(KC):
                    for q in range(TC):
                        mm = pe.transpose(ps_x[:, s, k // 2, (k % 2) * T + q * R:(k % 2) * T + q * R + R],
                                          x2_raw[:, u % SLOTS, q, 128 * k:128 * k + 128], identity[0:R, 0:R])
                mm.then_inc(xt_done, 1)

            def product(i, u):
                n, s = SLOTS * i + u, u % 2
                wait(pe, xtl_done, n + 1)
                wait(pe, pre_done, n - 1)
                if s == 0:
                    pe.wait_ge(base_done, 1)
                for q in range(TC):
                    j = 0
                    for xp, wp in ((xt_hi, 0), (xt_hi, 1), (xt_lo, 0)):
                        for k in range(KC):
                            mm = pe.matmul(ps_o[0:R, s, q, :], xp[:, s, k, q * R:q * R + R], wo[wp][:, k, :],
                                           start=(j == 0), stop=(j == 3 * KC - 1))
                            j += 1
                mm.then_inc(o_done, 1)

            turn(0, 0)

            def steps(i):
                for u in range(SLOTS):
                    turn(i, u + 1)
                    product(i, u)

            steps(0)
            with pe.Fori(1, B // SLOTS - 1) as i:
                steps(i)
            steps(B // SLOTS - 1)

        @block.scalar
        def _(act):
            def xth(n, u):
                if not within(n, B):
                    return
                wait(act, xt_done, n + 1)
                wait(act, o_done, n - 1)
                for k in range(2):
                    a = act.activation(xt_hi[:, u % 2, 2 * k:2 * k + 2, :], ps_x[:, u % 2, k, 0:2 * T], ACT.Copy)
                a.then_inc(xth_done, 1)

            def tanh(n, u):
                if not within(n, B):
                    return
                wait(act, pre_done, n + 1)
                wait(act, r_done, n - 1)
                act.activation(h[:, u % 2, :, :], pre[:, u % 2, :, :], ACT.Tanh).then_inc(h_done, 1)

            xth(0, 0)

            def steps(i):
                for u in range(SLOTS):
                    xth(SLOTS * i + u + 1, u + 1)
                    tanh(SLOTS * i + u, u)

            steps(0)
            with act.Fori(1, B // SLOTS - 1) as i:
                steps(i)
            steps(B // SLOTS - 1)

        @block.vector
        def _(dve):
            dve.wait_ge(base_mm, 1)
            dve.wait_ge(bo_in, 16)
            dve.tensor_tensor(base[:], ps_o[0:R, 0, :, :], bo_all[:, :].rearrange("p (a d) -> p a d", a=1).to_broadcast((R, TC, D)),
                              ALU.add).then_inc(base_done, 1)
            dve.wait_ge(base_done, 1)

            def xtl(n, u):
                if not within(n, B):
                    return
                s = u % 2
                wait(dve, xth_done, n + 1)
                for k in range(2):
                    v = dve.tensor_tensor(xt_lo[:, s, 2 * k:2 * k + 2, :], ps_x[:, s, k, 0:2 * T], xt_hi[:, s, 2 * k:2 * k + 2, :],
                                          ALU.subtract)
                v.then_inc(xtl_done, 1)

            def with_base(n, u):
                if not within(n, B):
                    return
                wait(dve, o_done, n + 1)
                wait(dve, h_done, n - 1)
                dve.tensor_tensor(pre[:, u % 2, :, :], ps_o[0:R, u % 2, :, :], base[:], ALU.add).then_inc(pre_done, 1)

            def statistics(n, u):
                if not within(n, B):
                    return
                s = u % 2
                wait(dve, r_done, n + 1)
                for q in range(TC):
                    v = dve.bn_stats(stats[:, s, q, :], r[:, s, q, :])
                v.then_inc(stats_done, 1)
                dve.wait_ge(base_done, 1)
                wait(dve, stats_done, n + 1)
                for q in range(TC):
                    v = dve.bn_aggr(mv[:, s, q, :], stats[:, s, q, :])
                v.then_inc(mv_done, 1)
                wait(dve, mv_done, n + 1)
                dve.tensor_scalar(veps[:, s, :, 0], mv[:, s, :, 1], EPS, None, ALU.add).then_inc(veps_done, 1)

            def norm(n, u):
                if not within(n, B):
                    return
                s = u % 2
                wait(dve, rstd_done, n + 1)
                wait(dve, stored[s], 8 * (n - s))
                for q in range(TC):
                    v = dve.tensor_scalar(y[:, s, q, :], r[:, s, q, :], mv[:, s, q, 0:1], rstd[:, s, q, :], ALU.subtract, ALU.mult)
                v.then_inc(y_done, 1)

            xtl(0, 0)

            def steps(i):
                for u in range(SLOTS):
                    n = SLOTS * i + u
                    xtl(n + 1, u + 1)
                    statistics(n - 1, u + 1)
                    with_base(n, u)
                    norm(n - 1, u + 1)

            steps(0)
            with dve.Fori(1, B // SLOTS - 1) as i:
                steps(i)
            steps(B // SLOTS - 1)
            statistics(B - 1, 1)
            norm(B - 1, 1)

        @block.gpsimd
        def _(pool):
            pool.memset(mhalf[:], -0.5).then_inc(made, 1)
            pool.wait_ge(made, 1)

            def residual(n, u):
                wait(pool, h_done, n + 1)
                wait(pool, y_done, n - 1)
                pool.tensor_tensor(r[:, u % 2, :, :], h[:, u % 2, :, :], x2_raw[:, u, :, :], ALU.add).then_inc(r_done, 1)

            def power(n, u):
                wait(pool, veps_done, n + 1)
                wait(pool, y_done, n - 1)
                pool.tensor_tensor(rstd[:, u % 2, :, :], veps[:, u % 2, :, :], mhalf[:], ALU.pow).then_inc(rstd_done, 1)

            def steps(i):
                for u in range(SLOTS):
                    residual(SLOTS * i + u, u)
                    power(SLOTS * i + u, u)

            steps(0)
            with pool.Fori(1, B // SLOTS) as i:
                steps(i)


def decoder(nc, io, out):
    x1 = nc.dram_tensor("x1_scratch", (B, T, D), F32, kind="Internal").ap()
    x2 = nc.dram_tensor("x2_scratch", (B, T, D), F32, kind="Internal").ap()
    with ExitStack() as ctx:
        raw = [ctx.enter_context(nc.sbuf_tensor(f"w_raw{i}", [128, KC, D], F32)) for i in range(3)]
        raw_in = [ctx.enter_context(nc.semaphore(f"w_raw_in{i}")) for i in range(3)]
        self_attention(nc, io, x1, raw, raw_in)
        cross_attention(nc, io, x1, x2, raw, raw_in)
        feed_forward(nc, io, x2, out, raw, raw_in)


def kernel(**inputs):
    from concourse import bacc
    from concourse.bass_utils import run_bass_kernel_spmd

    a = {k: np.asarray(v) for k, v in inputs.items()}
    laid_out = {
        "x": a["x"],
        "xt": a["x"].reshape(B, T, H, C).transpose(0, 3, 2, 1),
        "cx": a["ctx_1024"],
        "ct": a["ctx_1024"].transpose(0, 2, 1),
        "wq": a["L0_attn_Wq"],
        "wk": a["L0_attn_Wk"],
        "wv": a["L0_attn_Wv"],
        "wu_t": a["L0_attn_Wu"].T,
        "bu": a["L0_attn_bu"],
        "xwq": a["L0_xattn_Wq"],
        "xwk": a["L0_xattn_Wk"],
        "xwv_t": a["L0_xattn_Wv"].T,
        "xbq": a["L0_xattn_bq"],
        "xbk": a["L0_xattn_bk"],
        "xbv": a["L0_xattn_bv"],
        "in_c": a["L0_ffn_in_c"],
    }
    for n in "fico":
        laid_out["w" + n + "_t"] = a["L0_ffn_w" + n].T
        laid_out["u" + n + "_t"] = a["L0_ffn_u" + n].T
        laid_out["b" + n] = a["L0_ffn_b" + n]

    nc = bacc.Bacc("TRN2", target_bir_lowering=False, num_devices=1)
    arrays, io = {}, {}
    for name, array in laid_out.items():
        arrays["in_" + name] = np.ascontiguousarray(array)
        io[name] = nc.dram_tensor("in_" + name, array.shape, F32, kind="ExternalInput").ap()
    out = nc.dram_tensor("out", (B, T, D), F32, kind="ExternalOutput").ap()
    decoder(nc, io, out)
    result = run_bass_kernel_spmd(nc, [arrays], core_ids=[0])
    return result.results[0]["out"]
```

```python
from contextlib import ExitStack

import numpy as np
import concourse.bass as bass
from concourse import mybir

F32 = mybir.dt.float32
F32R = mybir.dt.float32r
BF16 = mybir.dt.bfloat16
ALU = mybir.AluOpType
ACT = mybir.ActivationFunctionType
AX = mybir.AxisListType

B, T, D = 16, 224, 512
H, C = 16, 32
TC = 2
R = T // TC
KC = D // 128
TX = 750
XC, XR = 6, 125
XH = TX // 2
G = 4
NG = H // G
NEG = -1.0e30
EPS = 1e-5


def wait(eng, sem, value):
    if not (isinstance(value, int) and value <= 0):
        eng.wait_ge(sem, value)


def within(n, end):
    return not isinstance(n, int) or 0 <= n < end


def load_weight(sp, buffer, landed, dram):
    sp.dma_start(buffer[:], dram.rearrange("(k p) e -> p k e", p=128)).then_inc(landed, 16)


def self_attention(nc, io, x1, raw, raw_in):
    with ExitStack() as ctx:
        def sb(name, shape, dt=F32):
            return ctx.enter_context(nc.sbuf_tensor("a_" + name, shape, dt))

        def sem(name):
            return ctx.enter_context(nc.semaphore("a_" + name))

        identity = sb("identity", [128, 128])
        identity_b = sb("identity_b", [R, R], BF16)
        mask = sb("mask", [R, G, R], BF16)
        ones = sb("ones", [R, 1])
        wq3 = sb("wq3", [C, 3, C])
        wk3 = sb("wk3", [C, 3, C])
        a_f = sb("a_f", [3 * C, 3 * C])
        a_stack = sb("a_stack", [3 * C, 3 * C], F32R)
        wv_diag = sb("wv_diag", [128, 128])
        wu_raw = sb("wu_raw", [128, KC, D])
        w_hi = sb("w_hi", [128, KC, D], F32R)
        w_lo = sb("w_lo", [128, KC, D], F32R)
        identity_r = sb("identity_r", [R, R], F32R)
        bu_all = sb("bu_all", [R, D])
        bu_hi = sb("bu_hi", [R, D], F32R)
        bu_lo = sb("bu_lo", [R, D], F32R)
        xs_raw = sb("xs_raw", [3 * C, NG, G, T])
        xs = sb("xs", [3 * C, NG, G, T], F32R)
        v_raw = sb("v_raw", [R, NG, TC, 128])
        v_hi = sb("v_hi", [R, 2, TC, 128], F32R)
        v_lo = sb("v_lo", [R, 2, TC, 128], F32R)
        zs = sb("zs", [3 * C, 2, G, T], F32R)
        nmax = sb("nmax", [R, 2, TC, G])
        rsum = sb("rsum", [R, 2, TC, G])
        rinv = sb("rinv", [R, 2, TC, G])
        p0 = sb("p0", [R, 2, G, R])
        p1 = sb("p1", [R, 2, G, T])
        pt0_hi = sb("pt0_hi", [R, 2, G, T], F32R)
        pt0_lo = sb("pt0_lo", [R, 2, G, T], F32R)
        pt1_hi = sb("pt1_hi", [R, 2, G, R], F32R)
        pt1_lo = sb("pt1_lo", [R, 2, G, R], F32R)
        yt_hi = sb("yt_hi", [128, 2, NG, T], F32R)
        yt_lo = sb("yt_lo", [128, 2, NG, T], F32R)
        xres = sb("xres", [R, TC, D])
        r = sb("r", [R, TC, D])
        stats = sb("stats", [R, TC, 6])
        mv = sb("mv", [R, TC, 2])
        veps = sb("veps", [R, TC, 1])
        mhalf = sb("mhalf", [R, TC, 1])
        rstd = sb("rstd", [R, TC, 1])
        xn = sb("xn", [R, TC, D])

        ps_s = ctx.enter_context(nc.psum_tensor("a_ps_s", [128, 3, 512], F32))
        ps_t = ctx.enter_context(nc.psum_tensor("a_ps_t", [128, 2, 512], F32))
        ps_w = ctx.enter_context(nc.psum_tensor("a_ps_w", [128, 512], F32))
        ps_y = ctx.enter_context(nc.psum_tensor("a_ps_y", [128, 2, 512], F32))

        const_ready = sem("const_ready")
        w_in = sem("w_in")
        wu_in = sem("wu_in")
        diag_in = sem("diag_in")
        bu_in = sem("bu_in")
        prep_id = sem("prep_id")
        prep_mm = sem("prep_mm")
        prep_act = sem("prep_act")
        prep_dve = sem("prep_dve")
        xs_in = [sem(f"xs_in{i}") for i in range(NG)]
        v_in = [sem(f"v_in{i}") for i in range(NG)]
        res_in = sem("res_in")
        xh_done = sem("xh_done")
        xl_done = sem("xl_done")
        vh_done = sem("vh_done")
        vl_done = sem("vl_done")
        z_done = sem("z_done")
        zh_done = sem("zh_done")
        zl_done = sem("zl_done")
        s_done = sem("s_done")
        max_done = sem("max_done")
        exp_done = sem("exp_done")
        rinv_done = sem("rinv_done")
        norm_done = sem("norm_done")
        t_done = sem("t_done")
        pth_done = sem("pth_done")
        ptl_done = sem("ptl_done")
        pv_done = sem("pv_done")
        yh_done = sem("yh_done")
        yl_done = sem("yl_done")
        wu_done = sem("wu_done")
        r_done = sem("r_done")
        stats_done = sem("stats_done")
        mv_done = sem("mv_done")
        veps_done = sem("veps_done")
        rstd_done = sem("rstd_done")
        xn_done = sem("xn_done")
        stored = sem("stored")

        STEPS = B * NG

        def unit_bank(unit):
            return ps_t[0:R, int(unit > 0), 0:G * R].rearrange("p (h t) -> p h t", h=G)

        def transposed(pt0, pt1, g, unit):
            return (pt0[:, g % 2, :, R:T], pt1[:, g % 2, :, :], pt0[:, g % 2, :, 0:R])[unit]

        block = ctx.enter_context(nc.Block())

        @block.sync
        def _(sp):
            for j in range(3):
                sp.dma_start(wq3[:, j, :], io["wq"]).then_inc(w_in, 16)
                sp.dma_start(wk3[:, j, :], io["wk"]).then_inc(w_in, 16)
            def loads(b, g):
                n = NG * b + g
                if g == 3 and within(b - 2, B):
                    wait(sp, r_done, TC * (b - 2))
                wait(sp, xl_done, n - 3)
                for j in range(3):
                    sp.dma_start(xs_raw[C * j:C * j + C, g, :, :],
                                 io["xt"][b, :, G * g:G * g + G, :]).then_inc(xs_in[g], 16)
                if g == 3 and within(b - 2, B):
                    residual_input(b - 2)
                if g == 0 and within(b - 4, B):
                    store(b - 4)
                if g >= 2:
                    values(b, g - 2)
                elif within(b - 1, B):
                    values(b - 1, g + 2)

            def values(b, g):
                wait(sp, vl_done, NG * b + g - 3)
                sp.dma_start(v_raw[:, g, :, :], io["x"][b, :, 128 * g:128 * g + 128]
                             .rearrange("(c p) d -> p c d", p=R)).then_inc(v_in[g], 16)

            def residual_input(b):
                sp.dma_start(xres[:], io["x"][b].rearrange("(c p) d -> p c d", p=R)).then_inc(res_in, 16)

            def store(b):
                sp.wait_ge(xn_done, TC * (b + 1))
                sp.dma_start(x1[b].rearrange("(c p) d -> p c d", p=R), xn[:]).then_inc(stored, 16)

            for g in range(2):
                loads(0, g)
            load_weight(sp, wu_raw, wu_in, io["wu_t"])
            sp.wait_ge(const_ready, 1)
            for g in range(G):
                sp.dma_start(wv_diag[C * g:C * g + C, C * g:C * g + C], io["wv"]).then_inc(diag_in, 16)
            sp.dma_start(bu_all[:], io["bu"].rearrange("(a d) -> a d", a=1).to_broadcast((R, D))).then_inc(bu_in, 16)

            for n in range(2, 4 * NG):
                loads(n // NG, n % NG)
            for i, name in enumerate(("xwq", "xwk", "xwv_t")):
                load_weight(sp, raw[i], raw_in[i], io[name])
            with sp.Fori(4, B) as b:
                for g in range(NG):
                    loads(b, g)
            values(B - 1, 2)
            values(B - 1, 3)
            store(B - 4)
            for b in (B - 2, B - 1):
                sp.wait_ge(r_done, TC * b)
                residual_input(b)
                store(b - 1)
            store(B - 1)
            sp.wait_ge(stored, 16 * B)

        @block.tensor
        def _(pe):
            pe.wait_ge(const_ready, 5)
            pe.wait_ge(w_in, 6 * 16)
            pe.matmul(ps_y[0:3 * C, 0, 0:3 * C], wq3[:, :, :], wk3[:, :, :], start=True, stop=True).then_inc(prep_mm, 1)


            def z(n, g, half):
                if not within(n, STEPS):
                    return
                if half == 0:
                    wait(pe, xl_done, n + 1)
                wait(pe, zl_done, 2 * (n - 1) + half + 1)
                wait(pe, yl_done, 2 * (n - 5) + half + 1)
                pe.matmul(ps_y[0:3 * C, half, 0:2 * T], a_stack[:], xs[:, g, 2 * half:2 * half + 2, :],
                          start=True, stop=True).then_inc(z_done, 1)

            def s(n, g, banks):
                if not within(n, STEPS):
                    return
                if 0 in banks:
                    wait(pe, zl_done, 2 * (n + 1))
                for bank in banks:
                    wait(pe, exp_done, 3 * (n - 1) + bank + 1)
                    if bank < 2:
                        for h in range(2):
                            pe.matmul(ps_s[0:R, bank, h * T:h * T + T], zs[:, g % 2, 2 * bank + h, R:T],
                                      xs[:, g, 2 * bank + h, :], start=(h == 0), stop=False, skip_group_check=True)
                        diagonal = ps_s[0:R, bank, 0:2 * T].rearrange("p (h t) -> p h t", h=2)[:, :, R:T]
                        pe.matmul(diagonal, identity_b[:], mask[:, 0:2, :], start=False, stop=True,
                                  skip_group_check=True).then_inc(s_done, 1)
                    else:
                        for h in range(G):
                            pe.matmul(ps_s[0:R, 2, h * R:h * R + R], zs[:, g % 2, h, 0:R], xs[:, g, h, 0:R],
                                      start=(h == 0), stop=False, skip_group_check=True)
                        pe.matmul(ps_s[0:R, 2, 0:G * R], identity_b[:], mask[:, :, :], start=False, stop=True,
                                  skip_group_check=True).then_inc(s_done, 1)

            def t(n, g, units):
                if not within(n, STEPS):
                    return
                for unit in units:
                    wait(pe, norm_done, 2 * n + (2 if unit == 2 else 1))
                    wait(pe, ptl_done, (3 * n - 2, 3 * n, 3 * n + 2)[unit])
                    for h in range(G):
                        src = (p1[:, g % 2, h, 0:R], p1[:, g % 2, h, R:T], p0[:, g % 2, h, :])[unit]
                        mm = pe.transpose(ps_t[0:R, int(unit > 0), h * R:h * R + R], src, identity[0:R, 0:R])
                    mm.then_inc(t_done, 1)

            def pv(n, g, half):
                if not within(n, STEPS):
                    return
                if half == 0:
                    wait(pe, ptl_done, 3 * (n + 1))
                    wait(pe, vl_done, n + 1)
                last_z = min(n + 4, STEPS - 1) if isinstance(n, int) else n + 4
                wait(pe, zl_done, 2 * last_z + half + 1)
                wait(pe, yl_done, 2 * (n - 1) + half + 1)
                terms = ((v_hi, pt0_hi, pt1_hi), (v_hi, pt0_lo, pt1_lo), (v_lo, pt0_hi, pt1_hi))
                for i, (v, pt0, pt1) in enumerate(terms):
                    pe.matmul(ps_y[:, half, 0:2 * T], v[:, g % 2, 0, :], pt0[:, g % 2, 2 * half:2 * half + 2, :],
                              start=(i == 0), stop=False, skip_group_check=True)
                    later = ps_y[:, half, 0:2 * T].rearrange("p (h t) -> p h t", h=2)[:, :, R:T]
                    mm = pe.matmul(later, v[:, g % 2, 1, :], pt1[:, g % 2, 2 * half:2 * half + 2, :],
                                   start=False, stop=(i == 2), skip_group_check=True)
                mm.then_inc(pv_done, 1)

            def wu(b, odd, c, part):
                if not within(b, B):
                    return
                if part == 0:
                    wait(pe, yl_done, 2 * NG * (b + 1))
                    wait(pe, r_done, TC * b + c)
                products = [(identity_r[:], bu_hi[:]), (identity_r[:], bu_lo[:])]
                for y, w in ((yt_hi, w_hi), (yt_hi, w_lo), (yt_lo, w_hi)):
                    products += [(y[:, odd, k, c * R:c * R + R], w[:, k, :]) for k in range(KC)]
                first, last = PARTS[part]
                for i in range(first, last):
                    mm = pe.matmul(ps_w[0:R, :], *products[i], start=(i == 0), stop=(i == len(products) - 1))
                if last == len(products):
                    mm.then_inc(wu_done, 1)

            PARTS = ((0, 3), (3, 8), (8, 2 + 3 * KC))

            pe.wait_ge(prep_dve, 1)
            for n in range(2):
                for half in range(2):
                    z(n, n, half)
            pe.wait_ge(wu_in, 16)
            pe.wait_ge(diag_in, 4 * 16)
            for k in range(KC):
                if k >= 2:
                    pe.wait_ge(prep_dve, k)
                pe.matmul(ps_s[:, k % 2, :], wv_diag[:], wu_raw[:, k, :], start=True, stop=True).then_inc(prep_mm, 1)
            pe.wait_ge(prep_dve, 2 + KC)

            def steps(b, odd):
                for g in range(NG):
                    n = NG * b + g
                    projection = {3: (b - 1, 1 - odd, 0), 0: (b - 2, odd, 1)}.get(g, (-1, 0, 0))
                    s(n, g, (0, 1))
                    wu(*projection, 0)
                    s(n, g, (2,))
                    for half in range(2):
                        pv(n - 3, (g - 3) % NG, half)
                    t(n - 2, (g - 2) % NG, (2,))
                    wu(*projection, 1)
                    for half in range(2):
                        z(n + 2, (g + 2) % NG, half)
                    wu(*projection, 2)
                    t(n - 1, (g - 1) % NG, (0, 1))

            for b in range(4):
                steps(b, b % 2)
            with pe.Fori(2, B // 2 - 1) as i:
                for odd in range(2):
                    steps(2 * i + odd, odd)
            for b in range(B - 2, B + 1):
                steps(b, b % 2)
            for part in range(3):
                wu(B - 1, (B - 1) % 2, 1, part)

        @block.scalar
        def _(act):
            act.wait_ge(prep_mm, 1)
            act.activation(a_f[:], ps_y[0:3 * C, 0, 0:3 * C], ACT.Copy, scale=float(D) ** -0.5).then_inc(prep_act, 1)
            act.wait_ge(prep_act, 1)
            act.activation(a_stack[:], a_f[:], ACT.Copy).then_inc(prep_act, 1)

            def exp(n, g, banks):
                if not within(n, STEPS):
                    return
                for bank in banks:
                    wait(act, t_done, 3 * (n - 2) + (3 if bank == 2 else 2))
                    wait(act, max_done, 3 * n + bank + 1)
                    c = 0 if bank == 2 else 1
                    for h in range(G) if bank == 2 else (2 * bank, 2 * bank + 1):
                        src = ps_s[0:R, 2, h * R:h * R + R] if c == 0 else ps_s[0:R, bank, (h % 2) * T:(h % 2) * T + T]
                        e = act.activation((p1 if c else p0)[:, g % 2, h, :], src, ACT.Exp, bias=nmax[:, g % 2, c, h:h + 1],
                                           accum_out=rsum[:, g % 2, c, h:h + 1])
                    e.then_inc(exp_done, 1)

            def pth(n, g, units):
                if not within(n, STEPS):
                    return
                wait(act, pv_done, 2 * (n - 1))
                for unit in units:
                    wait(act, t_done, 3 * n + unit + 1)
                    act.activation(transposed(pt0_hi, pt1_hi, g, unit), unit_bank(unit), ACT.Copy).then_inc(pth_done, 1)

            def yh(n, g, b, odd, half):
                if not within(n, STEPS):
                    return
                if g == 0 and half == 0:
                    wait(act, wu_done, TC * (b - 1))
                wait(act, pv_done, 2 * n + half + 1)
                for h in (2 * half, 2 * half + 1):
                    y = act.activation(yt_hi[C * h:C * h + C, odd, g, :], ps_y[C * h:C * h + C, half, (h % 2) * T:(h % 2) * T + T], ACT.Copy)
                y.then_inc(yh_done, 1)

            def zh(n, g, half):
                if not within(n, STEPS):
                    return
                wait(act, s_done, 3 * (n - 1))
                wait(act, z_done, 2 * n + half + 1)
                act.activation(zs[:, g % 2, 2 * half:2 * half + 2, :], ps_y[0:3 * C, half, 0:2 * T], ACT.Copy).then_inc(zh_done, 1)

            for n in range(2):
                for half in range(2):
                    zh(n, n, half)
            for k in range(KC):
                act.wait_ge(prep_mm, 2 + k)
                act.activation(w_hi[:, k, :], ps_s[:, k % 2, :], ACT.Copy).then_inc(prep_act, 1)
            act.wait_ge(const_ready, 5)
            act.activation(identity_r[:], identity[0:R, 0:R], ACT.Copy).then_inc(prep_act, 1)
            act.wait_ge(bu_in, 16)
            act.activation(bu_hi[:], bu_all[:], ACT.Copy).then_inc(prep_act, 1)

            def steps(b, odd):
                for g in range(NG):
                    n = NG * b + g
                    y_odd = odd if g == 3 else 1 - odd
                    pth(n - 2, (g - 2) % NG, (0, 1))
                    exp(n, g, (0,))
                    for half in range(2):
                        yh(n - 3, (g - 3) % NG, b, y_odd, half)
                    pth(n - 2, (g - 2) % NG, (2,))
                    exp(n, g, (1,))
                    for half in range(2):
                        zh(n + 2, (g + 2) % NG, half)
                    exp(n, g, (2,))

            for b in range(4):
                steps(b, b % 2)
            with act.Fori(2, B // 2 - 1) as i:
                for odd in range(2):
                    steps(2 * i + odd, odd)
            for b in range(B - 2, B + 1):
                steps(b, b % 2)

        @block.vector
        def _(dve):
            def xh(n, g, b):
                if not within(n, STEPS):
                    return
                wait(dve, xs_in[g], 48 * (b + 1))
                wait(dve, s_done, 3 * (n - 3))
                dve.tensor_copy(xs[:, g, :, :], xs_raw[:, g, :, :]).then_inc(xh_done, 1)

            def smax(n, g, banks):
                if not within(n, STEPS):
                    return
                for bank in banks:
                    wait(dve, s_done, 3 * n + bank + 1)
                    if bank == 2:
                        dve.tensor_reduce(nmax[:, g % 2, 0, :], ps_s[0:R, 2, 0:G * R].rearrange("p (h t) -> p h t", h=G),
                                          AX.X, ALU.max, negate=True).then_inc(max_done, 1)
                        continue
                    dve.tensor_reduce(nmax[:, g % 2, 1, 2 * bank:2 * bank + 2], ps_s[0:R, bank, 0:2 * T].rearrange("p (h t) -> p h t", h=2),
                                      AX.X, ALU.max, negate=True).then_inc(max_done, 1)

            def inverse(n, g):
                if not within(n, STEPS):
                    return
                wait(dve, exp_done, 3 * (n + 1))
                wait(dve, norm_done, 2 * (n - 1))
                dve.reciprocal(rinv[:, g % 2, :, :], rsum[:, g % 2, :, :]).then_inc(rinv_done, 1)

            def ptl(n, g, unit):
                if not within(n, STEPS):
                    return
                wait(dve, pth_done, 3 * n + unit + 1)
                dve.tensor_tensor(transposed(pt0_lo, pt1_lo, g, unit), unit_bank(unit), transposed(pt0_hi, pt1_hi, g, unit),
                                  ALU.subtract).then_inc(ptl_done, 1)

            def yl(n, g, odd, half):
                if not within(n, STEPS):
                    return
                wait(dve, yh_done, 2 * n + half + 1)
                for h in (2 * half, 2 * half + 1):
                    y = dve.tensor_tensor(yt_lo[C * h:C * h + C, odd, g, :], ps_y[C * h:C * h + C, half, (h % 2) * T:(h % 2) * T + T],
                                          yt_hi[C * h:C * h + C, odd, g, :], ALU.subtract)
                y.then_inc(yl_done, 1)

            def zl(n, g, half):
                if not within(n, STEPS):
                    return
                wait(dve, zh_done, 2 * n + half + 1)
                low = zs[2 * C:3 * C, g % 2, 2 * half:2 * half + 2, :]
                dve.tensor_tensor(low, ps_y[2 * C:3 * C, half, 0:2 * T], low, ALU.subtract).then_inc(zl_done, 1)

            def residual(b, c):
                if not within(b, B):
                    return
                wait(dve, res_in, 16 * (b + 1))
                wait(dve, wu_done, TC * b + c + 1)
                wait(dve, xn_done, TC * b)
                dve.tensor_tensor(r[:, c, :], ps_w[0:R, :], xres[:, c, :], ALU.add).then_inc(r_done, 1)

            def statistics(b):
                if not within(b, B):
                    return
                for c in range(TC):
                    wait(dve, r_done, TC * b + c + 1)
                    dve.bn_stats(stats[:, c, :], r[:, c, :]).then_inc(stats_done, 1)
                for c in range(TC):
                    dve.wait_ge(prep_act, 1)
                    wait(dve, stats_done, TC * b + c + 1)
                    dve.bn_aggr(mv[:, c, :], stats[:, c, :]).then_inc(mv_done, 1)
                wait(dve, mv_done, TC * (b + 1))
                dve.tensor_scalar(veps[:, :, 0], mv[:, :, 1], EPS, None, ALU.add).then_inc(veps_done, 1)

            def norm(b):
                if not within(b, B):
                    return
                wait(dve, rstd_done, b + 1)
                wait(dve, stored, 16 * b)
                for c in range(TC):
                    dve.tensor_scalar(xn[:, c, :], r[:, c, :], mv[:, c, 0:1], rstd[:, c, :], ALU.subtract, ALU.mult)\
                       .then_inc(xn_done, 1)

            xh(0, 0, 0)
            xh(1, 1, 0)
            xh(2, 2, 0)
            dve.wait_ge(prep_act, 2)
            dve.tensor_tensor(a_stack[2 * C:3 * C, :], a_f[2 * C:3 * C, :], a_stack[2 * C:3 * C, :], ALU.subtract).then_inc(prep_dve, 1)
            for n in range(2):
                for half in range(2):
                    zl(n, n, half)
            for k in range(KC):
                dve.wait_ge(prep_act, 3 + k)
                dve.tensor_tensor(w_lo[:, k, :], ps_s[:, k % 2, :], w_hi[:, k, :], ALU.subtract).then_inc(prep_dve, 1)
            dve.wait_ge(prep_act, 4 + KC)
            dve.tensor_tensor(bu_lo[:], bu_all[:], bu_hi[:], ALU.subtract).then_inc(prep_dve, 1)

            def steps(b, odd):
                for g in range(NG):
                    n = NG * b + g
                    y_odd = odd if g == 3 else 1 - odd
                    if g < TC:
                        residual(b - 2, g)
                    smax(n, g, (0, 1))
                    inverse(n - 1, (g - 1) % NG)
                    for unit in range(2):
                        ptl(n - 2, (g - 2) % NG, unit)
                    smax(n, g, (2,))
                    xh(n + 3, (g + 3) % NG, b + (g + 3) // NG)
                    for half in range(2):
                        yl(n - 3, (g - 3) % NG, y_odd, half)
                    ptl(n - 2, (g - 2) % NG, 2)
                    if g == 1:
                        statistics(b - 2)
                    if g == 2:
                        norm(b - 2)
                    for half in range(2):
                        zl(n + 2, (g + 2) % NG, half)

            for b in range(4):
                steps(b, b % 2)
            with dve.Fori(2, B // 2 - 1) as i:
                for odd in range(2):
                    steps(2 * i + odd, odd)
            for b in range(B - 2, B + 1):
                steps(b, b % 2)
            residual(B - 1, 0)
            residual(B - 1, 1)
            statistics(B - 1)
            norm(B - 1)

        @block.gpsimd
        def _(pool):
            pool.memset(wv_diag[:], 0.0).then_inc(const_ready, 1)
            pool.memset(identity[:], 1.0).then_inc(const_ready, 1)
            pool.memset(mask[:], 0.0).then_inc(const_ready, 1)
            pool.memset(mhalf[:], -0.5).then_inc(const_ready, 1)
            pool.wait_ge(const_ready, 4)
            pool.affine_select(out=identity[:], in_=identity[:], compare_op=ALU.is_equal, fill=0.0, base=0,
                               pattern=[[-1, 128]], channel_multiplier=1).then_inc(prep_id, 1)
            pool.affine_select(out=mask[:], in_=mask[:], compare_op=ALU.is_ge, fill=NEG, base=0,
                               pattern=[[0, G], [-1, R]], channel_multiplier=1).then_inc(prep_id, 1)
            pool.memset(ones[:], 1.0).then_inc(prep_id, 1)
            pool.wait_ge(prep_id, 3)
            pool.tensor_copy(identity_b[:], identity[0:R, 0:R]).then_inc(const_ready, 1)
            pool.wait_ge(const_ready, 5)

            def xl(n, g):
                if not within(n, STEPS):
                    return
                wait(pool, xh_done, n + 1)
                wait(pool, norm_done, 2 * (n - 3))
                wait(pool, vl_done, n - 5)
                low = xs[C:2 * C, g, :, :]
                pool.tensor_tensor(low, xs_raw[C:2 * C, g, :, :], low, ALU.subtract).then_inc(xl_done, 1)

            def values(n, g, b):
                if not within(n, STEPS):
                    return
                wait(pool, v_in[g], 16 * (b + 1))
                wait(pool, xl_done, min(n + 6, STEPS) if isinstance(n, int) else n + 6)
                wait(pool, pv_done, 2 * (n - 1))
                one = ones[:, :].rearrange("p (c d) -> p c d", c=1).to_broadcast((R, TC, 128))
                pool.tensor_tensor(v_hi[:, g % 2, :, :], v_raw[:, g, :, :], one, ALU.mult).then_inc(vh_done, 1)
                wait(pool, vh_done, n + 1)
                pool.tensor_tensor(v_lo[:, g % 2, :, :], v_raw[:, g, :, :], v_hi[:, g % 2, :, :], ALU.subtract)\
                    .then_inc(vl_done, 1)

            def normalise(n, g):
                if not within(n, STEPS):
                    return
                wait(pool, rinv_done, n + 1)
                wait(pool, xl_done, min(n + 4, STEPS) if isinstance(n, int) else n + 4)
                for c, p, w in ((1, p1, T), (0, p0, R)):
                    inv = rinv[:, g % 2, c, :].rearrange("p (h a) -> p h a", a=1).to_broadcast((R, G, w))
                    pool.tensor_tensor(p[:, g % 2, :, :], p[:, g % 2, :, :], inv, ALU.mult).then_inc(norm_done, 1)

            def power(b):
                if not within(b, B):
                    return
                wait(pool, veps_done, b + 1)
                wait(pool, xn_done, TC * b)
                pool.tensor_tensor(rstd[:], veps[:], mhalf[:], ALU.pow).then_inc(rstd_done, 1)
                wait(pool, rstd_done, b + 1)

            xl(0, 0)
            xl(1, 1)
            xl(2, 2)

            def steps(b):
                for g in range(NG):
                    n = NG * b + g
                    normalise(n - 1, (g - 1) % NG)
                    if g == 2:
                        power(b - 2)
                    xl(n + 3, (g + 3) % NG)
                    values(n - 2, (g - 2) % NG, b if g >= 2 else b - 1)

            for b in range(3):
                steps(b)
            with pool.Fori(3, B - 1) as b:
                steps(b)
            steps(B - 1)
            steps(B)
            power(B - 1)


def cross_attention(nc, io, x1, x2, raw, raw_in):
    with ExitStack() as ctx:
        def sb(name, shape, dt=F32):
            return ctx.enter_context(nc.sbuf_tensor("x_" + name, shape, dt))

        def sem(name):
            return ctx.enter_context(nc.semaphore("x_" + name))

        identity = sb("identity", [128, 128])
        m_hi = sb("m_hi", [128, KC, D], F32R)
        m_lo = sb("m_lo", [128, KC, D], F32R)
        wv_hi = sb("wv_hi", [128, KC, D], F32R)
        wv_lo = sb("wv_lo", [128, KC, D], F32R)
        zbias = sb("zbias", [128, KC])
        kbias = sb("kbias", [R, D])
        qk_bias = sb("qk_bias", [R, 1])
        bv_all = sb("bv_all", [R, D])
        mhalf = sb("mhalf", [R, TC, 1])

        wq, wk, wv = raw
        bq = sb("bq", [128, KC, 1])
        bk = sb("bk", [128, KC, 1])
        bk_all = sb("bk_all", [128, KC, R])
        ones = sb("ones", [128, R])

        x1_raw = sb("x1_raw", [R, TC, D])
        x1b = sb("x1b", [R, 2, TC, D])
        x1t_hi = sb("x1t_hi", [128, KC, T], F32R)
        x1t_lo = sb("x1t_lo", [128, KC, T], F32R)
        zt_hi = sb("zt_hi", [128, KC, T], F32R)
        zt_lo = sb("zt_lo", [128, KC, T], F32R)
        ct_raw = sb("ct_raw", [128, KC, TX])
        ct_hi = sb("ct_hi", [128, KC, TX + 2], F32R)
        ct_lo = sb("ct_lo", [128, KC, TX + 2], F32R)
        cx_raw = sb("cx_raw", [XR, XC, D])
        cx_hi = sb("cx_hi", [XR, XC, D], F32R)
        cx_lo = sb("cx_lo", [XR, XC, D], F32R)
        dot = sb("dot", [R, D])
        rowdot = sb("rowdot", [R, TC])
        rowbias = sb("rowbias", [R, TC])
        smax = sb("smax", [R, TC])
        biased_max = sb("biased_max", [R, TC])
        shift = sb("shift", [R, TC])
        rsum = sb("rsum", [R, TC])
        rinv = sb("rinv", [R, TC])
        p = sb("p", [R, TC, TX])
        pt_hi = sb("pt_hi", [XR, XC, T], F32R)
        pt_lo = sb("pt_lo", [XR, XC, T], F32R)
        ot_hi = sb("ot_hi", [128, KC, T], F32R)
        ot_lo = sb("ot_lo", [128, KC, T], F32R)
        r = sb("r", [R, TC, D])
        stats = sb("stats", [R, TC, 6])
        mv = sb("mv", [R, TC, 2])
        veps = sb("veps", [R, TC, 1])
        rstd = sb("rstd", [R, TC, 1])
        xn = sb("xn", [R, TC, D])

        ps_s = ctx.enter_context(nc.psum_tensor("x_ps_s", [128, 4, 512], F32))
        ps_g = ctx.enter_context(nc.psum_tensor("x_ps_g", [128, 2, 512], F32))
        ps_h = ctx.enter_context(nc.psum_tensor("x_ps_h", [128, 2, 512], F32))

        bias_in = sem("bias_in")
        made = sem("made")
        spread = sem("spread")
        prep_mm = sem("prep_mm")
        prep_hi = sem("prep_hi")
        prep_lo = sem("prep_lo")
        PREPARED = 2 * KC + 1
        pad_done = sem("pad_done")
        x1_in = sem("x1_in")
        ct_in = sem("ct_in")
        cx_in = sem("cx_in")
        x1b_done = sem("x1b_done")
        x1t_done = sem("x1t_done")
        x1th_done = sem("x1th_done")
        x1tl_done = sem("x1tl_done")
        cth_done = sem("cth_done")
        ctl_done = sem("ctl_done")
        cxh_done = sem("cxh_done")
        cxl_done = sem("cxl_done")
        zt_done = sem("zt_done")
        zth_done = sem("zth_done")
        ztl_done = sem("ztl_done")
        s_done = sem("s_done")
        dot_done = sem("dot_done")
        rowbias_done = sem("rowbias_done")
        max_done = sem("max_done")
        biased_done = sem("biased_done")
        shift_done = sem("shift_done")
        exp_done = sem("exp_done")
        rinv_done = sem("rinv_done")
        pt_done = sem("pt_done")
        pth_done = sem("pth_done")
        ptl_done = sem("ptl_done")
        ot_done = sem("ot_done")
        oth_done = sem("oth_done")
        otl_done = sem("otl_done")
        out_done = sem("out_done")
        r_done = sem("r_done")
        stats_done = sem("stats_done")
        mv_done = sem("mv_done")
        veps_done = sem("veps_done")
        rstd_done = sem("rstd_done")
        xn_done = sem("xn_done")
        stored = sem("stored")

        block = ctx.enter_context(nc.Block())

        def pair(bank, k):
            return bank[:, k // 2, (k % 2) * T:(k % 2) * T + T]

        @block.sync
        def _(sp):
            def loads(b):
                wait(sp, x1b_done, b)
                wait(sp, x1t_done, b)
                wait(sp, rowbias_done, b)
                sp.dma_start(x1_raw[:], x1[b].rearrange("(c p) d -> p c d", p=R)).then_inc(x1_in, 16)
                wait(sp, ctl_done, KC * b)
                sp.dma_start(ct_raw[:], io["ct"][b].rearrange("(k p) t -> p k t", p=128)).then_inc(ct_in, 16)
                if within(b - 3, B):
                    store(b - 3)
                wait(sp, cxl_done, XC * b)
                sp.dma_start(cx_raw[:], io["cx"][b].rearrange("(c p) d -> p c d", p=XR)).then_inc(cx_in, 16)

            def store(b):
                sp.wait_ge(xn_done, TC * (b + 1))
                sp.dma_start(x2[b].rearrange("(c p) d -> p c d", p=R), xn[:]).then_inc(stored, 16)

            sp.dma_start(bv_all[:], io["xbv"].rearrange("(a d) -> a d", a=1).to_broadcast((R, D))).then_inc(bias_in, 16)
            with nc.allow_non_contiguous_dma(reason="biases by partition"):
                sp.dma_start(bq[:], io["xbq"].rearrange("(k p a) -> p k a", p=128, a=1)).then_inc(bias_in, 16)
                sp.dma_start(bk[:], io["xbk"].rearrange("(k p a) -> p k a", p=128, a=1)).then_inc(bias_in, 16)
            for b in range(3):
                loads(b)
            sp.wait_ge(prep_lo, PREPARED)
            for i, name in enumerate(("wf_t", "wi_t", "wc_t")):
                load_weight(sp, raw[i], raw_in[i], io[name])
            with sp.Fori(3, B) as b:
                loads(b)
            for b in range(B - 3, B):
                store(b)
            sp.wait_ge(stored, 16 * B)

        @block.tensor
        def _(pe):
            pe.wait_ge(raw_in[0], 16)
            pe.wait_ge(raw_in[1], 16)
            for dk in range(KC):
                for k in range(KC):
                    mm = pe.matmul(ps_s[:, dk, :], wq[:, k, 128 * dk:128 * dk + 128], wk[:, k, :], start=(k == 0), stop=(k == KC - 1))
                mm.then_inc(prep_mm, 1)
            pe.wait_ge(bias_in, 48)
            pe.wait_ge(spread, KC)
            for k in range(KC):
                pe.matmul(ps_g[0:R, 1, :], bk_all[:, k, :], wq[:, k, :], start=(k == 0), stop=(k == KC - 1))
            for ck in range(KC):
                for k in range(KC):
                    pe.matmul(ps_g[:, 0, ck:ck + 1], wk[:, k, 128 * ck:128 * ck + 128], bq[:, k, :], start=(k == 0), stop=(k == KC - 1))
            for k in range(KC):
                mm = pe.matmul(ps_h[0:R, 0, 0:1], bk_all[:, k, :], bq[:, k, :], start=(k == 0), stop=(k == KC - 1))
            mm.then_inc(prep_mm, 1)
            pe.wait_ge(made, 4)
            pe.wait_ge(pad_done, 2)
            pe.wait_ge(prep_lo, PREPARED)

            def x1_turn(b):
                wait(pe, x1_in, 16 * (b + 1))
                wait(pe, otl_done, b - 1)
                for k in range(KC):
                    for c in range(TC):
                        mm = pe.transpose(ps_g[:, k // 2, (k % 2) * T + c * R:(k % 2) * T + c * R + R],
                                          x1_raw[:, c, 128 * k:128 * k + 128], identity[0:R, 0:R])
                mm.then_inc(x1t_done, 1)

            def p_turn(b):
                wait(pe, exp_done, TC * (b + 1))
                for j in range(XC):
                    for c in range(TC):
                        mm = pe.transpose(ps_s[0:XR, j // 2, (j % 2) * T + c * R:(j % 2) * T + c * R + R],
                                          p[:, c, XR * j:XR * j + XR], identity[0:R, 0:R])
                mm.then_inc(pt_done, 1)

            def zt(b):
                wait(pe, x1tl_done, b + 1)
                wait(pe, r_done, TC * (b - 1))
                for ck in range(KC):
                    i = 0
                    for m, x in ((m_hi, x1t_hi), (m_lo, x1t_hi), (m_hi, x1t_lo)):
                        for k in range(KC):
                            mm = pe.matmul(pair(ps_h, ck), m[:, k, 128 * ck:128 * ck + 128], x[:, k, :],
                                           start=(i == 0), stop=(i == 3 * KC - 1))
                            i += 1
                mm.then_inc(zt_done, 1)

            def ot(b):
                wait(pe, ptl_done, b + 1)
                wait(pe, cxl_done, XC * (b + 1))
                wait(pe, x1tl_done, min(b + 2, B) if isinstance(b, int) else b + 2)
                for dk in range(KC):
                    i = 0
                    for v, q in ((cx_hi, pt_hi), (cx_lo, pt_hi), (cx_hi, pt_lo)):
                        for j in range(XC):
                            mm = pe.matmul(pair(ps_g, dk), v[:, j, 128 * dk:128 * dk + 128], q[:, j, :],
                                           start=(i == 0), stop=(i == 3 * XC - 1))
                            i += 1
                mm.then_inc(ot_done, 1)

            def s(b):
                wait(pe, ztl_done, b + 1)
                wait(pe, ctl_done, KC * (b + 1))
                wait(pe, ptl_done, b)
                for c in range(TC):
                    i = 0
                    for z, x in ((zt_hi, ct_hi), (zt_hi, ct_lo), (zt_lo, ct_hi)):
                        for k in range(KC):
                            for half in range(2):
                                mm = pe.matmul(ps_s[0:R, 2 * c + half, 0:XH + 1], z[:, k, c * R:c * R + R],
                                               x[:, k, half * XH:half * XH + XH + 1], start=(i == 0), stop=(i == 3 * KC - 1))
                            i += 1
                    mm.then_inc(s_done, 1)

            def out(b):
                wait(pe, otl_done, b + 1)
                wait(pe, ztl_done, min(b + 2, B) if isinstance(b, int) else b + 2)
                for c in range(TC):
                    i = 0
                    for y, w in ((ot_hi, wv_hi), (ot_hi, wv_lo), (ot_lo, wv_hi)):
                        for k in range(KC):
                            mm = pe.matmul(ps_h[0:R, c, :], y[:, k, c * R:c * R + R], w[:, k, :],
                                           start=(i == 0), stop=(i == 3 * KC - 1))
                            i += 1
                    mm.then_inc(out_done, 1)

            def step(b):
                if within(b - 1, B):
                    p_turn(b - 1)
                if within(b, B):
                    zt(b)
                if within(b - 1, B):
                    ot(b - 1)
                if within(b, B):
                    s(b)
                if within(b + 1, B):
                    x1_turn(b + 1)
                if within(b - 1, B):
                    out(b - 1)

            x1_turn(0)
            for b in range(2):
                step(b)
            with pe.Fori(2, B - 1) as b:
                step(b)
            step(B - 1)
            step(B)

        @block.scalar
        def _(act):
            act.wait_ge(raw_in[2], 16)
            for dk in range(KC):
                act.activation(wv_hi[:, dk, :], wv[:, dk, :], ACT.Copy).then_inc(prep_hi, 1)
                act.wait_ge(prep_mm, dk + 1)
                act.activation(m_hi[:, dk, :], ps_s[:, dk, :], ACT.Copy).then_inc(prep_hi, 1)

            def x1th(b):
                wait(act, x1t_done, b + 1)
                wait(act, zt_done, b)
                act.activation(x1t_hi[:, 0:2, :], ps_g[:, 0, 0:2 * T], ACT.Copy)
                act.activation(x1t_hi[:, 2:4, :], ps_g[:, 1, 0:2 * T], ACT.Copy).then_inc(x1th_done, 1)

            def cth(b):
                wait(act, ct_in, 16 * (b + 1))
                wait(act, s_done, TC * b)
                for k in range(KC):
                    act.activation(ct_hi[:, k, 0:TX], ct_raw[:, k, :], ACT.Copy).then_inc(cth_done, 1)

            def pth(b):
                wait(act, pt_done, b + 1)
                wait(act, ot_done, b)
                for j in range(XC // 2):
                    a = act.activation(pt_hi[:, 2 * j:2 * j + 2, :], ps_s[0:XR, j, 0:2 * T], ACT.Copy)
                a.then_inc(pth_done, 1)

            def zth(b):
                wait(act, zt_done, b + 1)
                wait(act, s_done, TC * b)
                for k in range(KC):
                    a = act.activation(zt_hi[:, k, :], pair(ps_h, k), ACT.Identity, bias=zbias[:, k:k + 1])
                a.then_inc(zth_done, 1)

            def oth(b):
                wait(act, ot_done, b + 1)
                wait(act, out_done, TC * b)
                act.activation(ot_hi[:, 0:2, :], ps_g[:, 0, 0:2 * T], ACT.Copy)
                act.activation(ot_hi[:, 2:4, :], ps_g[:, 1, 0:2 * T], ACT.Copy).then_inc(oth_done, 1)

            def cxh(b):
                wait(act, cx_in, 16 * (b + 1))
                wait(act, ot_done, b)
                for j in range(XC):
                    act.activation(cx_hi[:, j, :], cx_raw[:, j, :], ACT.Copy).then_inc(cxh_done, 1)

            def exp(b):
                wait(act, pt_done, b)
                wait(act, rinv_done, b)
                for c in range(TC):
                    wait(act, shift_done, TC * b + c + 1)
                    act.activation(p[:, c, :].rearrange("p (a t) -> p a t", a=2), ps_s[0:R, 2 * c:2 * c + 2, 0:XH],
                                   ACT.Exp, bias=shift[:, c:c + 1], accum_out=rsum[:, c:c + 1]).then_inc(exp_done, 1)

            def step(b):
                if within(b - 1, B):
                    pth(b - 1)
                if within(b, B):
                    if not (isinstance(b, int) and b == 0):
                        cth(b)
                    zth(b)
                if within(b - 1, B):
                    oth(b - 1)
                if within(b, B):
                    cxh(b)
                    exp(b)
                if within(b + 1, B):
                    x1th(b + 1)

            cth(0)
            x1th(0)
            for b in range(2):
                step(b)
            with act.Fori(2, B - 1) as b:
                step(b)
            step(B - 1)
            step(B)

        @block.vector
        def _(dve):
            dve.wait_ge(made, 3)
            dve.wait_ge(bias_in, 48)
            for k in range(KC):
                dve.tensor_scalar(bk_all[:, k, :], ones[:], bk[:, k, :], None, ALU.mult).then_inc(spread, 1)
            for dk in range(KC):
                dve.wait_ge(prep_hi, 2 * dk + 1)
                dve.tensor_tensor(wv_lo[:, dk, :], wv[:, dk, :], wv_hi[:, dk, :], ALU.subtract).then_inc(prep_lo, 1)
                dve.wait_ge(prep_hi, 2 * dk + 2)
                dve.tensor_tensor(m_lo[:, dk, :], ps_s[:, dk, :], m_hi[:, dk, :], ALU.subtract).then_inc(prep_lo, 1)
            dve.wait_ge(prep_mm, KC + 1)
            dve.tensor_copy(zbias[:], ps_g[:, 0, 0:KC])
            dve.tensor_copy(kbias[:], ps_g[0:R, 1, :])
            dve.tensor_copy(qk_bias[:], ps_h[0:R, 0, 0:1]).then_inc(prep_lo, 1)
            dve.wait_ge(prep_lo, PREPARED)

            def x1tl(b):
                wait(dve, x1th_done, b + 1)
                dve.tensor_tensor(x1t_lo[:, 0:2, :], ps_g[:, 0, 0:2 * T], x1t_hi[:, 0:2, :], ALU.subtract)
                dve.tensor_tensor(x1t_lo[:, 2:4, :], ps_g[:, 1, 0:2 * T], x1t_hi[:, 2:4, :], ALU.subtract).then_inc(x1tl_done, 1)

            def row_bias(b):
                for c in range(TC):
                    wait(dve, dot_done, TC * b + c)
                    dve.tensor_tensor_reduce(out=dot[:], in0=x1_raw[:, c, :], in1=kbias[:], scale=1.0, scalar=0.0,
                                             op0=ALU.mult, op1=ALU.add, accum_out=rowdot[:, c:c + 1]).then_inc(dot_done, 1)
                wait(dve, dot_done, TC * (b + 1))
                wait(dve, shift_done, TC * b)
                dve.tensor_scalar(rowbias[:], rowdot[:], qk_bias[:, 0:1], None, ALU.add).then_inc(rowbias_done, 1)

            def ptl(b):
                wait(dve, pth_done, b + 1)
                for j in range(XC // 2):
                    q = dve.tensor_tensor(pt_lo[:, 2 * j:2 * j + 2, :], ps_s[0:XR, j, 0:2 * T], pt_hi[:, 2 * j:2 * j + 2, :],
                                          ALU.subtract)
                q.then_inc(ptl_done, 1)

            def ztl(b):
                wait(dve, zth_done, b + 1)
                for k in range(KC):
                    q = dve.scalar_tensor_tensor(out=zt_lo[:, k, :], in0=pair(ps_h, k), scalar=zbias[:, k:k + 1],
                                                 in1=zt_hi[:, k, :], op0=ALU.add, op1=ALU.subtract)
                q.then_inc(ztl_done, 1)

            def otl(b):
                wait(dve, oth_done, b + 1)
                dve.tensor_tensor(ot_lo[:, 0:2, :], ps_g[:, 0, 0:2 * T], ot_hi[:, 0:2, :], ALU.subtract)
                dve.tensor_tensor(ot_lo[:, 2:4, :], ps_g[:, 1, 0:2 * T], ot_hi[:, 2:4, :], ALU.subtract).then_inc(otl_done, 1)

            def row_max(b):
                wait(dve, rowbias_done, b + 1)
                for c in range(TC):
                    wait(dve, s_done, TC * b + c + 1)
                    dve.tensor_reduce(smax[:, c:c + 1], ps_s[0:R, 2 * c:2 * c + 2, 0:XH], AX.XY, ALU.max).then_inc(max_done, 1)
                    wait(dve, max_done, TC * b + c + 1)
                    dve.tensor_tensor(biased_max[:, c:c + 1], smax[:, c:c + 1], rowbias[:, c:c + 1], ALU.add).then_inc(biased_done, 1)
                    wait(dve, biased_done, TC * b + c + 1)
                    wait(dve, exp_done, TC * (b - 1) + c + 1)
                    dve.tensor_tensor(shift[:, c:c + 1], rowbias[:, c:c + 1], biased_max[:, c:c + 1], ALU.subtract)\
                       .then_inc(shift_done, 1)

            def residual(b, odd):
                wait(dve, x1b_done, b + 1)
                for c in range(TC):
                    wait(dve, out_done, TC * b + c + 1)
                    dve.scalar_tensor_tensor(out=r[:, c, :], in0=ps_h[0:R, c, :], scalar=rinv[:, c:c + 1], in1=x1b[:, odd, c, :],
                                             op0=ALU.mult, op1=ALU.add).then_inc(r_done, 1)

            def statistics(b):
                for c in range(TC):
                    wait(dve, r_done, TC * b + c + 1)
                    dve.bn_stats(stats[:, c, :], r[:, c, :]).then_inc(stats_done, 1)
                for c in range(TC):
                    dve.wait_ge(pad_done, 1)
                    wait(dve, stats_done, TC * b + c + 1)
                    dve.bn_aggr(mv[:, c, :], stats[:, c, :]).then_inc(mv_done, 1)
                wait(dve, mv_done, TC * (b + 1))
                dve.tensor_scalar(veps[:, :, 0], mv[:, :, 1], EPS, None, ALU.add).then_inc(veps_done, 1)

            def inverse(b):
                wait(dve, exp_done, TC * (b + 1))
                wait(dve, r_done, TC * b)
                dve.reciprocal(rinv[:], rsum[:]).then_inc(rinv_done, 1)

            def norm(b):
                wait(dve, rstd_done, b + 1)
                wait(dve, stored, 16 * b)
                for c in range(TC):
                    dve.tensor_scalar(xn[:, c, :], r[:, c, :], mv[:, c, 0:1], rstd[:, c, :], ALU.subtract, ALU.mult)\
                       .then_inc(xn_done, 1)

            def step(b, odd):
                if within(b - 1, B):
                    ptl(b - 1)
                if within(b, B):
                    row_bias(b)
                if within(b - 2, B):
                    statistics(b - 2)
                if within(b, B):
                    ztl(b)
                if within(b - 2, B):
                    norm(b - 2)
                if within(b - 1, B):
                    otl(b - 1)
                if within(b, B):
                    row_max(b)
                if within(b + 1, B):
                    x1tl(b + 1)
                if within(b - 1, B):
                    residual(b - 1, 1 - odd)
                if within(b, B):
                    inverse(b)

            x1tl(0)
            for b in range(4):
                step(b, b % 2)
            with dve.Fori(2, B // 2 - 1) as i:
                for odd in range(2):
                    step(2 * i + odd, odd)
            for b in range(B - 2, B + 2):
                step(b, b % 2)

        @block.gpsimd
        def _(pool):
            pool.memset(identity[:], 1.0).then_inc(made, 1)
            pool.memset(mhalf[:], -0.5).then_inc(made, 1)
            pool.memset(ones[:], 1.0).then_inc(made, 1)
            pool.wait_ge(made, 3)
            pool.affine_select(out=identity[:], in_=identity[:], compare_op=ALU.is_equal, fill=0.0, base=0,
                               pattern=[[-1, 128]], channel_multiplier=1).then_inc(made, 1)
            pool.wait_ge(bias_in, 48)
            pool.memset(ct_hi[:, :, TX:TX + 2].bitcast(F32), 0.0).then_inc(pad_done, 1)
            pool.memset(ct_lo[:, :, TX:TX + 2].bitcast(F32), 0.0).then_inc(pad_done, 1)

            def residual_bias(b, odd):
                wait(pool, x1_in, 16 * (b + 1))
                wait(pool, r_done, TC * (b - 1))
                pool.tensor_tensor(x1b[:, odd, :, :], x1_raw[:], bv_all[:, :].rearrange("p (a d) -> p a d", a=1).to_broadcast((R, TC, D)),
                                   ALU.add).then_inc(x1b_done, 1)

            def ctl(b):
                for k in range(KC):
                    wait(pool, cth_done, KC * b + k + 1)
                    pool.tensor_tensor(ct_lo[:, k, 0:TX], ct_raw[:, k, :], ct_hi[:, k, 0:TX], ALU.subtract).then_inc(ctl_done, 1)

            def cxl(b):
                for j in range(XC):
                    wait(pool, cxh_done, XC * b + j + 1)
                    pool.tensor_tensor(cx_lo[:, j, :], cx_raw[:, j, :], cx_hi[:, j, :], ALU.subtract).then_inc(cxl_done, 1)

            def power(b):
                wait(pool, veps_done, b + 1)
                wait(pool, xn_done, TC * b)
                pool.tensor_tensor(rstd[:], veps[:], mhalf[:], ALU.pow).then_inc(rstd_done, 1)

            def step(b, odd):
                if within(b, B):
                    residual_bias(b, odd)
                    ctl(b)
                if within(b - 2, B):
                    power(b - 2)
                if within(b, B):
                    cxl(b)

            for b in range(4):
                step(b, b % 2)
            with pool.Fori(2, B // 2) as i:
                for odd in range(2):
                    step(2 * i + odd, odd)
            for b in range(B, B + 2):
                step(b, b % 2)


def feed_forward(nc, io, x2, out, raw, raw_in):
    with ExitStack() as ctx:
        c_hi = ctx.enter_context(nc.sbuf_tensor("f_c_hi", [128, KC, T], F32R))
        c_lo = ctx.enter_context(nc.sbuf_tensor("f_c_lo", [128, KC, T], F32R))
        identity = ctx.enter_context(nc.sbuf_tensor("f_identity", [128, 128], F32))
        wo, uo = (tuple(ctx.enter_context(nc.sbuf_tensor(f"f_{n}_{part}", [128, KC, D], F32R)) for part in ("hi", "lo"))
                  for n in ("wo", "uo"))
        recurrence(nc, io, x2, identity, c_hi, c_lo, wo, uo, raw, raw_in)
        output_gate(nc, io, x2, out, identity, c_hi, c_lo, wo, uo)


def recurrence(nc, io, x2, identity, c_hi, c_lo, wo, uo, raw, raw_in):
    GATES = ("f", "i", "c")
    HC = KC // 2
    with ExitStack() as ctx:
        def sb(name, shape, dt=F32):
            return ctx.enter_context(nc.sbuf_tensor("f_" + name, shape, dt))

        def sem(name):
            return ctx.enter_context(nc.semaphore("f_" + name))

        w = {n: (sb(n + "_hi", [128, KC, D], F32R), sb(n + "_lo", [128, KC, D], F32R))
             for n in ("wf", "wi", "wc", "uf", "ui", "uc")}
        plan = [(io[n + "_t"], *w[n]) for n in w] + [(io["uo_t"], *uo), (io["wo_t"], *wo)]

        bias = sb("bias", [128, 3, KC])
        bias_raw = sb("bias_raw", [128, 3, KC])
        c0 = sb("c0", [128, KC])
        x2_raw = sb("x2_raw", [R, TC, D])
        xt_hi = sb("xt_hi", [128, KC, T], F32R)
        xt_lo = sb("xt_lo", [128, KC, T], F32R)
        gate = sb("gate", [128, 3, KC, T])
        keep = sb("keep", [128, KC, T])
        fresh = sb("fresh", [128, KC, T])
        c = sb("c", [128, KC, T])

        ps_gate = ctx.enter_context(nc.psum_tensor("f_ps_gate", [128, 6, 512], F32))
        ps_x = ctx.enter_context(nc.psum_tensor("f_ps_x", [128, 2, 512], F32))

        made = sem("made")
        w_rounded = sem("w_rounded")
        w_split = sem("w_split")
        b_in = sem("b_in")
        bias_done = sem("bias_done")
        x2_in = sem("x2_in")
        xt_done = sem("xt_done")
        xth_done = sem("xth_done")
        xtl_done = sem("xtl_done")
        xpart_done = sem("xpart_done")
        gate_done = sem("gate_done")
        act_done = sem("act_done")
        c_start = sem("c_start")
        keep_done = sem("keep_done")
        fresh_done = sem("fresh_done")
        sum_done = sem("sum_done")
        c_done = sem("c_done")
        ch_done = sem("ch_done")
        cl_done = sem("cl_done")

        block = ctx.enter_context(nc.Block())

        def region(bank, k):
            return ps_gate[:, bank, k * T:k * T + T]

        @block.sync
        def _(sp):
            def load(b):
                wait(sp, xt_done, b)
                sp.dma_start(x2_raw[:], x2[b].rearrange("(c p) d -> p c d", p=R)).then_inc(x2_in, 16)

            load(0)
            with nc.allow_non_contiguous_dma(reason="biases by partition"):
                for j, n in enumerate(GATES):
                    sp.dma_start(bias_raw[:, j, :], io["b" + n].rearrange("(k p) -> p k", p=128)).then_inc(b_in, 16)
                sp.dma_start(c0[:], io["in_c"].rearrange("(k p) -> p k", p=128)).then_inc(b_in, 16)

            for i in range(3, len(plan)):
                sp.wait_ge(w_split, i - 2)
                load_weight(sp, raw[i % 3], raw_in[i % 3], plan[i][0])
            with sp.Fori(1, B) as b:
                load(b)

        @block.gpsimd
        def _(pool):
            pool.memset(identity[:], 1.0).then_inc(made, 1)
            pool.memset(keep[:], 0.0).then_inc(made, 1)
            pool.wait_ge(made, 2)
            pool.affine_select(out=identity[:], in_=identity[:], compare_op=ALU.is_equal, fill=0.0, base=0,
                               pattern=[[-1, 128]], channel_multiplier=1).then_inc(made, 1)
            for i in range(6, 8):
                _, hi, lo = plan[i]
                pool.wait_ge(raw_in[i % 3], 16 * (i // 3 + 2))
                pool.wait_ge(w_split, i)
                pool.tensor_copy(hi[:], raw[i % 3][:]).then_inc(w_rounded, 1)
                pool.wait_ge(w_rounded, i + 1)
                pool.tensor_tensor(lo[:], raw[i % 3][:], hi[:], ALU.subtract).then_inc(w_split, 1)

        @block.tensor
        def _(pe):
            pe.wait_ge(made, 3)

            def x_turn(b):
                wait(pe, x2_in, 16 * (b + 1))
                wait(pe, xtl_done, b)
                for k in range(KC):
                    for q in range(TC):
                        mm = pe.transpose(ps_x[:, k // 2, (k % 2) * T + q * R:(k % 2) * T + q * R + R],
                                          x2_raw[:, q, 128 * k:128 * k + 128], identity[0:R, 0:R])
                mm.then_inc(xt_done, 1)

            def x_part(b):
                wait(pe, xtl_done, b + 1)
                for half in range(2):
                    for j, n in enumerate(GATES):
                        bank = 3 * half + j
                        if isinstance(b, int) and b == 0 and half == 0:
                            pe.wait_ge(w_split, j + 1)
                        wait(pe, act_done, 6 * (b - 1) + bank + 1)
                        for k2 in range(HC):
                            i = 0
                            for wp, xp in ((0, xt_hi), (1, xt_hi), (0, xt_lo)):
                                for k in range(KC):
                                    m = HC * half + k2
                                    mm = pe.matmul(region(bank, k2), w["w" + n][wp][:, k, 128 * m:128 * m + 128], xp[:, k, :],
                                                   start=(k2 == 0 and i == 0), stop=False, skip_group_check=True)
                                    i += 1
                mm.then_inc(xpart_done, 1)

            def c_part(b):
                wait(pe, cl_done, 2 * (b + 1))
                for half in range(2):
                    for j, n in enumerate(GATES):
                        bank = 3 * half + j
                        if isinstance(b, int) and b == 0 and half == 0:
                            pe.wait_ge(w_split, 3 + j + 1)
                        for k2 in range(HC):
                            i = 0
                            for up, cp in ((0, c_hi), (1, c_hi), (0, c_lo)):
                                for k in range(KC):
                                    m = HC * half + k2
                                    mm = pe.matmul(region(bank, k2), w["u" + n][up][:, k, 128 * m:128 * m + 128], cp[:, k, :],
                                                   start=False, stop=(i == 3 * KC - 1), skip_group_check=True)
                                    i += 1
                        mm.then_inc(gate_done, 1)

            def step(b, more=True):
                x_part(b)
                if more:
                    x_turn(b + 1)
                c_part(b)

            x_turn(0)
            step(0)
            with pe.Fori(1, B - 1) as b:
                step(b)
            step(B - 1, more=False)

        @block.scalar
        def _(act):
            act.wait_ge(b_in, 64)
            act.activation(bias[:, 0:2, :], bias_raw[:, 0:2, :], ACT.Copy, scale=0.5).then_inc(bias_done, 1)
            act.activation(bias[:, 2, :], bias_raw[:, 2, :], ACT.Copy).then_inc(bias_done, 1)
            act.wait_ge(bias_done, 2)

            def xth(b):
                wait(act, xt_done, b + 1)
                wait(act, xpart_done, b)
                act.activation(xt_hi[:, 0:2, :], ps_x[:, 0, 0:2 * T], ACT.Copy)
                act.activation(xt_hi[:, 2:4, :], ps_x[:, 1, 0:2 * T], ACT.Copy).then_inc(xth_done, 1)

            def gates(b):
                for half in range(2):
                    for j in range(3):
                        wait(act, gate_done, 6 * b + 3 * half + j + 1)
                        wait(act, sum_done, 2 * (b - 1) + half + 1)
                        for k2 in range(HC):
                            m = HC * half + k2
                            a = act.activation(gate[:, j, m, :], region(3 * half + j, k2), ACT.Tanh, bias=bias[:, j, m:m + 1],
                                               scale=0.5 if j < 2 else 1.0)
                        a.then_inc(act_done, 1)

            def step(b, more=True):
                if more:
                    xth(b + 1)
                gates(b)

            for i in range(6):
                act.wait_ge(raw_in[i % 3], 16 * (i // 3 + 2))
                act.activation(plan[i][1][:], raw[i % 3][:], ACT.Copy).then_inc(w_rounded, 1)
                if i == 0:
                    xth(0)
            step(0)
            with act.Fori(1, B - 1) as b:
                step(b)
            step(B - 1, more=False)

        @block.vector
        def _(dve):
            def start():
                dve.wait_ge(b_in, 64)
                dve.wait_ge(made, 2)
                for k in range(KC):
                    dve.tensor_scalar(c[:, k, :], keep[:, k, :], c0[:, k:k + 1], None, ALU.add).then_inc(c_start, 1)
                dve.wait_ge(c_start, KC)
                dve.tensor_copy(c_hi[:], c[:]).then_inc(c_start, 1)
                dve.wait_ge(c_start, KC + 1)
                dve.tensor_tensor(c_lo[:], c[:], c_hi[:], ALU.subtract).then_inc(cl_done, 2)

            def xtl(b):
                wait(dve, xth_done, b + 1)
                dve.tensor_tensor(xt_lo[:, 0:2, :], ps_x[:, 0, 0:2 * T], xt_hi[:, 0:2, :], ALU.subtract)
                dve.tensor_tensor(xt_lo[:, 2:4, :], ps_x[:, 1, 0:2 * T], xt_hi[:, 2:4, :], ALU.subtract).then_inc(xtl_done, 1)

            def state(b):
                for half in range(2):
                    n = 2 * b + half
                    cols = slice(HC * half, HC * half + HC)
                    wait(dve, act_done, 6 * b + 3 * half + 1)
                    dve.scalar_tensor_tensor(out=keep[:, cols, :], in0=gate[:, 0, cols, :], scalar=1.0, in1=c[:, cols, :],
                                             op0=ALU.add, op1=ALU.mult).then_inc(keep_done, 1)
                    wait(dve, act_done, 6 * b + 3 * half + 3)
                    dve.scalar_tensor_tensor(out=fresh[:, cols, :], in0=gate[:, 1, cols, :], scalar=1.0, in1=gate[:, 2, cols, :],
                                             op0=ALU.add, op1=ALU.mult).then_inc(fresh_done, 1)
                    wait(dve, keep_done, n + 1)
                    wait(dve, fresh_done, n + 1)
                    dve.tensor_tensor(keep[:, cols, :], keep[:, cols, :], fresh[:, cols, :], ALU.add).then_inc(sum_done, 1)
                    wait(dve, sum_done, n + 1)
                    dve.tensor_scalar(c[:, cols, :], keep[:, cols, :], 0.5, None, ALU.mult).then_inc(c_done, 1)
                for half in range(2):
                    n = 2 * b + half
                    cols = slice(HC * half, HC * half + HC)
                    wait(dve, c_done, n + 1)
                    wait(dve, gate_done, 6 * (b + 1))
                    dve.tensor_copy(c_hi[:, cols, :], c[:, cols, :]).then_inc(ch_done, 1)
                    wait(dve, ch_done, n + 1)
                    dve.tensor_tensor(c_lo[:, cols, :], c[:, cols, :], c_hi[:, cols, :], ALU.subtract).then_inc(cl_done, 1)

            def step(b, more=True):
                if more:
                    xtl(b + 1)
                state(b)

            for i in range(6):
                dve.wait_ge(w_rounded, i + 1)
                dve.tensor_tensor(plan[i][2][:], raw[i % 3][:], plan[i][1][:], ALU.subtract).then_inc(w_split, 1)
                if i == 0:
                    xtl(0)
                if i == 1:
                    start()
            step(0)
            with dve.Fori(1, B - 1) as b:
                step(b)
            step(B - 1, more=False)


def output_gate(nc, io, x2, out, identity, c_hi, c_lo, wo, uo):
    SLOTS = 4
    with ExitStack() as ctx:
        def sb(name, shape, dt=F32):
            return ctx.enter_context(nc.sbuf_tensor("o_" + name, shape, dt))

        def sem(name):
            return ctx.enter_context(nc.semaphore("o_" + name))

        bo_all = sb("bo_all", [R, D])
        mhalf = sb("mhalf", [R, TC, 1])
        base = sb("base", [R, TC, D])
        x2_raw = sb("x2_raw", [R, SLOTS, TC, D])
        xt_hi = sb("xt_hi", [128, 2, KC, T], F32R)
        xt_lo = sb("xt_lo", [128, 2, KC, T], F32R)
        pre = sb("pre", [R, 2, TC, D])
        h = sb("h", [R, 2, TC, D])
        r = sb("r", [R, 2, TC, D])
        stats = sb("stats", [R, 2, TC, 6])
        mv = sb("mv", [R, 2, TC, 2])
        veps = sb("veps", [R, 2, TC, 1])
        rstd = sb("rstd", [R, 2, TC, 1])
        y = sb("y", [R, 2, TC, D])

        ps_x = ctx.enter_context(nc.psum_tensor("o_ps_x", [128, 2, 2, 512], F32))
        ps_o = ctx.enter_context(nc.psum_tensor("o_ps_o", [128, 2, 2, 512], F32))

        made = sem("made")
        bo_in = sem("bo_in")
        x2_in = [sem(f"x2_in{i}") for i in range(SLOTS)]
        base_mm = sem("base_mm")
        base_done = sem("base_done")
        xt_done = sem("xt_done")
        xth_done = sem("xth_done")
        xtl_done = sem("xtl_done")
        o_done = sem("o_done")
        pre_done = sem("pre_done")
        h_done = sem("h_done")
        r_done = sem("r_done")
        stats_done = sem("stats_done")
        mv_done = sem("mv_done")
        veps_done = sem("veps_done")
        rstd_done = sem("rstd_done")
        y_done = sem("y_done")
        stored = [sem(f"stored{i}") for i in range(2)]

        block = ctx.enter_context(nc.Block())


        @block.sync
        def _(sp):
            sp.dma_start(bo_all[:], io["bo"].rearrange("(a d) -> a d", a=1).to_broadcast((R, D))).then_inc(bo_in, 16)

            def load(n, u):
                wait(sp, r_done, n - SLOTS + 1)
                sp.dma_start(x2_raw[:, u, :, :], x2[n].rearrange("(c p) d -> p c d", p=R)).then_inc(x2_in[u], 16)

            def store(n, s):
                sp.wait_ge(y_done, n + 1)
                sp.dma_start(out[n].rearrange("(c p) d -> p c d", p=R), y[:, s, :, :]).then_inc(stored[s], 16)

            for u in range(SLOTS):
                load(u, u)
            with sp.Fori(1, B // SLOTS) as i:
                for u in range(SLOTS):
                    load(SLOTS * i + u, u)
                    store(SLOTS * (i - 1) + u, u % 2)
            for u in range(SLOTS):
                store(B - SLOTS + u, u % 2)
            for s in range(2):
                sp.wait_ge(stored[s], 16 * (B // 2))

        @block.tensor
        def _(pe):
            for q in range(TC):
                i = 0
                for cp, up in ((c_hi, 0), (c_hi, 1), (c_lo, 0)):
                    for k in range(KC):
                        mm = pe.matmul(ps_o[0:R, 0, q, :], cp[:, k, q * R:q * R + R], uo[up][:, k, :],
                                       start=(i == 0), stop=(i == 3 * KC - 1))
                        i += 1
            mm.then_inc(base_mm, 1)

            def turn(i, u):
                n, s = SLOTS * i + u, u % 2
                if not within(n, B):
                    return
                wait(pe, x2_in[u % SLOTS], 16 * (i + u // SLOTS + 1))
                wait(pe, xtl_done, n - 1)
                for k in range(KC):
                    for q in range(TC):
                        mm = pe.transpose(ps_x[:, s, k // 2, (k % 2) * T + q * R:(k % 2) * T + q * R + R],
                                          x2_raw[:, u % SLOTS, q, 128 * k:128 * k + 128], identity[0:R, 0:R])
                mm.then_inc(xt_done, 1)

            def product(i, u):
                n, s = SLOTS * i + u, u % 2
                wait(pe, xtl_done, n + 1)
                wait(pe, pre_done, n - 1)
                if s == 0:
                    pe.wait_ge(base_done, 1)
                for q in range(TC):
                    j = 0
                    for xp, wp in ((xt_hi, 0), (xt_hi, 1), (xt_lo, 0)):
                        for k in range(KC):
                            mm = pe.matmul(ps_o[0:R, s, q, :], xp[:, s, k, q * R:q * R + R], wo[wp][:, k, :],
                                           start=(j == 0), stop=(j == 3 * KC - 1))
                            j += 1
                mm.then_inc(o_done, 1)

            turn(0, 0)

            def steps(i):
                for u in range(SLOTS):
                    turn(i, u + 1)
                    product(i, u)

            steps(0)
            with pe.Fori(1, B // SLOTS - 1) as i:
                steps(i)
            steps(B // SLOTS - 1)

        @block.scalar
        def _(act):
            def xth(n, u):
                if not within(n, B):
                    return
                wait(act, xt_done, n + 1)
                wait(act, o_done, n - 1)
                for k in range(2):
                    a = act.activation(xt_hi[:, u % 2, 2 * k:2 * k + 2, :], ps_x[:, u % 2, k, 0:2 * T], ACT.Copy)
                a.then_inc(xth_done, 1)

            def tanh(n, u):
                if not within(n, B):
                    return
                wait(act, pre_done, n + 1)
                wait(act, r_done, n - 1)
                act.activation(h[:, u % 2, :, :], pre[:, u % 2, :, :], ACT.Tanh).then_inc(h_done, 1)

            xth(0, 0)

            def steps(i):
                for u in range(SLOTS):
                    xth(SLOTS * i + u + 1, u + 1)
                    tanh(SLOTS * i + u, u)

            steps(0)
            with act.Fori(1, B // SLOTS - 1) as i:
                steps(i)
            steps(B // SLOTS - 1)

        @block.vector
        def _(dve):
            dve.wait_ge(base_mm, 1)
            dve.wait_ge(bo_in, 16)
            dve.tensor_tensor(base[:], ps_o[0:R, 0, :, :], bo_all[:, :].rearrange("p (a d) -> p a d", a=1).to_broadcast((R, TC, D)),
                              ALU.add).then_inc(base_done, 1)
            dve.wait_ge(base_done, 1)

            def xtl(n, u):
                if not within(n, B):
                    return
                s = u % 2
                wait(dve, xth_done, n + 1)
                for k in range(2):
                    v = dve.tensor_tensor(xt_lo[:, s, 2 * k:2 * k + 2, :], ps_x[:, s, k, 0:2 * T], xt_hi[:, s, 2 * k:2 * k + 2, :],
                                          ALU.subtract)
                v.then_inc(xtl_done, 1)

            def with_base(n, u):
                if not within(n, B):
                    return
                wait(dve, o_done, n + 1)
                wait(dve, h_done, n - 1)
                dve.tensor_tensor(pre[:, u % 2, :, :], ps_o[0:R, u % 2, :, :], base[:], ALU.add).then_inc(pre_done, 1)

            def statistics(n, u):
                if not within(n, B):
                    return
                s = u % 2
                wait(dve, r_done, n + 1)
                for q in range(TC):
                    v = dve.bn_stats(stats[:, s, q, :], r[:, s, q, :])
                v.then_inc(stats_done, 1)
                dve.wait_ge(base_done, 1)
                wait(dve, stats_done, n + 1)
                for q in range(TC):
                    v = dve.bn_aggr(mv[:, s, q, :], stats[:, s, q, :])
                v.then_inc(mv_done, 1)
                wait(dve, mv_done, n + 1)
                dve.tensor_scalar(veps[:, s, :, 0], mv[:, s, :, 1], EPS, None, ALU.add).then_inc(veps_done, 1)

            def norm(n, u):
                if not within(n, B):
                    return
                s = u % 2
                wait(dve, rstd_done, n + 1)
                wait(dve, stored[s], 8 * (n - s))
                for q in range(TC):
                    v = dve.tensor_scalar(y[:, s, q, :], r[:, s, q, :], mv[:, s, q, 0:1], rstd[:, s, q, :], ALU.subtract, ALU.mult)
                v.then_inc(y_done, 1)

            xtl(0, 0)

            def steps(i):
                for u in range(SLOTS):
                    n = SLOTS * i + u
                    xtl(n + 1, u + 1)
                    statistics(n - 1, u + 1)
                    with_base(n, u)
                    norm(n - 1, u + 1)

            steps(0)
            with dve.Fori(1, B // SLOTS - 1) as i:
                steps(i)
            steps(B // SLOTS - 1)
            statistics(B - 1, 1)
            norm(B - 1, 1)

        @block.gpsimd
        def _(pool):
            pool.memset(mhalf[:], -0.5).then_inc(made, 1)
            pool.wait_ge(made, 1)

            def residual(n, u):
                wait(pool, h_done, n + 1)
                wait(pool, y_done, n - 1)
                pool.tensor_tensor(r[:, u % 2, :, :], h[:, u % 2, :, :], x2_raw[:, u, :, :], ALU.add).then_inc(r_done, 1)

            def power(n, u):
                wait(pool, veps_done, n + 1)
                wait(pool, y_done, n - 1)
                pool.tensor_tensor(rstd[:, u % 2, :, :], veps[:, u % 2, :, :], mhalf[:], ALU.pow).then_inc(rstd_done, 1)

            def steps(i):
                for u in range(SLOTS):
                    residual(SLOTS * i + u, u)
                    power(SLOTS * i + u, u)

            steps(0)
            with pool.Fori(1, B // SLOTS) as i:
                steps(i)


def decoder(nc, io, out):
    x1 = nc.dram_tensor("x1_scratch", (B, T, D), F32, kind="Internal").ap()
    x2 = nc.dram_tensor("x2_scratch", (B, T, D), F32, kind="Internal").ap()
    with ExitStack() as ctx:
        raw = [ctx.enter_context(nc.sbuf_tensor(f"w_raw{i}", [128, KC, D], F32)) for i in range(3)]
        raw_in = [ctx.enter_context(nc.semaphore(f"w_raw_in{i}")) for i in range(3)]
        self_attention(nc, io, x1, raw, raw_in)
        cross_attention(nc, io, x1, x2, raw, raw_in)
        feed_forward(nc, io, x2, out, raw, raw_in)


def kernel(**inputs):
    from concourse import bacc
    from concourse.bass_utils import run_bass_kernel_spmd

    a = {k: np.asarray(v) for k, v in inputs.items()}
    laid_out = {
        "x": a["x"],
        "xt": a["x"].reshape(B, T, H, C).transpose(0, 3, 2, 1),
        "cx": a["ctx_1024"],
        "ct": a["ctx_1024"].transpose(0, 2, 1),
        "wq": a["L0_attn_Wq"],
        "wk": a["L0_attn_Wk"],
        "wv": a["L0_attn_Wv"],
        "wu_t": a["L0_attn_Wu"].T,
        "bu": a["L0_attn_bu"],
        "xwq": a["L0_xattn_Wq"],
        "xwk": a["L0_xattn_Wk"],
        "xwv_t": a["L0_xattn_Wv"].T,
        "xbq": a["L0_xattn_bq"],
        "xbk": a["L0_xattn_bk"],
        "xbv": a["L0_xattn_bv"],
        "in_c": a["L0_ffn_in_c"],
    }
    for n in "fico":
        laid_out["w" + n + "_t"] = a["L0_ffn_w" + n].T
        laid_out["u" + n + "_t"] = a["L0_ffn_u" + n].T
        laid_out["b" + n] = a["L0_ffn_b" + n]

    nc = bacc.Bacc("TRN2", target_bir_lowering=False, num_devices=1)
    arrays, io = {}, {}
    for name, array in laid_out.items():
        arrays["in_" + name] = np.ascontiguousarray(array)
        io[name] = nc.dram_tensor("in_" + name, array.shape, F32, kind="ExternalInput").ap()
    out = nc.dram_tensor("out", (B, T, D), F32, kind="ExternalOutput").ap()
    decoder(nc, io, out)
    result = run_bass_kernel_spmd(nc, [arrays], core_ids=[0])
    return result.results[0]["out"]
```
